# Optimizing a Trainium2 kernel written in Bass

```python
import numpy as np
import jax
import jax.numpy as jnp

def _softmax(x, axis=-1):
    return jax.nn.softmax(x, axis=axis)

def _gelu(x):
    return jax.nn.gelu(x, approximate=True)

def _silu(x):
    return jax.nn.silu(x)

def _sigmoid(x):
    return jax.nn.sigmoid(x)

def _layernorm(x, axis=-1, eps=1e-05):
    m = jnp.mean(x, axis=axis, keepdims=True)
    v = jnp.var(x, axis=axis, keepdims=True)
    return (x - m) / jnp.sqrt(v + eps)

def _scatter_add(tgt, idx, src, axis=0):
    return tgt.at[idx].add(src)

def _segment_sum(src, seg, n):
    return jax.ops.segment_sum(src, seg, n)
kernel_name = 'mk_gnn_resnorm_d4_gnn_r64_8f1290'

def setup_inputs(seed: int=0):
    np.random.seed(seed)
    _w = jnp.asarray

    def _rec_inputs():
        import jax
        import jax.numpy as jnp
        _gk = jax.random.key(seed)
        x = -0.000202 + 1 * jax.random.normal(jax.random.fold_in(_gk, 1), (100000, 128), jnp.float32)
        src = jax.random.randint(jax.random.fold_in(_gk, 2), (25000,), 0, 100000, jnp.int32)
        dst = jnp.minimum((100000 * jax.random.uniform(jax.random.fold_in(_gk, 3), (25000,)) ** 2.0).astype(jnp.int32), 99999)
        _o = jnp.argsort(dst, stable=True)
        src = src[_o]
        dst = dst[_o]
        return (x, src, dst)
    x, src, dst = _rec_inputs()

    def _L0_gnn_setup():
        import jax, jax.numpy as jnp
        import numpy as np
        N_NODES = 50000
        N_EDGES = 25000
        HIDDEN = 128
        HEADS = 8
        PER_HEAD = HIDDEN // HEADS
        NEG_SLOPE = 0.2
        key = jax.random.key(seed)
        ks = jax.random.split(key, 7)
        feat = jax.random.normal(ks[0], (N_NODES, HIDDEN), dtype=jnp.float32)
        src = jax.random.randint(ks[1], (N_EDGES,), 0, N_NODES, dtype=jnp.int32)
        dst = jax.random.randint(ks[2], (N_EDGES,), 0, N_NODES, dtype=jnp.int32)
        W = jax.random.normal(ks[3], (HIDDEN, HEADS * PER_HEAD), dtype=jnp.float32) / np.sqrt(HIDDEN)
        attn_l = jax.random.normal(ks[4], (HEADS, PER_HEAD), dtype=jnp.float32) / np.sqrt(PER_HEAD)
        attn_r = jax.random.normal(ks[5], (HEADS, PER_HEAD), dtype=jnp.float32) / np.sqrt(PER_HEAD)
        bias = jnp.zeros((HEADS * PER_HEAD,), dtype=jnp.float32)
        return {'feat': feat, 'src': src, 'dst': dst, 'W': W, 'attn_l': attn_l, 'attn_r': attn_r, 'bias': bias}
    _L0_gnn_all = _L0_gnn_setup()
    _L0_gnn_in = {k: v for k, v in _L0_gnn_all.items() if k in ('W', 'attn_l', 'attn_r', 'bias')}
    del _L0_gnn_all

    def _L1_gnn_setup():
        import jax, jax.numpy as jnp
        import numpy as np
        K = 4
        ROUTIT = 6
        EPS = 1e-12

        def l2norm(v):
            n = jnp.linalg.norm(v, axis=-1, keepdims=True)
            return v / jnp.maximum(n, EPS)
        key = jax.random.key(seed)
        k1, k2, k3, k4 = jax.random.split(key, 4)
        n, in_dim = (100000, 128)
        m = 25000
        d = K * 32
        x = jax.random.normal(k1, (n, in_dim), dtype=jnp.float32)
        src_trg = jax.random.randint(k2, (2, m), 0, n, dtype=jnp.int64)
        lim = 1.0 / np.sqrt(in_dim)
        W = jax.random.uniform(k3, (d, in_dim), minval=-lim, maxval=lim, dtype=jnp.float32)
        b = jax.random.uniform(k4, (d,), minval=-lim, maxval=lim, dtype=jnp.float32)
        return {'x': x, 'src_trg': src_trg, 'W': W, 'b': b}
    _L1_gnn_all = _L1_gnn_setup()
    _L1_gnn_in = {k: v for k, v in _L1_gnn_all.items() if k in ('W', 'b')}
    del _L1_gnn_all

    def _L2_gnn_setup():
        import jax, jax.numpy as jnp
        import numpy as np
        NUM_STEPS = 1

        def _seg_mean(vals, idx, num_nodes):
            s = jax.ops.segment_sum(vals, idx, num_segments=num_nodes)
            cnt = jax.ops.segment_sum(jnp.ones((vals.shape[0],), vals.dtype), idx, num_segments=num_nodes)
            return s / jnp.maximum(cnt, 1.0)[:, None]

        def _gru_cell(a, h, w_ih, w_hh, b_ih, b_hh):
            gi = a @ w_ih.T + b_ih
            gh = h @ w_hh.T + b_hh
            H = h.shape[1]
            i_r, i_z, i_n = (gi[:, :H], gi[:, H:2 * H], gi[:, 2 * H:])
            h_r, h_z, h_n = (gh[:, :H], gh[:, H:2 * H], gh[:, 2 * H:])
            r = jax.nn.sigmoid(i_r + h_r)
            z = jax.nn.sigmoid(i_z + h_z)
            n = jnp.tanh(i_n + r * h_n)
            return (1.0 - z) * n + z * h
        key = jax.random.key(seed)
        ks = jax.random.split(key, 8)
        N, E, H = (100000, 10000, 128)
        sc = 1.0 / np.sqrt(H)
        feat = jax.random.normal(ks[0], (N, H), jnp.float32)
        src = jax.random.randint(ks[1], (E,), 0, N, jnp.int32)
        dst = jax.random.randint(ks[2], (E,), 0, N, jnp.int32)
        W_in = jax.random.normal(ks[3], (H, H), jnp.float32) * sc
        W_out = jax.random.normal(ks[4], (H, H), jnp.float32) * sc
        w_ih = jax.random.normal(ks[5], (3 * H, 2 * H), jnp.float32) * sc
        w_hh = jax.random.normal(ks[6], (3 * H, H), jnp.float32) * sc
        return {'feat': feat, 'src': src, 'dst': dst, 'W_in': W_in, 'b_in': jnp.zeros((H,), jnp.float32), 'W_out': W_out, 'b_out': jnp.zeros((H,), jnp.float32), 'w_ih': w_ih, 'w_hh': w_hh, 'b_ih': jnp.zeros((3 * H,), jnp.float32), 'b_hh': jnp.zeros((3 * H,), jnp.float32)}
    _L2_gnn_all = _L2_gnn_setup()
    _L2_gnn_in = {k: v for k, v in _L2_gnn_all.items() if k in ('W_in', 'b_in', 'W_out', 'b_out', 'w_ih', 'w_hh', 'b_ih', 'b_hh')}
    del _L2_gnn_all

    def _L3_gnn_setup():
        import jax, jax.numpy as jnp
        import numpy as np
        TAU = 1.0
        EPS = 1e-30
        LN_EPS = 1e-05

        def _scatter_logsumexp(src, index, dim_size):
            scaled = src.astype(jnp.float32) / TAU
            mx = jax.ops.segment_max(scaled, index, num_segments=dim_size)
            exp_val = jnp.exp(scaled - mx[index])
            sum_exp = jax.ops.segment_sum(exp_val, index, num_segments=dim_size)
            out = TAU * (mx + jnp.log(jnp.maximum(sum_exp, EPS)))
            deg = jax.ops.segment_sum(jnp.ones_like(index, dtype=jnp.int32), index, num_segments=dim_size)
            return jnp.where((deg > 0)[:, None], out, 0.0)
        key = jax.random.key(seed)
        ks = jax.random.split(key, 5)
        N, E, D_in, D_out = (50000, 12500, 128, 128)
        x = jax.random.normal(ks[0], (N, D_in), dtype=jnp.float32)
        edge_src = jax.random.randint(ks[1], (E,), 0, N, dtype=jnp.int64)
        edge_dst = jax.random.randint(ks[2], (E,), 0, N, dtype=jnp.int64)
        W = jax.random.normal(ks[3], (2 * D_in, D_out), dtype=jnp.float32) * (1.0 / np.sqrt(2 * D_in))
        b = jnp.zeros((D_out,), dtype=jnp.float32)
        gamma = jnp.ones((D_out,), dtype=jnp.float32)
        beta = jnp.zeros((D_out,), dtype=jnp.float32)
        return {'x': x, 'edge_src': edge_src, 'edge_dst': edge_dst, 'W': W, 'b': b, 'gamma': gamma, 'beta': beta}
    _L3_gnn_all = _L3_gnn_setup()
    _L3_gnn_in = {k: v for k, v in _L3_gnn_all.items() if k in ('W', 'b', 'gamma', 'beta')}
    del _L3_gnn_all
    return {'x': x, 'src': src, 'dst': dst, 'L0_gnn_W': _L0_gnn_in['W'], 'L0_gnn_attn_l': _L0_gnn_in['attn_l'], 'L0_gnn_attn_r': _L0_gnn_in['attn_r'], 'L0_gnn_bias': _L0_gnn_in['bias'], 'L1_gnn_W': _L1_gnn_in['W'], 'L1_gnn_b': _L1_gnn_in['b'], 'L2_gnn_W_in': _L2_gnn_in['W_in'], 'L2_gnn_b_in': _L2_gnn_in['b_in'], 'L2_gnn_W_out': _L2_gnn_in['W_out'], 'L2_gnn_b_out': _L2_gnn_in['b_out'], 'L2_gnn_w_ih': _L2_gnn_in['w_ih'], 'L2_gnn_w_hh': _L2_gnn_in['w_hh'], 'L2_gnn_b_ih': _L2_gnn_in['b_ih'], 'L2_gnn_b_hh': _L2_gnn_in['b_hh'], 'L3_gnn_W': _L3_gnn_in['W'], 'L3_gnn_b': _L3_gnn_in['b'], 'L3_gnn_gamma': _L3_gnn_in['gamma'], 'L3_gnn_beta': _L3_gnn_in['beta']}

def reference(x, src, dst, L0_gnn_W, L0_gnn_attn_l, L0_gnn_attn_r, L0_gnn_bias, L1_gnn_W, L1_gnn_b, L2_gnn_W_in, L2_gnn_b_in, L2_gnn_W_out, L2_gnn_b_out, L2_gnn_w_ih, L2_gnn_w_hh, L2_gnn_b_ih, L2_gnn_b_hh, L3_gnn_W, L3_gnn_b, L3_gnn_gamma, L3_gnn_beta):
    import jax
    import jax.numpy as jnp

    def _L0_gnn_ref(feat, src, dst, W, attn_l, attn_r, bias):
        import jax, jax.numpy as jnp
        import numpy as np
        N_NODES = 50000
        N_EDGES = 25000
        HIDDEN = 128
        HEADS = 8
        PER_HEAD = HIDDEN // HEADS
        NEG_SLOPE = 0.2
        N = feat.shape[0]
        z = (feat @ W).reshape(N, HEADS, PER_HEAD)
        el = jnp.einsum('nhp,hp->nh', z, attn_l)
        er = jnp.einsum('nhp,hp->nh', z, attn_r)
        e = jax.nn.leaky_relu(el[src] + er[dst], negative_slope=NEG_SLOPE)
        emax = jax.ops.segment_max(e, dst, num_segments=N)
        emax = jnp.where(jnp.isfinite(emax), emax, 0.0)
        a = jnp.exp(e - emax[dst])
        denom = jax.ops.segment_sum(a, dst, num_segments=N)
        msg = z[src] * a[:, :, None]
        agg = jax.ops.segment_sum(msg, dst, num_segments=N)
        out = agg / jnp.maximum(denom, 1e-09)[:, :, None]
        out = out + bias.reshape(1, HEADS, PER_HEAD)
        return out.reshape(N, HEADS * PER_HEAD)

    def _L1_gnn_ref(x, src_trg, W, b):
        import jax, jax.numpy as jnp
        import numpy as np
        K = 4
        ROUTIT = 6
        EPS = 1e-12

        def l2norm(v):
            n = jnp.linalg.norm(v, axis=-1, keepdims=True)
            return v / jnp.maximum(n, EPS)
        n = x.shape[0]
        d = W.shape[0]
        dd = d // K
        src, trg = (src_trg[0], src_trg[1])
        h = x @ W.T + b
        h = l2norm(h.reshape(n, K, dd))
        z = h[src]
        c = h
        for _ in range(ROUTIT):
            p = jnp.sum(z * c[trg], axis=2)
            p = jax.nn.softmax(p, axis=1)
            ws = p[:, :, None] * z
            c = c.at[trg].add(ws)
            c = l2norm(c)
        return c.reshape(n, d)

    def _L2_gnn_ref(feat, src, dst, W_in, b_in, W_out, b_out, w_ih, w_hh, b_ih, b_hh):
        import jax, jax.numpy as jnp
        import numpy as np
        NUM_STEPS = 1

        def _seg_mean(vals, idx, num_nodes):
            s = jax.ops.segment_sum(vals, idx, num_segments=num_nodes)
            cnt = jax.ops.segment_sum(jnp.ones((vals.shape[0],), vals.dtype), idx, num_segments=num_nodes)
            return s / jnp.maximum(cnt, 1.0)[:, None]

        def _gru_cell(a, h, w_ih, w_hh, b_ih, b_hh):
            gi = a @ w_ih.T + b_ih
            gh = h @ w_hh.T + b_hh
            H = h.shape[1]
            i_r, i_z, i_n = (gi[:, :H], gi[:, H:2 * H], gi[:, 2 * H:])
            h_r, h_z, h_n = (gh[:, :H], gh[:, H:2 * H], gh[:, 2 * H:])
            r = jax.nn.sigmoid(i_r + h_r)
            z = jax.nn.sigmoid(i_z + h_z)
            n = jnp.tanh(i_n + r * h_n)
            return (1.0 - z) * n + z * h
        N = feat.shape[0]
        h = feat
        for _ in range(NUM_STEPS):
            feat_in = h @ W_in.T + b_in
            feat_out = h @ W_out.T + b_out
            a_in = _seg_mean(feat_in[src], dst, N)
            a_out = _seg_mean(feat_out[dst], src, N)
            a = jnp.concatenate((a_in, a_out), axis=1)
            h = _gru_cell(a, h, w_ih, w_hh, b_ih, b_hh)
        return h

    def _L3_gnn_ref(x, edge_src, edge_dst, W, b, gamma, beta):
        import jax, jax.numpy as jnp
        import numpy as np
        TAU = 1.0
        EPS = 1e-30
        LN_EPS = 1e-05

        def _scatter_logsumexp(src, index, dim_size):
            scaled = src.astype(jnp.float32) / TAU
            mx = jax.ops.segment_max(scaled, index, num_segments=dim_size)
            exp_val = jnp.exp(scaled - mx[index])
            sum_exp = jax.ops.segment_sum(exp_val, index, num_segments=dim_size)
            out = TAU * (mx + jnp.log(jnp.maximum(sum_exp, EPS)))
            deg = jax.ops.segment_sum(jnp.ones_like(index, dtype=jnp.int32), index, num_segments=dim_size)
            return jnp.where((deg > 0)[:, None], out, 0.0)
        N = x.shape[0]
        src_feat = x[edge_src]
        agg = _scatter_logsumexp(src_feat, edge_dst, N)
        h = jnp.concatenate([x, agg], axis=-1) @ W + b
        mean = jnp.mean(h, axis=-1, keepdims=True)
        var = jnp.var(h, axis=-1, keepdims=True)
        h = (h - mean) * jax.lax.rsqrt(var + LN_EPS) * gamma + beta
        return jax.nn.relu(h)
    edge_index = jnp.stack([src, dst])
    x = _layernorm(x + _L0_gnn_ref(x, src, dst, L0_gnn_W, L0_gnn_attn_l, L0_gnn_attn_r, L0_gnn_bias), axis=-1)
    x = _layernorm(x + _L1_gnn_ref(x, edge_index, L1_gnn_W, L1_gnn_b), axis=-1)
    x = _layernorm(x + _L2_gnn_ref(x, src, dst, L2_gnn_W_in, L2_gnn_b_in, L2_gnn_W_out, L2_gnn_b_out, L2_gnn_w_ih, L2_gnn_w_hh, L2_gnn_b_ih, L2_gnn_b_hh), axis=-1)
    x = _layernorm(x + _L3_gnn_ref(x, src, dst, L3_gnn_W, L3_gnn_b, L3_gnn_gamma, L3_gnn_beta), axis=-1)
    return x

_drawn_inputs = setup_inputs


def setup_inputs(seed=0):
    import zlib

    import numpy as np

    out = dict(_drawn_inputs(seed))
    spreads = {'L0_gnn_bias': (0.0, 0.1),
     'L2_gnn_b_in': (0.0, 0.662),
     'L2_gnn_b_out': (0.0, 0.616),
     'L2_gnn_b_ih': (0.0, 0.1),
     'L2_gnn_b_hh': (0.0, 0.395),
     'L3_gnn_b': (0.0, 0.1),
     'L3_gnn_gamma': (1.0, 0.2),
     'L3_gnn_beta': (0.0, 0.1)}
    factors = {'L0_gnn_attn_r': 3.581, 'L1_gnn_b': 3.192}
    for name, (base, spread) in spreads.items():
        noise = np.random.default_rng([zlib.crc32(name.encode()), seed]).standard_normal(out[name].shape)
        drawn = base * np.exp(spread * noise) if base else spread * noise
        out[name] = jnp.asarray(drawn.astype(out[name].dtype))
    for name, factor in factors.items():
        out[name] = (out[name] * factor).astype(out[name].dtype)
    return out
```

```python
import numpy as np
from contextlib import ExitStack, contextmanager

import concourse.bass as bass
from concourse import mybir

F32 = mybir.dt.float32
BF16 = mybir.dt.bfloat16
I32 = mybir.dt.int32
ALU = mybir.AluOpType
ACT = mybir.ActivationFunctionType
AX = mybir.AxisListType.X

P = 128
D = 128
N = 100000
E = 25000
K = 4
CH = K * P
NCH = 2 * -(-E // (2 * CH))
SLOTS = NCH * CH
T = SLOTS // P
HEADS, PER_HEAD = 8, 16
GROUPS, PER_GROUP = 4, 32
ROUTINGS = 6
LN_EPS = 1e-5
OUTSIDE = 1 << 20
RADIX_BITS = (6, 6, 5)
NEG = -1e30
AW = D + 4


class Step:
    CREDIT = 2

    def __init__(self, sem):
        self.sem = sem

    def wait(self, eng, chunk, back=0):
        eng.wait_ge(self.sem, chunk + (self.CREDIT + 1 - back))


class Dma:

    def __init__(self, sems, each, primed):
        self.sems, self.each, self.primed = sems, each, primed

    def wait(self, eng, pair, u):
        eng.wait_ge(self.sems[u], pair * (16 * self.each) + 16 * self.each + 16 * self.primed)

    def wait_before(self, eng, pair, u):
        eng.wait_ge(self.sems[u], pair * (16 * self.each) + 16)

    def wait_all(self, eng, pairs):
        for s in self.sems:
            eng.wait_ge(s, 16 * (self.each * pairs + self.primed))


class Phase:

    def __init__(self, nc, name, primer):
        self.nc, self.name, self.primer = nc, name, primer
        self.ctx = ExitStack()
        self.steps, self.dmas, self.sems = [], [], []

    def sb(self, name, shape, dt=F32):
        return self.ctx.enter_context(self.nc.sbuf_tensor(f"{self.name}_{name}", shape, dt))

    def ps(self, name, shape, dt=F32):
        return self.ctx.enter_context(self.nc.psum_tensor(f"{self.name}_ps_{name}", shape, dt))

    def sem(self, name):
        s = self.nc.alloc_semaphore(f"{self.name}_{name}")
        self.sems.append(s)
        return s

    def step(self, name):
        self.steps.append(Step(self.sem(name)))
        return self.steps[-1]

    def dma(self, name, each=1, primed_by=None):
        d = Dma([self.sem(f"{name}{u}") for u in range(2)], each, int(primed_by is not None))
        if primed_by:
            self.dmas.append((d, primed_by))
        return d

    def prime(self, eng, who):
        for n, (d, by) in enumerate(self.dmas):
            if by == who:
                for u in range(2):
                    eng.dma_start(self.primer[0][2 * n + u], self.primer[1][2 * n + u]).then_inc(d.sems[u], 16)
        if who == "sp":
            for s in self.steps:
                eng.sem_inc(s.sem, Step.CREDIT)

    def close(self):
        self.ctx.close()
        self.nc.clear_and_free_semaphores(self.sems)
        self.nc.all_engine_barrier()


def chunks(eng, n=NCH):
    with eng.Fori(0, n // 2) as i:
        for u in range(2):
            yield 2 * i + u, i, u


def chain(eng, sem, per_chunk):
    def link(ins, chunk, n):
        ins.then_inc(sem, 1)
        eng.wait_ge(sem, chunk * per_chunk + n)
    return link


def rank_and_scatter(nc, primer, name, shift, bits, load, table_out, iota_in, tri_in, ones_in):
    B = 1 << bits
    SC = 10
    ph = Phase(nc, name, primer)
    pairs = ph.sb("pairs", [P, T, 2], I32)
    dig_i = ph.sb("dig_i", [P, T], I32)
    dig = ph.sb("dig", [P, T])
    onehot = ph.sb("onehot", [P, B, T], BF16)
    count = ph.sb("count", [P, B, T])
    iota = ph.sb("iota", [P, B])
    tri = ph.sb("tri", [P, P])
    ones = ph.sb("ones", [P, P])
    ends = ph.sb("ends", [P, B])
    before = ph.sb("before", [P, B])
    held = ph.sb("held", [P, B])
    cum = ph.sb("cum", [P, B])
    base = ph.sb("base", [P, B])
    rank = ph.sb("rank", [P, T])
    rank_i = ph.sb("rank_i", [P, T], I32)
    st_rank = ph.sb("st_rank", [P, 2, SC], I32)
    st_pair = ph.sb("st_pair", [P, 2, SC, 2], I32)
    ps_below = ph.ps("below", [P, B])
    ps_total = ph.ps("total", [P, B])
    loaded, ranked, counted, summed, link_s = (ph.sem(x) for x in ("loaded", "ranked", "counted", "summed", "link"))
    staged = ph.sem("staged")
    passed = ph.sem("passed")
    scattered = ph.dma("scattered", each=SC, primed_by="pool")
    n_loads = [0]

    with nc.Block() as block:
        @block.sync
        def _(sp):
            ph.prime(sp, "sp")
            for dst, src in ((iota[:], iota_in[:, 0:B]), (tri[:], tri_in), (ones[:], ones_in)):
                sp.dma_start(dst, src).then_inc(loaded, 16)
            n_loads[0] = 3 + load(sp, pairs, loaded)

        @block.vector
        def _(dve):
            v = nc.vector
            n = [0]

            def link(ins):
                n[0] += 1
                ins.then_inc(link_s, 1)
                dve.wait_ge(link_s, n[0])

            dve.wait_ge(loaded, 16 * n_loads[0])
            link(v.tensor_scalar(dig_i[:], pairs[:, :, 0], shift, B - 1, ALU.logical_shift_right, ALU.bitwise_and))
            link(v.tensor_copy(dig[:], dig_i[:]))
            link(v.tensor_tensor(onehot[:], dig[:, None, :].to_broadcast([P, B, T]),
                                 iota[:, :, None].to_broadcast([P, B, T]), ALU.is_equal))
            flat_hot = onehot[:].rearrange("p b t -> p (b t)")
            flat = count[:].rearrange("p b t -> p (b t)")
            link(v.tensor_tensor_scan(out=flat, data0=flat_hot, data1=flat_hot, initial=0.0, op0=ALU.add, op1=ALU.max))
            link(v.tensor_copy(ends[:], count[:, :, T - 1]))
            v.memset(before[:, 0:1], 0.0)
            link(v.tensor_copy(before[:, 1:B], ends[:, 0:B - 1]))
            v.tensor_tensor(held[:], ends[:], before[:], ALU.subtract).then_inc(counted, 1)
            dve.wait_ge(summed, 1)
            link(v.tensor_copy(held[:], ps_total[:]))
            link(v.tensor_tensor_scan(out=cum[:], data0=held[:], data1=held[:], initial=0.0, op0=ALU.add, op1=ALU.max))
            link(v.tensor_tensor(base[:], cum[:], held[:], ALU.subtract))
            link(v.tensor_tensor(base[:], base[:], ps_below[:], ALU.add))
            link(v.scalar_tensor_tensor(base[:], base[:], -1.0, before[:], ALU.add, ALU.subtract))
            link(v.tensor_tensor(count[:], count[:], base[:, :, None].to_broadcast([P, B, T]), ALU.add))
            link(v.tensor_tensor(count[:], count[:], onehot[:], ALU.mult))
            link(v.tensor_reduce(rank[:], count[:].rearrange("p b t -> p t b"), AX, ALU.add))
            v.tensor_copy(rank_i[:], rank[:]).then_inc(ranked, 1)

        @block.tensor
        def _(pe):
            pe.wait_ge(loaded, 48)
            pe.wait_ge(counted, 1)
            nc.tensor.matmul(ps_below[:], tri[:], held[:], start=True, stop=True)
            nc.tensor.matmul(ps_total[:], ones[:], held[:], start=True, stop=True).then_inc(summed, 1)

        @block.gpsimd
        def _(pool):
            ph.prime(pool, "pool")
            pool.wait_ge(ranked, 1)
            for c, i, u in chunks(pool, T // SC):
                scattered.wait_before(pool, i, u)
                nc.gpsimd.tensor_copy(st_rank[:, u], rank_i[:, bass.ds(c * SC, SC)])
                nc.gpsimd.tensor_copy(st_pair[:, u], pairs[:, bass.ds(c * SC, SC), :]).then_inc(staged, 1)
                pool.wait_ge(staged, c + 1)
                pool.sem_inc(passed, 1)
                for k in range(SC):
                    nc.gpsimd.indirect_dma_start(
                        table_out, bass.IndirectOffsetOnAxis(ap=st_rank[:, u, k:k + 1], axis=0),
                        st_pair[:, u, k], None).then_inc(scattered.sems[u], 16)
            scattered.wait_all(pool, T // SC // 2)
    ph.close()


def sort_edges(nc, primer, src, dst, tables, consts):
    own = E // T

    def load_inputs(sp, pairs, loaded):
        sp.dma_start(pairs[own:P], consts["padding"][own:P]).then_inc(loaded, 16)
        with nc.allow_non_contiguous_dma(reason="interleaves the edge list once"):
            sp.dma_start(pairs[0:own, :, 0], dst.rearrange("(p t) -> p t", t=T)).then_inc(loaded, 16)
            sp.dma_start(pairs[0:own, :, 1], src.rearrange("(p t) -> p t", t=T)).then_inc(loaded, 16)
        return 3

    def load_table(table):
        def load(sp, pairs, loaded):
            sp.dma_start(pairs[:], table.rearrange("(p t) w -> p t w", t=T)).then_inc(loaded, 16)
            return 1
        return load

    loads = [load_inputs, load_table(tables[0]), load_table(tables[1])]
    outs = [tables[0], tables[1], tables[0]]
    shift = 0
    for n, bits in enumerate(RADIX_BITS):
        rank_and_scatter(nc, primer, f"sort{n}", shift, bits, loads[n], outs[n], consts["iota"], consts["tri"], consts["ones"])
        shift += bits


def slot_tables(nc, primer, table, masks, lists, src_row, idx, src_col):
    ph = Phase(nc, "slots", primer)
    pairs = ph.sb("pairs", [P, T, 2], I32)
    edge = ph.sb("edge", [P, 2, 2], I32)
    key = ph.sb("key", [P, T + 2])
    mk = ph.sb("mk", [P, 6, T], BF16)
    same = ph.sb("same", [P, 2, T])
    row = ph.sb("row", [P, 6, T])
    row_i = ph.sb("row_i", [P, 5, T], I32)
    cleared, loaded, link_s, built, stored, indexed = (
        ph.sem(x) for x in ("cleared", "loaded", "link", "built", "stored", "indexed"))
    flat = table.rearrange("(p t) w -> p t w", t=T)
    with nc.Block() as block:
        @block.sync
        def _(sp):
            sp.dma_start(pairs[:], flat).then_inc(loaded, 16)
            sp.wait_ge(cleared, 1)
            sp.dma_start(edge[1:P, 0], flat[0:P - 1, T - 1]).then_inc(loaded, 16)
            sp.dma_start(edge[0:P - 1, 1], flat[1:P, 0]).then_inc(loaded, 16)
            sp.wait_ge(built, 1)
            for d in range(2):
                for m in range(3):
                    sp.dma_start(masks[d, m].rearrange("(p t) -> p t", t=T), mk[:, 3 * d + m]).then_inc(stored, 16)
            for n in range(5):
                sp.dma_start(lists[n].rearrange("(p t) -> p t", t=T), row_i[:, n]).then_inc(stored, 16)
            sp.dma_start(src_row.rearrange("(p t) -> p t", t=T), row[:, 4]).then_inc(stored, 16)
            sp.wait_ge(stored, 16 * 12)
            with nc.allow_non_contiguous_dma(reason="slot t * 128 + p to partition p, once"):
                for n in range(5):
                    sp.dma_start(idx[:, n], lists[n].rearrange("(t p) -> p t", p=P)).then_inc(indexed, 16)
            sp.wait_ge(indexed, 16 * 5)

        @block.vector
        def _(dve):
            v = nc.vector
            n = [0]

            def link(ins):
                n[0] += 1
                ins.then_inc(link_s, 1)
                dve.wait_ge(link_s, n[0])

            v.memset(edge[:], -1).then_inc(cleared, 1)
            dve.wait_ge(loaded, 48)
            v.tensor_copy(key[:, 1:T + 1], pairs[:, :, 0])
            v.tensor_copy(key[:, 0:1], edge[:, 0, 0:1])
            v.tensor_copy(key[:, T + 1:T + 2], edge[:, 1, 0:1])
            link(v.tensor_copy(row[:, 0], pairs[:, :, 1]))
            v.tensor_tensor(same[:, 0], key[:, 1:T + 1], key[:, 0:T], ALU.is_equal)
            link(v.tensor_tensor(same[:, 1], key[:, 1:T + 1], key[:, 2:T + 2], ALU.is_equal))
            for d in range(2):
                v.tensor_copy(mk[:, 3 * d], same[:, d])
                v.tensor_scalar(mk[:, 3 * d + 1], same[:, d], -1.0, 1.0, ALU.mult, ALU.add)
                v.tensor_scalar(mk[:, 3 * d + 2], same[:, d], -1.0, -NEG, ALU.add, ALU.mult)
            v.tensor_scalar(row[:, 1], key[:, 1:T + 1], float(N - 1), None, ALU.min)
            v.scalar_tensor_tensor(row[:, 2], same[:, 0], float(OUTSIDE), key[:, 1:T + 1], ALU.mult, ALU.add)
            v.scalar_tensor_tensor(row[:, 3], same[:, 1], float(OUTSIDE), key[:, 1:T + 1], ALU.mult, ALU.add)
            link(v.tensor_scalar(row[:, 5], key[:, 1:T + 1], float(N), float(OUTSIDE), ALU.is_ge, ALU.mult))
            link(v.tensor_tensor(row[:, 4], row[:, 5], row[:, 0], ALU.add))
            v.tensor_copy(row_i[:], row[:, 0:5]).then_inc(built, 1)
            dve.wait_ge(indexed, 16 * 5)
            v.tensor_copy(src_col[:], idx[:, 4])
    ph.close()


class Chain:

    def __init__(self, eng, sem, per_pair):
        self.eng, self.sem, self.per_pair, self.n, self.pair = eng, sem, per_pair, 0, 0

    def start(self, pair):
        self.pair, self.n = pair, 0

    def did(self, ins):
        ins.then_inc(self.sem, 1)
        self.n += 1
        return ins

    def sync(self, passed=None):
        self.eng.wait_ge(self.sem, self.pair * self.per_pair + self.n)
        if passed is not None:
            self.eng.sem_inc(passed, 1)

    def end(self):
        assert self.n == self.per_pair, (self.n, self.per_pair)


def pairs(eng, n, peeled=0):
    with eng.Fori(0, n // 2 - peeled) as i:
        yield i
    for i in range(n // 2 - peeled, n // 2):
        yield i


def stream(sp, n, load, store, peeled=0):
    for u in range(2):
        load(u, 0, u)
    with sp.Fori(0, n // 2 - 1 - peeled) as i:
        for u in range(2):
            store(2 * i + u, i, u)
            load(2 * i + u + 2, i + 1, u)
    for i in range(n // 2 - 1 - peeled, n // 2 - 1):
        for u in range(2):
            store(2 * i + u, i, u)
            load(2 * i + u + 2, i + 1, u)
    for u in range(2):
        store(n - 2 + u, n // 2 - 1, u)


def row_norm(nc, chain, passed, src, stats, mv, k=K):
    for j in range(k):
        chain.did(nc.vector.bn_stats(stats[:, j], src[:, j]))
    chain.sync(passed)
    for j in range(k):
        last = nc.vector.bn_aggr(mv[:, j], stats[:, j])
    return last


def row_scale(nc, out, src, mv, rstd, k=K):
    for j in range(k):
        last = nc.vector.tensor_scalar(out[:, j], src[:, j], mv[:, j, 0:1], rstd[:, j:j + 1], ALU.subtract, ALU.mult)
    return last


def spread(row):
    return row[None, :].to_broadcast([P, row.shape[0]])


NG = -(-N // CH) // 2 * 2 + (-(-N // CH)) % 2 * 2
assert NG * CH >= N and (NG - 1) * CH < N


def group_rows(table, c):
    start = N - CH if isinstance(c, int) and c == NG - 1 else c * CH
    return table[bass.ds(start, CH)].rearrange("(p k) d -> p k d", k=K)


def dense_first(nc, primer, x, x1, x2, w1t, bias0, b1, ident, small, tables_to_clear):
    ph = Phase(nc, "d1", primer)
    W = ph.sb("w", [P, D]); B0 = ph.sb("b0", [P, D]); B1 = ph.sb("b1", [P, D]); I = ph.sb("i", [P, P])
    sm = ph.sb("sm", [P, 4])
    zeros = ph.sb("zeros", [P, 5000])
    xin = ph.sb("xin", [P, 2, K, D]); xb = ph.sb("xb", [P, 2, K, D]); x1r = ph.sb("x1r", [P, 2, K, D])
    x1t = ph.sb("x1t", [P, 2, CH]); h = ph.sb("h", [P, 2, K, D]); sq = ph.sb("sq", [P, 2, K, D])
    hn = ph.sb("hn", [P, 2, K, D]); y = ph.sb("y", [P, 2, K, D]); x2r = ph.sb("x2r", [P, 2, K, D])
    st = ph.sb("st", [P, 2, 2, K, 6]); mv = ph.sb("mv", [P, 2, 2, K, 2])
    lnv = ph.sb("lnv", [P, 2, 2, K]); rstd = ph.sb("rstd", [P, 2, 2, K])
    n2 = ph.sb("n2", [P, 2, K * GROUPS]); ln2 = ph.sb("ln2", [P, 2, K * GROUPS]); rn = ph.sb("rn", [P, 2, K * GROUPS])
    ps_t = ph.ps("t", [P, 2, CH]); ps_h = ph.ps("h", [P, 2, K, D])
    consts, cleared = ph.sem("consts"), ph.sem("cleared")
    zero = ph.sem("zero")
    vchain, achain, passed = ph.sem("vchain"), ph.sem("achain"), ph.sem("passed")
    loaded = ph.dma("loaded")
    stored1 = ph.dma("stored1", primed_by="sp"); stored2 = ph.dma("stored2", primed_by="sp")
    biased, moved0, scaled0, x1_made, x1_turned, x1t_made, h_made, h_biased, squared, summed, n_made, h_normed, \
        added, moved1, scaled1, x2_made = (ph.step(s) for s in (
            "biased", "moved0", "scaled0", "x1_made", "x1_turned", "x1t_made", "h_made", "h_biased", "squared",
            "summed", "n_made", "h_normed", "added", "moved1", "scaled1", "x2_made"))
    with nc.Block() as block:
        @block.sync
        def _(sp):
            ph.prime(sp, "sp")
            for a, b in ((W[:], w1t), (B0[:], spread(bias0)), (B1[:], spread(b1)), (I[:], ident), (sm[:], small)):
                sp.dma_start(a, b).then_inc(consts, 16)

            def load(c, i, u):
                biased.wait(sp, c, back=2)
                sp.dma_start(xin[:, u], group_rows(x, c)).then_inc(loaded.sems[u], 16)

            def store(c, i, u):
                if isinstance(c, int) and c == NG - 1:
                    stored1.wait(sp, i, 0)
                    stored2.wait(sp, i, 0)
                x1_made.wait(sp, c)
                sp.dma_start(group_rows(x1, c), x1r[:, u]).then_inc(stored1.sems[u], 16)
                x2_made.wait(sp, c)
                sp.dma_start(group_rows(x2, c), x2r[:, u]).then_inc(stored2.sems[u], 16)
            stream(sp, NG, load, store, peeled=1)
            stored1.wait_all(sp, NG // 2)
            stored2.wait_all(sp, NG // 2)

        @block.gpsimd
        def _(pool):
            g = nc.gpsimd
            pool.wait_ge(consts, 80)
            for i in pairs(pool, NG):
                for u in range(2):
                    c = 2 * i + u
                    loaded.wait(pool, i, u)
                    x1_made.wait(pool, c, back=2)
                    g.tensor_tensor(xb[:, u], xin[:, u], B0[:, None, :].to_broadcast([P, K, D]), ALU.add).then_inc(biased.sem, 1)
                for u in range(2):
                    c = 2 * i + u
                    h_normed.wait(pool, c)
                    x2_made.wait(pool, c, back=2)
                    g.tensor_tensor(y[:, u], hn[:, u], x1r[:, u], ALU.add).then_inc(added.sem, 1)

        @block.vector
        def _(dve):
            v = nc.vector
            v.memset(zeros[:], 0.0).then_inc(zero, 1)
            dve.wait_ge(consts, 80)
            ch = Chain(dve, vchain, 18)
            for i in pairs(dve, NG):
                ch.start(i)
                for u in range(2):
                    biased.wait(dve, 2 * i + u)
                    row_norm(nc, ch, passed, xb[:, u], st[:, u, 0], mv[:, u, 0]).then_inc(moved0.sem, 1)
                for u in range(2):
                    c = 2 * i + u
                    scaled0.wait(dve, c)
                    stored1.wait_before(dve, i, u)
                    added.wait(dve, c, back=2)
                    x1_turned.wait(dve, c, back=2)
                    row_scale(nc, x1r[:, u], xb[:, u], mv[:, u, 0], rstd[:, u, 0]).then_inc(x1_made.sem, 1)
                for u in range(2):
                    c = 2 * i + u
                    h_made.wait(dve, c)
                    h_normed.wait(dve, c, back=2)
                    squared.wait(dve, c, back=2)
                    v.tensor_tensor(h[:, u], ps_h[:, u], B1[:, None, :].to_broadcast([P, K, D]), ALU.add).then_inc(h_biased.sem, 1)
                for u in range(2):
                    c = 2 * i + u
                    squared.wait(dve, c)
                    ch.did(v.tensor_reduce(n2[:, u], sq[:, u].rearrange("p k (g e) -> p (k g) e", g=GROUPS), AX, ALU.add))
                    ch.sync()
                    v.tensor_scalar(n2[:, u], n2[:, u], 1e-25, None, ALU.max).then_inc(summed.sem, 1)
                for u in range(2):
                    c = 2 * i + u
                    n_made.wait(dve, c)
                    h_biased.wait(dve, c)
                    added.wait(dve, c, back=2)
                    v.tensor_tensor(hn[:, u].rearrange("p k (g e) -> p (k g) e", g=GROUPS),
                                    h[:, u].rearrange("p k (g e) -> p (k g) e", g=GROUPS),
                                    rn[:, u][:, :, None].to_broadcast([P, K * GROUPS, PER_GROUP]), ALU.mult).then_inc(h_normed.sem, 1)
                for u in range(2):
                    added.wait(dve, 2 * i + u)
                    row_norm(nc, ch, passed, y[:, u], st[:, u, 1], mv[:, u, 1]).then_inc(moved1.sem, 1)
                for u in range(2):
                    c = 2 * i + u
                    scaled1.wait(dve, c)
                    stored2.wait_before(dve, i, u)
                    row_scale(nc, x2r[:, u], y[:, u], mv[:, u, 1], rstd[:, u, 1]).then_inc(x2_made.sem, 1)
                ch.end()

        @block.scalar
        def _(act):
            a = nc.scalar
            a.preload_act_table_set("natural_log_exp_and_others")
            act.wait_ge(consts, 80)
            act.wait_ge(zero, 1)
            n_clear = 0
            for t in tables_to_clear:
                rows = t.rearrange("a b -> (a b)").rearrange("(p c) -> p c", p=P)
                for lo in range(0, rows.shape[1], 5000):
                    w = min(5000, rows.shape[1] - lo)
                    act.dma_start(rows[:, lo:lo + w], zeros[:, 0:w]).then_inc(cleared, 16)
                    n_clear += 1
            ch = Chain(act, achain, 6)
            for i in pairs(act, NG):
                ch.start(i)
                for u in range(2):
                    c = 2 * i + u
                    moved0.wait(act, c)
                    ch.did(a.activation(lnv[:, u, 0], mv[:, u, 0, :, 1], ACT.Ln, bias=sm[:, 0:1]))
                    ch.sync()
                    a.activation(rstd[:, u, 0], lnv[:, u, 0], ACT.Exp, scale=-0.5).then_inc(scaled0.sem, 1)
                for u in range(2):
                    c = 2 * i + u
                    x1_turned.wait(act, c)
                    h_made.wait(act, c, back=2)
                    a.copy(x1t[:, u], ps_t[:, u]).then_inc(x1t_made.sem, 1)
                for u in range(2):
                    c = 2 * i + u
                    h_biased.wait(act, c)
                    summed.wait(act, c, back=2)
                    a.activation(sq[:, u], h[:, u], ACT.Square).then_inc(squared.sem, 1)
                for u in range(2):
                    c = 2 * i + u
                    summed.wait(act, c)
                    ch.did(a.activation(ln2[:, u], n2[:, u], ACT.Ln, scale=2.0 ** 20))
                    ch.sync()
                    a.activation(rn[:, u], ln2[:, u], ACT.Exp, scale=-0.5, bias=sm[:, 1:2]).then_inc(n_made.sem, 1)
                for u in range(2):
                    c = 2 * i + u
                    moved1.wait(act, c)
                    ch.did(a.activation(lnv[:, u, 1], mv[:, u, 1, :, 1], ACT.Ln, bias=sm[:, 0:1]))
                    ch.sync()
                    a.activation(rstd[:, u, 1], lnv[:, u, 1], ACT.Exp, scale=-0.5).then_inc(scaled1.sem, 1)
                ch.end()
            act.wait_ge(cleared, 16 * n_clear)

        @block.tensor
        def _(pe):
            pe.wait_ge(consts, 80)
            for i in pairs(pe, NG):
                for u in range(2):
                    c = 2 * i + u
                    x1_made.wait(pe, c)
                    x1t_made.wait(pe, c, back=2)
                    for k in range(K):
                        last = nc.tensor.transpose(ps_t[:, u, k * P:(k + 1) * P], x1r[:, u, k], I[:])
                    last.then_inc(x1_turned.sem, 1)
                for u in range(2):
                    c = 2 * i + u
                    x1t_made.wait(pe, c)
                    h_biased.wait(pe, c, back=2)
                    for k in range(K):
                        last = nc.tensor.matmul(ps_h[:, u, k], x1t[:, u, k * P:(k + 1) * P], W[:], start=True, stop=True)
                    last.then_inc(h_made.sem, 1)
    ph.close()


SRC, DST, FIRST, LAST, SRC_OUT = range(5)


class Rows:

    def __init__(self, ph, nc, idx, name, n_lists):
        self.nc, self.idx = nc, idx
        self.at = ph.sb(f"{name}_at", [P, 2, n_lists, K], I32)
        self.staged, self.passed = ph.sem(f"{name}_staged"), ph.sem(f"{name}_passed")
        self.n_lists = n_lists

    def stage(self, pool, chunk, count, u, lists):
        for n, which in enumerate(lists):
            last = self.nc.gpsimd.tensor_copy(self.at[:, u, n], self.idx[:, which, bass.ds(chunk * K, K)])
        last.then_inc(self.staged, 1)
        pool.wait_ge(self.staged, count + 1)
        pool.sem_inc(self.passed, 1)

    def gather(self, u, n, rows, table, sem):
        for k in range(K):
            self.nc.gpsimd.indirect_dma_start(rows[:, k], None, table, bass.IndirectOffsetOnAxis(
                ap=self.at[:, u, n, k:k + 1], axis=0)).then_inc(sem, 16)

    def scatter(self, u, n, rows, table, sem):
        for k in range(K):
            self.nc.gpsimd.indirect_dma_start(table, bass.IndirectOffsetOnAxis(
                ap=self.at[:, u, n, k:k + 1], axis=0), rows[:, k], None,
                bounds_check=N - 1, oob_is_err=False).then_inc(sem, 16)


def mask_rows(masks, direction, first, n, chunk):
    return masks[direction, first:first + n, bass.ds(chunk * CH, CH)][None].to_broadcast([P, n, CH])


def gat_forward(nc, primer, x, idx, masks, w0, wt0, al, ar, bo16, ident, l0t, xd0):
    ph = Phase(nc, "g0", primer)
    W = ph.sb("w", [P, D]); WT = ph.sb("wt", [P, D]); B16 = ph.sb("b16", [P, P]); I = ph.sb("i", [P, P])
    acol = ph.sb("acol", [P, 2]); ab = ph.sb("ab", [P, 2, P]); WA = ph.sb("wa", [P, 2, P])
    rows = ph.sb("rows", [P, 2, 2, K, D])
    xt = ph.sb("xt", [P, 2, 2, CH]); mk = ph.sb("mk", [P, 2, 1, CH], BF16)
    er = ph.sb("er", [P, 2, CH]); o = ph.sb("o", [P, 2, 3, CH])
    ps_x = ph.ps("x", [P, 2, 2, CH]); ps_ze = ph.ps("ze", [P, 2, 2, CH])
    rr = Rows(ph, nc, idx, "rows", 2)
    consts, ready, vinit = ph.sem("consts"), ph.sem("ready"), ph.sem("vinit")
    gathered = ph.dma("gathered", each=2 * K)
    masked = ph.dma("masked")
    stored = ph.dma("stored", each=2, primed_by="sp")
    turned, moved, made, copied, scanned = (ph.step(s) for s in ("turned", "moved", "made", "copied", "scanned"))
    moved_v = ph.step("moved_v")
    vchain = ph.sem("vchain")
    with nc.Block() as block:
        @block.sync
        def _(sp):
            ph.prime(sp, "sp")
            for a, b in ((W[:], w0), (WT[:], wt0), (B16[:], bo16), (I[:], ident), (acol[:, 0:1], al), (acol[:, 1:2], ar)):
                sp.dma_start(a, b).then_inc(consts, 16)

            def load(c, i, u):
                scanned.wait(sp, c, back=2)
                sp.dma_start(mk[:, u], mask_rows(masks, 0, 2, 1, c)).then_inc(masked.sems[u], 16)

            def store(c, i, u):
                scanned.wait(sp, c)
                copied.wait(sp, c)
                sp.dma_start(l0t[c], o[:, u]).then_inc(stored.sems[u], 16)
                gathered.wait(sp, i, u)
                sp.dma_start(xd0[c], rows[:, u, 1]).then_inc(stored.sems[u], 16)
            stream(sp, NCH, load, store)
            stored.wait_all(sp, NCH // 2)

        @block.gpsimd
        def _(pool):
            for i in pairs(pool, NCH):
                for u in range(2):
                    c = 2 * i + u
                    turned.wait(pool, c, back=2)
                    stored.wait_before(pool, i, u)
                    rr.stage(pool, c, c, u, (SRC, DST))
                    rr.gather(u, 0, rows[:, u, 0], x, gathered.sems[u])
                    rr.gather(u, 1, rows[:, u, 1], x, gathered.sems[u])

        @block.vector
        def _(dve):
            v = nc.vector
            dve.wait_ge(consts, 96)
            for j in range(2):
                v.tensor_scalar(ab[:, j], B16[:], acol[:, j:j + 1], None, ALU.mult).then_inc(vinit, 1)
            dve.wait_ge(ready, 1)
            v.memset(o[:, 1, 2, CH - 1:CH], 0.0).then_inc(vinit, 1)
            v.tensor_copy(WA[:], ps_x[:, 0, 0, 0:2 * P].rearrange("p (j o) -> p j o", j=2)).then_inc(vinit, 1)
            dve.wait_ge(vinit, 4)
            ch = Chain(dve, vchain, 4)
            for i in pairs(dve, NCH):
                ch.start(i)
                for u in range(2):
                    c = 2 * i + u
                    turned.wait(dve, c)
                    made.wait(dve, c, back=2)
                    v.tensor_copy(xt[:, u, 1], ps_x[:, u, 1]).then_inc(moved_v.sem, 1)
                for u in range(2):
                    c = 2 * i + u
                    copied.wait(dve, c)
                    stored.wait_before(dve, i, u)
                    masked.wait(dve, i, u)
                    ch.did(v.scalar_tensor_tensor(o[:, u, 1], er[:, u], 0.2, er[:, u], ALU.mult, ALU.max))
                    ch.sync()
                    ch.did(v.tensor_tensor_scan(out=o[:, u, 2], data0=mk[:, u, 0], data1=o[:, u, 1],
                                                initial=o[:, 1 - u, 2, CH - 1:CH], op0=ALU.add, op1=ALU.max))
                    ch.sync()
                    dve.sem_inc(scanned.sem, 1)
                ch.end()

        @block.scalar
        def _(act):
            a = nc.scalar
            for i in pairs(act, NCH):
                for u in range(2):
                    c = 2 * i + u
                    turned.wait(act, c)
                    made.wait(act, c, back=2)
                    a.copy(xt[:, u, 0], ps_x[:, u, 0]).then_inc(moved.sem, 1)
                for u in range(2):
                    c = 2 * i + u
                    made.wait(act, c)
                    stored.wait_before(act, i, u)
                    scanned.wait(act, c, back=2)
                    a.copy(o[:, u, 0], ps_ze[:, u, 0])
                    a.copy(er[:, u], ps_ze[:, u, 1]).then_inc(copied.sem, 1)

        @block.tensor
        def _(pe):
            t = nc.tensor
            pe.wait_ge(consts, 96)
            pe.wait_ge(vinit, 2)
            for j in range(2):
                last = t.matmul(ps_x[:, 0, 0, j * P:(j + 1) * P], WT[:], ab[:, j], start=True, stop=True)
            last.then_inc(ready, 1)
            pe.wait_ge(vinit, 4)
            for i in pairs(pe, NCH):
                for u in range(2):
                    c = 2 * i + u
                    gathered.wait(pe, i, u)
                    moved.wait(pe, c, back=2)
                    moved_v.wait(pe, c, back=2)
                    for j in range(2):
                        for k in range(K):
                            last = t.transpose(ps_x[:, u, j, k * P:(k + 1) * P], rows[:, u, j, k], I[:])
                    last.then_inc(turned.sem, 1)
                for u in range(2):
                    c = 2 * i + u
                    moved.wait(pe, c)
                    moved_v.wait(pe, c)
                    copied.wait(pe, c, back=2)
                    t.matmul(ps_ze[:, u, 0], W[:], xt[:, u, 0], start=True, stop=True)
                    t.matmul(ps_ze[:, u, 1], WA[:, 0], xt[:, u, 0], start=True, stop=False)
                    t.matmul(ps_ze[:, u, 1], WA[:, 1], xt[:, u, 1], start=False, stop=True).then_inc(made.sem, 1)
    ph.close()


def gat_backward(nc, primer, idx, masks, bias0, sel8, ident, small, l0t, xd0, x1):
    ph = Phase(nc, "g1", primer)
    B0 = ph.sb("b0", [P, D]); S8 = ph.sb("s8", [P, HEADS]); I = ph.sb("i", [P, P]); sm = ph.sb("sm", [P, 4])
    zem = ph.sb("zem", [P, 2, 3, CH]); xd = ph.sb("xd", [P, 2, K, D]); mk = ph.sb("mk", [P, 2, 2, CH], BF16)
    t1 = ph.sb("t1", [P, 2, CH]); mx = ph.sb("mx", [P, 2, CH]); a_ = ph.sb("a", [P, 2, CH]); msg = ph.sb("msg", [P, 2, CH])
    nd = ph.sb("nd", [P, 2, 2, CH])
    xb = ph.sb("xb", [P, 2, K, D]); den = ph.sb("den", [P, 2, K * HEADS]); agg = ph.sb("agg", [P, 2, K, D])
    st = ph.sb("st", [P, 2, K, 6]); mv = ph.sb("mv", [P, 2, K, 2]); lnv = ph.sb("lnv", [P, 2, K]); rstd = ph.sb("rstd", [P, 2, K])
    x1r = ph.sb("x1r", [P, 2, K, D])
    ps_n = ph.ps("n", [P, 2, CH]); ps_d = ph.ps("d", [P, 2, CH])
    rr = Rows(ph, nc, idx, "rows", 1)
    consts, vinit, vchain, achain, passed = (ph.sem(s) for s in ("consts", "vinit", "vchain", "achain", "passed"))
    loaded = ph.dma("loaded", each=3)
    scattered = ph.dma("scattered", each=K, primed_by="pool")
    started, shifted, exped, weighed, scanned, turned, meaned, scaled, x1_made, biased = (ph.step(s) for s in (
        "started", "shifted", "exped", "weighed", "scanned", "turned", "meaned", "scaled", "x1_made", "biased"))
    back = lambda c: c * -1 + (NCH - 1)
    with nc.Block() as block:
        @block.sync
        def _(sp):
            ph.prime(sp, "sp")
            for a, b in ((B0[:], spread(bias0)), (S8[:], sel8), (I[:], ident), (sm[:], small)):
                sp.dma_start(a, b).then_inc(consts, 16)
            for i in pairs(sp, NCH):
                for u in range(2):
                    c = 2 * i + u
                    scanned.wait(sp, c, back=2)
                    biased.wait(sp, c, back=2)
                    sp.dma_start(zem[:, u], l0t[back(c)]).then_inc(loaded.sems[u], 16)
                    sp.dma_start(xd[:, u], xd0[back(c)]).then_inc(loaded.sems[u], 16)
                    sp.dma_start(mk[:, u], mask_rows(masks, 1, 0, 2, back(c))).then_inc(loaded.sems[u], 16)

        @block.gpsimd
        def _(pool):
            g = nc.gpsimd
            ph.prime(pool, "pool")
            pool.wait_ge(consts, 64)
            for i in pairs(pool, NCH):
                for u in range(2):
                    c = 2 * i + u
                    loaded.wait(pool, i, u)
                    shifted.wait(pool, c, back=2)
                    g.tensor_tensor(t1[:, u], mk[:, u, 1], zem[:, u, 2], ALU.mult).then_inc(started.sem, 1)
                    meaned.wait(pool, c, back=2)
                    g.tensor_tensor(xb[:, u], xd[:, u], B0[:, None, :].to_broadcast([P, K, D]), ALU.add).then_inc(biased.sem, 1)
                for u in range(2):
                    c = 2 * i + u
                    exped.wait(pool, c)
                    scanned.wait(pool, c, back=2)
                    g.tensor_tensor(msg[:, u], zem[:, u, 0], a_[:, u], ALU.mult).then_inc(weighed.sem, 1)
                for u in range(2):
                    c = 2 * i + u
                    scattered.wait_before(pool, i, u)
                    x1_made.wait(pool, c)
                    rr.stage(pool, back(c), c, u, (FIRST,))
                    rr.scatter(u, 0, x1r[:, u], x1, scattered.sems[u])
            scattered.wait_all(pool, NCH // 2)

        @block.vector
        def _(dve):
            v = nc.vector
            v.memset(mx[:, 1, 0:1], 0.0).then_inc(vinit, 1)
            v.memset(nd[:, 1, :, 0:1], 0.0).then_inc(vinit, 1)
            dve.wait_ge(vinit, 2)
            ch = Chain(dve, vchain, 2 + 4 + 8 + 2 * K)
            for i in pairs(dve, NCH):
                ch.start(i)
                for u in range(2):
                    c = 2 * i + u
                    started.wait(dve, c)
                    ch.did(v.tensor_tensor_scan(out=mx[:, u, ::-1], data0=mk[:, u, 0, ::-1], data1=t1[:, u, ::-1],
                                                initial=mx[:, 1 - u, 0:1], op0=ALU.mult, op1=ALU.add))
                    ch.sync()
                    exped.wait(dve, c, back=2)
                    v.tensor_tensor(zem[:, u, 1], zem[:, u, 1], mx[:, u], ALU.subtract).then_inc(shifted.sem, 1)
                for u in range(2):
                    c = 2 * i + u
                    weighed.wait(dve, c)
                    turned.wait(dve, c, back=2)
                    for j, src in enumerate((msg, a_)):
                        ch.did(v.tensor_tensor_scan(out=nd[:, u, j, ::-1], data0=mk[:, u, 0, ::-1], data1=src[:, u, ::-1],
                                                    initial=nd[:, 1 - u, j, 0:1], op0=ALU.mult, op1=ALU.add))
                    ch.sync()
                    dve.sem_inc(scanned.sem, 1)
                for u in range(2):
                    c = 2 * i + u
                    turned.wait(dve, c)
                    biased.wait(dve, c)
                    ch.did(v.tensor_scalar(den[:, u], ps_d[:, u, 0:K * HEADS], 1e-9, None, ALU.max))
                    ch.sync()
                    ch.did(v.reciprocal(den[:, u], den[:, u]))
                    ch.sync()
                    ch.did(v.tensor_tensor(agg[:, u].rearrange("p k (h e) -> p (k h) e", h=HEADS),
                                           ps_n[:, u].rearrange("p (g e) -> p g e", e=PER_HEAD),
                                           den[:, u][:, :, None].to_broadcast([P, K * HEADS, PER_HEAD]), ALU.mult))
                    ch.sync()
                    ch.did(v.tensor_tensor(agg[:, u], agg[:, u], xb[:, u], ALU.add))
                    ch.sync()
                    row_norm(nc, ch, passed, agg[:, u], st[:, u], mv[:, u]).then_inc(meaned.sem, 1)
                for u in range(2):
                    c = 2 * i + u
                    scaled.wait(dve, c)
                    scattered.wait_before(dve, i, u)
                    row_scale(nc, x1r[:, u], agg[:, u], mv[:, u], rstd[:, u]).then_inc(x1_made.sem, 1)
                ch.end()

        @block.scalar
        def _(act):
            a = nc.scalar
            a.preload_act_table_set("natural_log_exp_and_others")
            act.wait_ge(consts, 64)
            ch = Chain(act, achain, 2)
            for i in pairs(act, NCH):
                ch.start(i)
                for u in range(2):
                    c = 2 * i + u
                    shifted.wait(act, c)
                    scanned.wait(act, c, back=2)
                    weighed.wait(act, c, back=2)
                    a.activation(a_[:, u], zem[:, u, 1], ACT.Exp).then_inc(exped.sem, 1)
                for u in range(2):
                    c = 2 * i + u
                    meaned.wait(act, c)
                    ch.did(a.activation(lnv[:, u], mv[:, u, :, 1], ACT.Ln, bias=sm[:, 0:1]))
                    ch.sync()
                    x1_made.wait(act, c, back=2)
                    a.activation(rstd[:, u], lnv[:, u], ACT.Exp, scale=-0.5).then_inc(scaled.sem, 1)
                ch.end()

        @block.tensor
        def _(pe):
            t = nc.tensor
            pe.wait_ge(consts, 64)
            for i in pairs(pe, NCH):
                for u in range(2):
                    c = 2 * i + u
                    scanned.wait(pe, c)
                    meaned.wait(pe, c, back=2)
                    for k in range(K):
                        t.transpose(ps_n[:, u, k * P:(k + 1) * P], nd[:, u, 0, k * P:(k + 1) * P], I[:])
                    for k in range(K):
                        last = t.matmul(ps_d[:, u, k * HEADS:(k + 1) * HEADS], nd[:, u, 1, k * P:(k + 1) * P], S8[:],
                                        start=True, stop=True)
                    last.then_inc(turned.sem, 1)
    ph.close()


def route_start(nc, primer, x1, idx, w1t, b1, bo32, ident, small, zt, ct, x1d):
    ph = Phase(nc, "r0", primer)
    W = ph.sb("w", [P, D]); BO = ph.sb("bo", [P, P]); I = ph.sb("i", [P, P]); bcol = ph.sb("bcol", [P, 1]); sm = ph.sb("sm", [P, 4])
    rows = ph.sb("rows", [P, 2, 2, K, D])
    xt = ph.sb("xt", [P, 2, 2, CH]); h = ph.sb("h", [P, 2, 2, CH]); sq = ph.sb("sq", [P, 2, 2, CH])
    n2 = ph.sb("n2", [P, 2, 2, CH]); rn = ph.sb("rn", [P, 2, 2, CH]); o = ph.sb("o", [P, 2, 2, CH])
    ps_x = ph.ps("x", [P, 2, 2, CH]); ps_h = ph.ps("h", [P, 2, 2, CH])
    rr = Rows(ph, nc, idx, "rows", 2)
    consts, achain = ph.sem("consts"), ph.sem("achain")
    gathered = ph.dma("gathered", each=2 * K)
    stored = ph.dma("stored", each=3, primed_by="sp")
    turned, moved, moved_v, made, biased, squared, summed, clamped, inverted, normed, normed_v = (ph.step(s) for s in (
        "turned", "moved", "moved_v", "made", "biased", "squared", "summed", "clamped", "inverted", "normed", "normed_v"))
    with nc.Block() as block:
        @block.sync
        def _(sp):
            ph.prime(sp, "sp")
            for a, b in ((W[:], w1t), (BO[:], bo32), (I[:], ident), (bcol[:], b1[:, None]), (sm[:], small)):
                sp.dma_start(a, b).then_inc(consts, 16)
            for i in pairs(sp, NCH):
                for u in range(2):
                    c = 2 * i + u
                    gathered.wait(sp, i, u)
                    sp.dma_start(x1d[c], rows[:, u, 1]).then_inc(stored.sems[u], 16)
                    normed.wait(sp, c)
                    normed_v.wait(sp, c)
                    sp.dma_start(zt[c], o[:, u, 0]).then_inc(stored.sems[u], 16)
                    sp.dma_start(ct[c], o[:, u, 1]).then_inc(stored.sems[u], 16)
            stored.wait_all(sp, NCH // 2)

        @block.gpsimd
        def _(pool):
            for i in pairs(pool, NCH):
                for u in range(2):
                    c = 2 * i + u
                    turned.wait(pool, c, back=2)
                    stored.wait_before(pool, i, u)
                    rr.stage(pool, c, c, u, (SRC, DST))
                    rr.gather(u, 0, rows[:, u, 0], x1, gathered.sems[u])
                    rr.gather(u, 1, rows[:, u, 1], x1, gathered.sems[u])
                for u in range(2):
                    c = 2 * i + u
                    inverted.wait(pool, c)
                    stored.wait_before(pool, i, u)
                    nc.gpsimd.tensor_tensor(o[:, u, 0], h[:, u, 0], rn[:, u, 0], ALU.mult).then_inc(normed.sem, 1)

        @block.vector
        def _(dve):
            v = nc.vector
            for i in pairs(dve, NCH):
                for u in range(2):
                    c = 2 * i + u
                    turned.wait(dve, c)
                    made.wait(dve, c, back=2)
                    v.tensor_copy(xt[:, u, 1], ps_x[:, u, 1]).then_inc(moved_v.sem, 1)
                for u in range(2):
                    c = 2 * i + u
                    summed.wait(dve, c)
                    inverted.wait(dve, c, back=2)
                    v.tensor_scalar(n2[:, u], ps_x[:, u], 1e-24, None, ALU.max).then_inc(clamped.sem, 1)
                for u in range(2):
                    c = 2 * i + u
                    inverted.wait(dve, c)
                    stored.wait_before(dve, i, u)
                    v.tensor_tensor(o[:, u, 1], h[:, u, 1], rn[:, u, 1], ALU.mult).then_inc(normed_v.sem, 1)

        @block.scalar
        def _(act):
            a = nc.scalar
            a.preload_act_table_set("natural_log_exp_and_others")
            act.wait_ge(consts, 80)
            ch = Chain(act, achain, 2)
            for i in pairs(act, NCH):
                ch.start(i)
                for u in range(2):
                    c = 2 * i + u
                    turned.wait(act, c)
                    made.wait(act, c, back=2)
                    a.copy(xt[:, u, 0], ps_x[:, u, 0]).then_inc(moved.sem, 1)
                for u in range(2):
                    c = 2 * i + u
                    made.wait(act, c)
                    normed.wait(act, c, back=2)
                    normed_v.wait(act, c, back=2)
                    a.activation(h[:, u], ps_h[:, u], ACT.Identity, bias=bcol[:]).then_inc(biased.sem, 1)
                    biased.wait(act, c)
                    summed.wait(act, c, back=2)
                    a.activation(sq[:, u], h[:, u], ACT.Square).then_inc(squared.sem, 1)
                for u in range(2):
                    c = 2 * i + u
                    clamped.wait(act, c)
                    ch.did(a.activation(n2[:, u], n2[:, u], ACT.Ln, scale=2.0 ** 20))
                    ch.sync()
                    a.activation(rn[:, u], n2[:, u], ACT.Exp, scale=-0.5, bias=sm[:, 1:2]).then_inc(inverted.sem, 1)
                ch.end()

        @block.tensor
        def _(pe):
            t = nc.tensor
            pe.wait_ge(consts, 80)
            for i in pairs(pe, NCH):
                for u in range(2):
                    c = 2 * i + u
                    gathered.wait(pe, i, u)
                    clamped.wait(pe, c, back=2)
                    for j in range(2):
                        for k in range(K):
                            last = t.transpose(ps_x[:, u, j, k * P:(k + 1) * P], rows[:, u, j, k], I[:])
                    last.then_inc(turned.sem, 1)
                for u in range(2):
                    c = 2 * i + u
                    moved.wait(pe, c)
                    moved_v.wait(pe, c)
                    biased.wait(pe, c, back=2)
                    t.matmul(ps_h[:, u, 0], W[:], xt[:, u, 0], start=True, stop=True)
                    t.matmul(ps_h[:, u, 1], W[:], xt[:, u, 1], start=True, stop=True).then_inc(made.sem, 1)
                for u in range(2):
                    c = 2 * i + u
                    squared.wait(pe, c)
                    t.matmul(ps_x[:, u, 0], BO[:], sq[:, u, 0], start=True, stop=True)
                    t.matmul(ps_x[:, u, 1], BO[:], sq[:, u, 1], start=True, stop=True).then_inc(summed.sem, 1)
    ph.close()


def route(nc, primer, n, idx, masks, bo32, av32, ident, small, zt, ct, x1d, x2):
    first, last = n == 0, n == ROUTINGS
    d = n % 2
    at = (lambda c: c) if d == 0 else (lambda c: c * -1 + (NCH - 1))
    way = slice(None) if d == 0 else slice(None, None, -1)
    end = slice(CH - 1, CH) if d == 0 else slice(0, 1)
    ph = Phase(nc, f"rt{n}", primer)
    BO = ph.sb("bo", [P, P]); AV = ph.sb("av", [P, P]); I = ph.sb("i", [P, P]); sm = ph.sb("sm", [P, 4])
    z = ph.sb("z", [P, 2, CH]); cin = ph.sb("cin", [P, 2, CH]); mk = ph.sb("mk", [P, 2, 2, CH], BF16)
    t1 = ph.sb("t1", [P, 2, CH]); whole = ph.sb("whole", [P, 2, CH]); sq = ph.sb("sq", [P, 2, CH])
    n2 = ph.sb("n2", [P, 2, CH]); rn = ph.sb("rn", [P, 2, CH]); cn = ph.sb("cn", [P, 2, CH])
    pr = ph.sb("pr", [P, 2, CH]); ex = ph.sb("ex", [P, 2, CH]); ld = ph.sb("ld", [P, 2, CH]); pm = ph.sb("pm", [P, 2, CH])
    ws = ph.sb("ws", [P, 2, CH]); t2 = ph.sb("t2", [P, 2, CH]); cout = ph.sb("cout", [P, 2, CH])
    xd = ph.sb("xd", [P, 2, K, D]); y = ph.sb("y", [P, 2, K, D]); x2r = ph.sb("x2r", [P, 2, K, D])
    st = ph.sb("st", [P, 2, K, 6]); mv = ph.sb("mv", [P, 2, K, 2]); lnv = ph.sb("lnv", [P, 2, K]); rstd = ph.sb("rstd", [P, 2, K])
    ps_n = ph.ps("n", [P, 2, CH]); ps_p = ph.ps("p", [P, 2, CH]); ps_d = ph.ps("d", [P, 2, CH])
    consts, vinit, vchain, achain, passed, pchain = (ph.sem(s) for s in ("consts", "vinit", "vchain", "achain", "passed", "pchain"))
    loaded = ph.dma("loaded", each=3)
    stored = ph.dma("stored", primed_by="sp")
    started, spread_, squared, summed, clamped, inverted, centred, multiplied, scored, exped, totalled, logged, shifted, \
        weighted, added, scanned = (ph.step(s) for s in (
            "started", "spread", "squared", "summed", "clamped", "inverted", "centred", "multiplied", "scored", "exped",
            "totalled", "logged", "shifted", "weighted", "added", "scanned"))
    if last:
        rr = Rows(ph, nc, idx, "rows", 1)
        scattered = ph.dma("scattered", each=K, primed_by="pool")
        turned, meaned, scaled, x2_made = (ph.step(s) for s in ("turned", "meaned", "scaled", "x2_made"))
    cs = cin if first else cn
    with nc.Block() as block:
        @block.sync
        def _(sp):
            ph.prime(sp, "sp")
            for a, b in ((BO[:], bo32), (AV[:], av32), (I[:], ident), (sm[:], small)):
                sp.dma_start(a, b).then_inc(consts, 16)

            def load(c, i, u):
                if last:
                    meaned.wait(sp, c, back=2)
                    sp.dma_start(xd[:, u], x1d[at(c)]).then_inc(loaded.sems[u], 16)
                else:
                    added.wait(sp, c, back=2)
                    scanned.wait(sp, c, back=2)
                    sp.dma_start(z[:, u], zt[at(c)]).then_inc(loaded.sems[u], 16)
                sp.dma_start(cin[:, u], ct[at(c)]).then_inc(loaded.sems[u], 16)
                sp.dma_start(mk[:, u], mask_rows(masks, d, 0, 2, at(c))).then_inc(loaded.sems[u], 16)

            def store(c, i, u):
                if last:
                    x2_made.wait(sp, c)
                    sp.dma_start(x1d[at(c)], x2r[:, u]).then_inc(stored.sems[u], 16)
                else:
                    scanned.wait(sp, c)
                    sp.dma_start(ct[at(c)], cout[:, u]).then_inc(stored.sems[u], 16)
            stream(sp, NCH, load, store)
            stored.wait_all(sp, NCH // 2)

        @block.gpsimd
        def _(pool):
            g = nc.gpsimd
            ph.prime(pool, "pool")
            ch = Chain(pool, pchain, 4)
            for i in pairs(pool, NCH):
                ch.start(i)
                for u in range(2):
                    if first:
                        continue
                    c = 2 * i + u
                    loaded.wait(pool, i, u)
                    spread_.wait(pool, c, back=2)
                    g.tensor_tensor(t1[:, u], mk[:, u, 1], cin[:, u], ALU.mult).then_inc(started.sem, 1)
                if last:
                    for u in range(2):
                        c = 2 * i + u
                        scattered.wait_before(pool, i, u)
                        x2_made.wait(pool, c)
                        rr.stage(pool, c, c, u, (FIRST,))
                        rr.scatter(u, 0, x2r[:, u], x2, scattered.sems[u])
                    continue
                for u in range(2):
                    c = 2 * i + u
                    loaded.wait(pool, i, u)
                    if not first:
                        centred.wait(pool, c)
                    scored.wait(pool, c, back=2)
                    g.tensor_tensor(pr[:, u], z[:, u], cs[:, u], ALU.mult).then_inc(multiplied.sem, 1)
                for u in range(2):
                    c = 2 * i + u
                    ch.did(g.tensor_tensor(t2[:, u], mk[:, u, 1], cs[:, u], ALU.mult))
                for u in range(2):
                    c = 2 * i + u
                    weighted.wait(pool, c)
                    scanned.wait(pool, c, back=2)
                    ch.did(g.tensor_tensor(ws[:, u], z[:, u], pm[:, u], ALU.mult))
                    ch.sync()
                    g.tensor_tensor(ws[:, u], ws[:, u], t2[:, u], ALU.add).then_inc(added.sem, 1)
                ch.end()
            if last:
                scattered.wait_all(pool, NCH // 2)

        @block.vector
        def _(dve):
            v = nc.vector
            v.memset(whole[:, 1, end], 0.0).then_inc(vinit, 1)
            v.memset(cout[:, 1, end], 0.0).then_inc(vinit, 1)
            dve.wait_ge(vinit, 2)
            ch = Chain(dve, vchain, (0 if first else 2) + (2 * K + 2 if last else 2))
            for i in pairs(dve, NCH):
                ch.start(i)
                for u in range(2):
                    if first:
                        continue
                    c = 2 * i + u
                    started.wait(dve, c)
                    centred.wait(dve, c, back=2)
                    squared.wait(dve, c, back=2)
                    ch.did(v.tensor_tensor_scan(out=whole[:, u, way], data0=mk[:, u, 0, way], data1=t1[:, u, way],
                                                initial=whole[:, 1 - u, end], op0=ALU.mult, op1=ALU.add))
                    ch.sync()
                    dve.sem_inc(spread_.sem, 1)
                for u in range(2):
                    if first:
                        continue
                    c = 2 * i + u
                    summed.wait(dve, c)
                    inverted.wait(dve, c, back=2)
                    v.tensor_scalar(n2[:, u], ps_n[:, u], 1e-24, None, ALU.max).then_inc(clamped.sem, 1)
                for u in range(2):
                    if first:
                        continue
                    c = 2 * i + u
                    inverted.wait(dve, c)
                    if last:
                        turned.wait(dve, c, back=2)
                    else:
                        added.wait(dve, c, back=2)
                    v.tensor_tensor(cn[:, u], whole[:, u], rn[:, u], ALU.mult).then_inc(centred.sem, 1)
                if last:
                    for u in range(2):
                        c = 2 * i + u
                        turned.wait(dve, c)
                        ch.did(v.tensor_tensor(y[:, u].rearrange("p k d -> p (k d)"), ps_p[:, u],
                                               xd[:, u].rearrange("p k d -> p (k d)"), ALU.add))
                        ch.sync()
                        row_norm(nc, ch, passed, y[:, u], st[:, u], mv[:, u]).then_inc(meaned.sem, 1)
                    for u in range(2):
                        c = 2 * i + u
                        scaled.wait(dve, c)
                        scattered.wait_before(dve, i, u)
                        stored.wait_before(dve, i, u)
                        row_scale(nc, x2r[:, u], y[:, u], mv[:, u], rstd[:, u]).then_inc(x2_made.sem, 1)
                    ch.end()
                    continue
                for u in range(2):
                    c = 2 * i + u
                    logged.wait(dve, c)
                    weighted.wait(dve, c, back=2)
                    v.tensor_tensor(ld[:, u], ps_p[:, u], ld[:, u], ALU.subtract).then_inc(shifted.sem, 1)
                for u in range(2):
                    c = 2 * i + u
                    added.wait(dve, c)
                    stored.wait_before(dve, i, u)
                    ch.did(v.tensor_tensor_scan(out=cout[:, u, way], data0=mk[:, u, 0, way], data1=ws[:, u, way],
                                                initial=cout[:, 1 - u, end], op0=ALU.mult, op1=ALU.add))
                    ch.sync()
                    dve.sem_inc(scanned.sem, 1)
                ch.end()

        @block.scalar
        def _(act):
            a = nc.scalar
            a.preload_act_table_set("natural_log_exp_and_others")
            act.wait_ge(consts, 64)
            ch = Chain(act, achain, (0 if first else 2) + (2 if last else 0))
            for i in pairs(act, NCH):
                ch.start(i)
                for u in range(2):
                    if first:
                        continue
                    c = 2 * i + u
                    spread_.wait(act, c)
                    summed.wait(act, c, back=2)
                    a.activation(sq[:, u], whole[:, u], ACT.Square).then_inc(squared.sem, 1)
                for u in range(2):
                    if first:
                        continue
                    c = 2 * i + u
                    clamped.wait(act, c)
                    ch.did(a.activation(n2[:, u], n2[:, u], ACT.Ln, scale=2.0 ** 20))
                    ch.sync()
                    centred.wait(act, c, back=2)
                    a.activation(rn[:, u], n2[:, u], ACT.Exp, scale=-0.5, bias=sm[:, 1:2]).then_inc(inverted.sem, 1)
                if last:
                    for u in range(2):
                        c = 2 * i + u
                        meaned.wait(act, c)
                        ch.did(a.activation(lnv[:, u], mv[:, u, :, 1], ACT.Ln, bias=sm[:, 0:1]))
                        ch.sync()
                        x2_made.wait(act, c, back=2)
                        a.activation(rstd[:, u], lnv[:, u], ACT.Exp, scale=-0.5).then_inc(scaled.sem, 1)
                    ch.end()
                    continue
                for u in range(2):
                    c = 2 * i + u
                    scored.wait(act, c)
                    totalled.wait(act, c, back=2)
                    a.activation(ex[:, u], ps_p[:, u], ACT.Exp).then_inc(exped.sem, 1)
                for u in range(2):
                    c = 2 * i + u
                    totalled.wait(act, c)
                    weighted.wait(act, c, back=2)
                    a.activation(ld[:, u], ps_d[:, u], ACT.Ln).then_inc(logged.sem, 1)
                for u in range(2):
                    c = 2 * i + u
                    shifted.wait(act, c)
                    added.wait(act, c, back=2)
                    a.activation(pm[:, u], ld[:, u], ACT.Exp).then_inc(weighted.sem, 1)
                ch.end()

        @block.tensor
        def _(pe):
            t = nc.tensor
            pe.wait_ge(consts, 64)
            for i in pairs(pe, NCH):
                for u in range(2):
                    if first:
                        continue
                    c = 2 * i + u
                    squared.wait(pe, c)
                    clamped.wait(pe, c, back=2)
                    t.matmul(ps_n[:, u], BO[:], sq[:, u], start=True, stop=True).then_inc(summed.sem, 1)
                if last:
                    for u in range(2):
                        c = 2 * i + u
                        centred.wait(pe, c)
                        meaned.wait(pe, c, back=2)
                        for k in range(K):
                            done = t.transpose(ps_p[:, u, k * P:(k + 1) * P], cn[:, u, k * P:(k + 1) * P], I[:])
                        done.then_inc(turned.sem, 1)
                    continue
                for u in range(2):
                    c = 2 * i + u
                    multiplied.wait(pe, c)
                    shifted.wait(pe, c, back=2)
                    t.matmul(ps_p[:, u], BO[:], pr[:, u], start=True, stop=True).then_inc(scored.sem, 1)
                for u in range(2):
                    c = 2 * i + u
                    exped.wait(pe, c)
                    logged.wait(pe, c, back=2)
                    t.matmul(ps_d[:, u], AV[:], ex[:, u], start=True, stop=True).then_inc(totalled.sem, 1)
    ph.close()


def edge_means(nc, primer, x2, idx, src_col, masks, src_row, a, ident, x2d, ain, aout):
    ph = Phase(nc, "m", primer)
    WI = ph.sb("wi", [P, D]); WO = ph.sb("wo", [P, D]); I = ph.sb("i", [P, P]); bi = ph.sb("bi", [P, 1]); BOU = ph.sb("bou", [P, D])
    U = ph.sb("u", [P, P]); sm = ph.sb("sm", [P, 4]); one = ph.sb("one", [P, CH])
    rows = ph.sb("rows", [P, 2, K, D]); xd = ph.sb("xd", [P, 2, K, D]); mk = ph.sb("mk", [P, 2, 1, CH], BF16)
    srow = ph.sb("srow", [P, 2, K, P]); scol = ph.sb("scol", [P, 2, K])
    xt = ph.sb("xt", [P, 2, 2, CH]); fin = ph.sb("fin", [P, 2, CH]); run = ph.sb("run", [P, 2, 2, CH])
    rc = ph.sb("rc", [P, 2, K]); mean = ph.sb("mean", [P, 2, K, D]); fo = ph.sb("fo", [P, 2, K, AW])
    same = ph.sb("same", [P, 2, K, P]); later = ph.sb("later", [P, K, P]); nl = ph.sb("nl", [P, 2, K]); to = ph.sb("to", [P, 2, K], I32)
    tot = ph.sb("tot", [P, 2, K, AW])
    ps_x = ph.ps("x", [P, 2, CH]); ps_f = ph.ps("f", [P, CH]); ps_r = ph.ps("r", [P, CH]); ps_o = ph.ps("o", [P, K, D])
    ps_c = ph.ps("c", [P, K]); ps_t = ph.ps("t", [P, K, 256])
    rr = Rows(ph, nc, idx, "rows", 2)
    consts, vinit, vchain, passed, serial = (ph.sem(s) for s in ("consts", "vinit", "vchain", "passed", "serial"))
    gathered = ph.dma("gathered", each=K)
    loaded = ph.dma("loaded", each=3)
    scattered = ph.dma("scattered", each=K, primed_by="pool")
    turned, moved, moved_v, made, biased, fo_made, scanned, run_turned, mean_made, fo_biased, compared, listed, summed, \
        copied, accumulated, staged = (ph.step(s) for s in (
            "turned", "moved", "moved_v", "made", "biased", "fo_made", "scanned", "run_turned", "mean_made", "fo_biased",
            "compared", "listed", "summed", "copied", "accumulated", "staged"))
    with nc.Block() as block:
        @block.sync
        def _(sp):
            ph.prime(sp, "sp")
            for p, q in ((WI[:], a["w_in_t"]), (WO[:], a["w_out_t"]), (I[:], ident), (bi[:], a["b_in"][:, None]),
                         (BOU[:], spread(a["b_out"])), (U[:], a["tri"]), (sm[:], a["small"])):
                sp.dma_start(p, q).then_inc(consts, 16)
            for i in pairs(sp, NCH):
                for u in range(2):
                    c = 2 * i + u
                    turned.wait(sp, c, back=2)
                    scanned.wait(sp, c, back=2)
                    compared.wait(sp, c, back=2)
                    sp.dma_start(xd[:, u], x2d[c]).then_inc(loaded.sems[u], 16)
                    sp.dma_start(mk[:, u], mask_rows(masks, 0, 0, 1, c)).then_inc(loaded.sems[u], 16)
                    sp.dma_start(srow[:, u].rearrange("p k e -> p (k e)"), spread(src_row[bass.ds(c * CH, CH)])).then_inc(loaded.sems[u], 16)

        @block.gpsimd
        def _(pool):
            g = nc.gpsimd
            ph.prime(pool, "pool")
            for i in pairs(pool, NCH):
                for u in range(2):
                    c = 2 * i + u
                    turned.wait(pool, c, back=2)
                    compared.wait(pool, c, back=2)
                    scattered.wait_before(pool, i, u)
                    g.tensor_copy(scol[:, u], src_col[:, bass.ds(c * K, K)]).then_inc(staged.sem, 1)
                    rr.stage(pool, c, c, u, (SRC, LAST))
                    rr.gather(u, 0, rows[:, u], x2, gathered.sems[u])
                for u in range(2):
                    c = 2 * i + u
                    mean_made.wait(pool, c)
                    pool.sem_inc(passed, 1)
                    rr.scatter(u, 1, mean[:, u], ain, scattered.sems[u])
                    copied.wait(pool, c)
                    listed.wait(pool, c)
                    pool.sem_inc(passed, 1)
                    for k in range(K):
                        g.indirect_dma_start(aout, bass.IndirectOffsetOnAxis(ap=to[:, u, k:k + 1], axis=0), tot[:, u, k], None,
                                             compute_op=ALU.add).then_inc(serial, 16)
                        pool.wait_ge(serial, c * (16 * K) + 16 * (k + 1))
                        pool.sem_inc(passed, 1)
                    pool.sem_inc(accumulated.sem, 1)
            scattered.wait_all(pool, NCH // 2)

        @block.vector
        def _(dve):
            v = nc.vector
            v.memset(one[:], 1.0).then_inc(vinit, 1)
            v.memset(run[:, 1, :, CH - 1:CH], 0.0).then_inc(vinit, 1)
            v.memset(fo[:, :, :, D:AW], 1.0).then_inc(vinit, 1)
            dve.wait_ge(vinit, 3)
            dve.wait_ge(consts, 16 * 7)
            ch = Chain(dve, vchain, 14)
            for i in pairs(dve, NCH):
                ch.start(i)
                for u in range(2):
                    c = 2 * i + u
                    turned.wait(dve, c)
                    fo_made.wait(dve, c, back=2)
                    v.tensor_copy(xt[:, u, 1], ps_x[:, 1]).then_inc(moved_v.sem, 1)
                for u in range(2):
                    c = 2 * i + u
                    loaded.wait(dve, i, u)
                    staged.wait(dve, c)
                    summed.wait(dve, c, back=2)
                    listed.wait(dve, c, back=1)
                    for k in range(K):
                        last_ = v.tensor_scalar(same[:, u, k], srow[:, u, k], scol[:, u, k:k + 1], None, ALU.is_equal)
                    last_.then_inc(compared.sem, 1)
                    compared.wait(dve, c)
                    ch.did(v.tensor_tensor(later[:], same[:, u], U[:, None, :].to_broadcast([P, K, P]), ALU.mult))
                    ch.sync()
                    ch.did(v.tensor_reduce(nl[:, u], later[:], AX, ALU.max))
                    ch.sync()
                    ch.did(v.scalar_tensor_tensor(nl[:, u], nl[:, u], sm[:, 3:4], scol[:, u], ALU.mult, ALU.max))
                    ch.sync()
                    accumulated.wait(dve, c, back=2)
                    v.tensor_scalar(to[:, u], nl[:, u], sm[:, 3:4], None, ALU.min).then_inc(listed.sem, 1)
                for u in range(2):
                    c = 2 * i + u
                    biased.wait(dve, c)
                    run_turned.wait(dve, c, back=2)
                    ch.did(v.tensor_tensor_scan(out=run[:, u, 0], data0=mk[:, u, 0], data1=fin[:, u],
                                                initial=run[:, 1 - u, 0, CH - 1:CH], op0=ALU.mult, op1=ALU.add))
                    ch.did(v.tensor_tensor_scan(out=run[:, u, 1], data0=mk[:, u, 0], data1=one[:],
                                                initial=run[:, 1 - u, 1, CH - 1:CH], op0=ALU.mult, op1=ALU.add))
                    ch.sync()
                    dve.sem_inc(scanned.sem, 1)
                    fo_made.wait(dve, c)
                    v.tensor_tensor(fo[:, u, :, 0:D], ps_o[:], BOU[:, None, :].to_broadcast([P, K, D]), ALU.add).then_inc(fo_biased.sem, 1)
                for u in range(2):
                    c = 2 * i + u
                    run_turned.wait(dve, c)
                    ch.did(v.tensor_copy(rc[:, u], ps_c[:]))
                    ch.sync()
                    ch.did(v.reciprocal(rc[:, u], rc[:, u]))
                    ch.sync()
                    scattered.wait_before(dve, i, u)
                    v.tensor_tensor(mean[:, u], ps_r[:].rearrange("p (k d) -> p k d", k=K),
                                    rc[:, u][:, :, None].to_broadcast([P, K, D]), ALU.mult).then_inc(mean_made.sem, 1)
                ch.end()

        @block.scalar
        def _(act):
            s = nc.scalar
            act.wait_ge(consts, 16 * 7)
            for i in pairs(act, NCH):
                for u in range(2):
                    c = 2 * i + u
                    turned.wait(act, c)
                    made.wait(act, c, back=2)
                    s.copy(xt[:, u, 0], ps_x[:, 0]).then_inc(moved.sem, 1)
                for u in range(2):
                    c = 2 * i + u
                    made.wait(act, c)
                    scanned.wait(act, c, back=2)
                    s.activation(fin[:, u], ps_f[:], ACT.Identity, bias=bi[:]).then_inc(biased.sem, 1)
                for u in range(2):
                    c = 2 * i + u
                    summed.wait(act, c)
                    accumulated.wait(act, c, back=2)
                    s.copy(tot[:, u], ps_t[:, :, 0:AW]).then_inc(copied.sem, 1)

        @block.tensor
        def _(pe):
            t = nc.tensor
            pe.wait_ge(consts, 16 * 7)
            for i in pairs(pe, NCH):
                for u in range(2):
                    c = 2 * i + u
                    gathered.wait(pe, i, u)
                    loaded.wait(pe, i, u)
                    moved.wait(pe, c, back=1)
                    moved_v.wait(pe, c, back=1)
                    for j, src in enumerate((rows, xd)):
                        for k in range(K):
                            done = t.transpose(ps_x[:, j, k * P:(k + 1) * P], src[:, u, k], I[:])
                    done.then_inc(turned.sem, 1)
                for u in range(2):
                    c = 2 * i + u
                    moved.wait(pe, c)
                    biased.wait(pe, c, back=1)
                    t.matmul(ps_f[:], WI[:], xt[:, u, 0], start=True, stop=True).then_inc(made.sem, 1)
                    moved_v.wait(pe, c)
                    fo_biased.wait(pe, c, back=1)
                    for k in range(K):
                        done = t.matmul(ps_o[:, k], xt[:, u, 1, k * P:(k + 1) * P], WO[:], start=True, stop=True)
                    done.then_inc(fo_made.sem, 1)
                for u in range(2):
                    c = 2 * i + u
                    scanned.wait(pe, c)
                    mean_made.wait(pe, c, back=1)
                    for k in range(K):
                        t.transpose(ps_r[:, k * P:(k + 1) * P], run[:, u, 0, k * P:(k + 1) * P], I[:])
                    for k in range(K):
                        done = t.matmul(ps_c[:, k:k + 1], run[:, u, 1, k * P:(k + 1) * P], sm[:, 2:3], start=True, stop=True)
                    done.then_inc(run_turned.sem, 1)
                    fo_biased.wait(pe, c)
                    compared.wait(pe, c)
                    copied.wait(pe, c, back=1)
                    for k in range(K):
                        done = t.matmul(ps_t[:, k, 0:AW], same[:, u, k], fo[:, u, k], start=True, stop=True)
                    done.then_inc(summed.sem, 1)
    ph.close()


def dense_second(nc, primer, x2, ain, aout, x3, out, a, ident, small):
    ph = Phase(nc, "d2", primer)
    WIH = ph.sb("wih", [P, 2, 3 * D]); WHH = ph.sb("whh", [P, 3 * D]); W3 = ph.sb("w3", [P, D]); I = ph.sb("i", [P, P])
    bih = ph.sb("bih", [P, 3]); bhh = ph.sb("bhh", [P, 3]); brz = ph.sb("brz", [P, 2])
    B3 = ph.sb("b3", [P, D]); GA = ph.sb("ga", [P, D]); BE = ph.sb("be", [P, D]); half = ph.sb("half", [P, K])
    xin = ph.sb("xin", [P, 2, K, D]); ai = ph.sb("ai", [P, 2, K, D]); ao = ph.sb("ao", [P, 2, K, AW])
    rc = ph.sb("rc", [P, 2, K]); aon = ph.sb("aon", [P, 2, K, D])
    xt = ph.sb("xt", [P, 2, 3, CH])
    rz = ph.sb("rz", [P, 2, 2, CH]); t_ = ph.sb("t", [P, 2, CH]); n_ = ph.sb("n", [P, 2, CH])
    df = ph.sb("df", [P, 2, CH]); y = ph.sb("y", [P, 2, CH])
    st = ph.sb("st", [P, 2, 3, K, 6]); mv = ph.sb("mv", [P, 2, 3, K, 2]); ve = ph.sb("ve", [P, 2, 3, K]); rstd = ph.sb("rstd", [P, 2, 3, K])
    x3r = ph.sb("x3r", [P, 2, K, D]); x3t = ph.sb("x3t", [P, 2, CH]); h = ph.sb("h", [P, 2, K, D]); hn = ph.sb("hn", [P, 2, K, D])
    w_ = ph.sb("w", [P, 2, K, D]); o = ph.sb("o", [P, 2, K, D])
    ps_x = ph.ps("x", [P, 3, CH]); ps_g = ph.ps("g", [P, 4, CH]); ps_h = ph.ps("h", [P, K, D])
    consts, vinit, biases, vchain, passed, pchain = (ph.sem(s) for s in ("consts", "vinit", "biases", "vchain", "passed", "pchain"))
    loaded = ph.dma("loaded", each=3)
    stored = ph.dma("stored", each=2, primed_by="sp")
    names = ("counted averaged turned moved gated rz_made gate_n tanhed mixed y_turned moved0 scaled0 x3_made x3_turned "
             "x3t_made h_made h_biased moved1 scaled1 h_normed affine activated moved2 scaled2 out_made").split()
    s = {n: ph.step(n) for n in names}
    with nc.Block() as block:
        @block.sync
        def _(sp):
            ph.prime(sp, "sp")
            for p, q in ((WIH[:], a["w_ih_t"].rearrange("j d g -> d j g")), (WHH[:], a["w_hh_t"]), (W3[:], a["w3"][0]), (I[:], ident),
                         (B3[:], spread(a["b3"])), (GA[:], spread(a["gamma"])), (BE[:], spread(a["beta"]))):
                sp.dma_start(p, q).then_inc(consts, 16)
            with nc.allow_non_contiguous_dma(reason="biases to columns, once"):
                sp.dma_start(bih[:], a["b_ih"].rearrange("(g d) -> d g", g=3)).then_inc(consts, 16)
                sp.dma_start(bhh[:], a["b_hh"].rearrange("(g d) -> d g", g=3)).then_inc(consts, 16)

            def load(c, i, u):
                s["turned"].wait(sp, c, back=2)
                s["averaged"].wait(sp, c, back=2)
                sp.dma_start(xin[:, u], group_rows(x2, c)).then_inc(loaded.sems[u], 16)
                sp.dma_start(ai[:, u], group_rows(ain, c)).then_inc(loaded.sems[u], 16)
                sp.dma_start(ao[:, u], group_rows(aout, c)).then_inc(loaded.sems[u], 16)

            def store(c, i, u):
                if isinstance(c, int) and c == NG - 1:
                    stored.wait(sp, i, 0)
                s["x3_made"].wait(sp, c)
                sp.dma_start(group_rows(x3, c), x3r[:, u]).then_inc(stored.sems[u], 16)
                s["out_made"].wait(sp, c)
                sp.dma_start(group_rows(out, c), o[:, u]).then_inc(stored.sems[u], 16)
            stream(sp, NG, load, store, peeled=1)
            stored.wait_all(sp, NG // 2)

        @block.gpsimd
        def _(pool):
            g = nc.gpsimd
            ph.prime(pool, "pool")
            pool.wait_ge(consts, 16 * 9)
            g.memset(half[:], -0.5).then_inc(vinit, 1)
            pool.wait_ge(vinit, 1)
            ch = Chain(pool, pchain, 6)
            for i in pairs(pool, NG):
                ch.start(i)

                def invert(c, u, j):
                    s[f"moved{j}"].wait(pool, c)
                    g.tensor_tensor(rstd[:, u, j], ve[:, u, j], half[:], ALU.pow).then_inc(s[f"scaled{j}"].sem, 1)
                for u in range(2):
                    c = 2 * i + u
                    s["counted"].wait(pool, c)
                    s["turned"].wait(pool, c, back=2)
                    g.tensor_tensor(aon[:, u], ao[:, u, :, 0:D], rc[:, u][:, :, None].to_broadcast([P, K, D]), ALU.mult).then_inc(s["averaged"].sem, 1)
                for u in range(2):
                    c = 2 * i + u
                    s["tanhed"].wait(pool, c)
                    s["y_turned"].wait(pool, c, back=2)
                    ch.did(g.tensor_tensor(df[:, u], xt[:, u, 0], n_[:, u], ALU.subtract))
                    ch.sync()
                    ch.did(g.tensor_tensor(df[:, u], df[:, u], rz[:, u, 1], ALU.mult))
                    ch.did(g.tensor_tensor(y[:, u], xt[:, u, 0], n_[:, u], ALU.add))
                    ch.sync()
                    g.tensor_tensor(y[:, u], y[:, u], df[:, u], ALU.add).then_inc(s["mixed"].sem, 1)
                for u in range(2):
                    invert(2 * i + u, u, 0)
                for u in range(2):
                    invert(2 * i + u, u, 1)
                for u in range(2):
                    c = 2 * i + u
                    s["h_normed"].wait(pool, c)
                    g.tensor_tensor(w_[:, u], hn[:, u], GA[:, None, :].to_broadcast([P, K, D]), ALU.mult).then_inc(s["affine"].sem, 1)
                    s["affine"].wait(pool, c)
                    g.tensor_tensor(w_[:, u], w_[:, u], BE[:, None, :].to_broadcast([P, K, D]), ALU.add).then_inc(s["activated"].sem, 1)
                for u in range(2):
                    invert(2 * i + u, u, 2)
                ch.end()

        @block.vector
        def _(dve):
            v = nc.vector
            dve.wait_ge(consts, 16 * 9)
            v.tensor_tensor(brz[:], bih[:, 0:2], bhh[:, 0:2], ALU.add).then_inc(biases, 1)
            ch = Chain(dve, vchain, 2 + 2 + 6 * K + 6 + 2)
            for i in pairs(dve, NG):
                ch.start(i)

                def moments(c, u, j, src):
                    ch.did(row_norm(nc, ch, passed, src, st[:, u, j], mv[:, u, j]))
                    ch.sync()
                    return v.tensor_scalar(ve[:, u, j], mv[:, u, j, :, 1], LN_EPS, None, ALU.add)
                for u in range(2):
                    c = 2 * i + u
                    loaded.wait(dve, i, u)
                    ch.did(v.tensor_scalar(rc[:, u], ao[:, u, :, D], 1.0, None, ALU.max))
                    ch.sync()
                    v.reciprocal(rc[:, u], rc[:, u]).then_inc(s["counted"].sem, 1)
                for u in range(2):
                    c = 2 * i + u
                    s["rz_made"].wait(dve, c)
                    s["tanhed"].wait(dve, c, back=2)
                    ch.did(v.scalar_tensor_tensor(t_[:, u], ps_g[:, 3], bhh[:, 2:3], rz[:, u, 0], ALU.add, ALU.mult))
                    ch.sync()
                    v.tensor_tensor(t_[:, u], t_[:, u], ps_g[:, 2], ALU.add).then_inc(s["gate_n"].sem, 1)
                for u in range(2):
                    c = 2 * i + u
                    s["y_turned"].wait(dve, c)
                    yr = ps_x[:, 0].rearrange("p (k d) -> p k d", k=K)
                    moments(c, u, 0, yr).then_inc(s["moved0"].sem, 1)
                    s["scaled0"].wait(dve, c)
                    stored.wait_before(dve, i, u)
                    s["x3_turned"].wait(dve, c, back=2)
                    s["moved2"].wait(dve, c, back=2)
                    row_scale(nc, x3r[:, u], yr, mv[:, u, 0], rstd[:, u, 0]).then_inc(s["x3_made"].sem, 1)
                for u in range(2):
                    c = 2 * i + u
                    s["h_made"].wait(dve, c)
                    v.tensor_tensor(h[:, u], ps_h[:], B3[:, None, :].to_broadcast([P, K, D]), ALU.add).then_inc(s["h_biased"].sem, 1)
                    s["h_biased"].wait(dve, c)
                    moments(c, u, 1, h[:, u]).then_inc(s["moved1"].sem, 1)
                for u in range(2):
                    c = 2 * i + u
                    s["scaled1"].wait(dve, c)
                    s["affine"].wait(dve, c, back=2)
                    row_scale(nc, hn[:, u], h[:, u], mv[:, u, 1], rstd[:, u, 1]).then_inc(s["h_normed"].sem, 1)
                for u in range(2):
                    c = 2 * i + u
                    s["activated"].wait(dve, c)
                    ch.did(v.scalar_tensor_tensor(w_[:, u], w_[:, u], 0.0, x3r[:, u], ALU.max, ALU.add))
                    ch.sync()
                    moments(c, u, 2, w_[:, u]).then_inc(s["moved2"].sem, 1)
                for u in range(2):
                    c = 2 * i + u
                    s["scaled2"].wait(dve, c)
                    stored.wait_before(dve, i, u)
                    row_scale(nc, o[:, u], w_[:, u], mv[:, u, 2], rstd[:, u, 2]).then_inc(s["out_made"].sem, 1)
                ch.end()

        @block.scalar
        def _(act):
            f = nc.scalar
            f.preload_act_table_set("sigmoid_and_others")
            act.wait_ge(consts, 16 * 9)
            act.wait_ge(biases, 1)
            for i in pairs(act, NG):
                for u in range(2):
                    c = 2 * i + u
                    s["turned"].wait(act, c)
                    s["gated"].wait(act, c, back=2)
                    s["mixed"].wait(act, c, back=2)
                    f.copy(xt[:, u], ps_x[:]).then_inc(s["moved"].sem, 1)
                for u in range(2):
                    c = 2 * i + u
                    s["gated"].wait(act, c)
                    s["mixed"].wait(act, c, back=2)
                    f.activation(rz[:, u, 0], ps_g[:, 0], ACT.Sigmoid, bias=brz[:, 0:1])
                    f.activation(rz[:, u, 1], ps_g[:, 1], ACT.Sigmoid, bias=brz[:, 1:2]).then_inc(s["rz_made"].sem, 1)
                    s["gate_n"].wait(act, c)
                    f.activation(n_[:, u], t_[:, u], ACT.Tanh, bias=bih[:, 2:3]).then_inc(s["tanhed"].sem, 1)
                for u in range(2):
                    c = 2 * i + u
                    s["x3_turned"].wait(act, c)
                    s["h_made"].wait(act, c, back=2)
                    f.copy(x3t[:, u], ps_x[:, 0]).then_inc(s["x3t_made"].sem, 1)

        @block.tensor
        def _(pe):
            t = nc.tensor
            pe.wait_ge(consts, 16 * 9)
            for i in pairs(pe, NG):
                for u in range(2):
                    c = 2 * i + u
                    loaded.wait(pe, i, u)
                    s["averaged"].wait(pe, c)
                    if u == 0:
                        s["x3t_made"].wait(pe, c, back=1)
                    else:
                        s["moved"].wait(pe, c, back=1)
                    for j, src in enumerate((xin, ai, aon)):
                        for k in range(K):
                            done = t.transpose(ps_x[:, j, k * P:(k + 1) * P], src[:, u, k], I[:])
                    done.then_inc(s["turned"].sem, 1)
                for u in range(2):
                    c = 2 * i + u
                    s["moved"].wait(pe, c)
                    s["rz_made"].wait(pe, c, back=1)
                    s["gate_n"].wait(pe, c, back=1)
                    for gate in range(2):
                        cols = slice(gate * D, (gate + 1) * D)
                        t.matmul(ps_g[:, gate], WHH[:, cols], xt[:, u, 0], start=True, stop=False)
                        t.matmul(ps_g[:, gate], WIH[:, 0, cols], xt[:, u, 1], start=False, stop=False)
                        t.matmul(ps_g[:, gate], WIH[:, 1, cols], xt[:, u, 2], start=False, stop=True)
                    t.matmul(ps_g[:, 2], WIH[:, 0, 2 * D:], xt[:, u, 1], start=True, stop=False)
                    t.matmul(ps_g[:, 2], WIH[:, 1, 2 * D:], xt[:, u, 2], start=False, stop=True)
                    t.matmul(ps_g[:, 3], WHH[:, 2 * D:], xt[:, u, 0], start=True, stop=True).then_inc(s["gated"].sem, 1)
                for u in range(2):
                    c = 2 * i + u
                    s["mixed"].wait(pe, c)
                    if u == 0:
                        s["moved"].wait(pe, c, back=-1)
                    else:
                        s["x3_made"].wait(pe, c, back=1)
                    for k in range(K):
                        done = t.transpose(ps_x[:, 0, k * P:(k + 1) * P], y[:, u, k * P:(k + 1) * P], I[:])
                    done.then_inc(s["y_turned"].sem, 1)
                for u in range(2):
                    c = 2 * i + u
                    if u == 0:
                        s["x3_made"].wait(pe, c, back=-1)
                    else:
                        s["x3t_made"].wait(pe, c, back=1)
                    for k in range(K):
                        done = t.transpose(ps_x[:, 0, k * P:(k + 1) * P], x3r[:, u, k], I[:])
                    done.then_inc(s["x3_turned"].sem, 1)
                    s["x3t_made"].wait(pe, c)
                    s["h_biased"].wait(pe, c, back=1)
                    for k in range(K):
                        done = t.matmul(ps_h[:, k], x3t[:, u, k * P:(k + 1) * P], W3[:], start=True, stop=True)
                    done.then_inc(s["h_made"].sem, 1)
    ph.close()


def lse_forward(nc, primer, x3, idx, masks, ident, xm):
    ph = Phase(nc, "l0", primer)
    I = ph.sb("i", [P, P]); rows = ph.sb("rows", [P, 2, K, D]); mk = ph.sb("mk", [P, 2, 1, CH], BF16); o = ph.sb("o", [P, 2, 2, CH])
    ps_x = ph.ps("x", [P, 2, CH])
    rr = Rows(ph, nc, idx, "rows", 1)
    consts, vinit, vchain = (ph.sem(s) for s in ("consts", "vinit", "vchain"))
    gathered = ph.dma("gathered", each=K)
    masked = ph.dma("masked")
    stored = ph.dma("stored", primed_by="sp")
    turned, moved, scanned = (ph.step(s) for s in ("turned", "moved", "scanned"))
    with nc.Block() as block:
        @block.sync
        def _(sp):
            ph.prime(sp, "sp")
            sp.dma_start(I[:], ident).then_inc(consts, 16)

            def load(c, i, u):
                scanned.wait(sp, c, back=2)
                sp.dma_start(mk[:, u], mask_rows(masks, 0, 2, 1, c)).then_inc(masked.sems[u], 16)

            def store(c, i, u):
                scanned.wait(sp, c)
                sp.dma_start(xm[c, :, 0:2], o[:, u]).then_inc(stored.sems[u], 16)
            stream(sp, NCH, load, store)
            stored.wait_all(sp, NCH // 2)

        @block.gpsimd
        def _(pool):
            for i in pairs(pool, NCH):
                for u in range(2):
                    c = 2 * i + u
                    turned.wait(pool, c, back=2)
                    rr.stage(pool, c, c, u, (SRC,))
                    rr.gather(u, 0, rows[:, u], x3, gathered.sems[u])

        @block.vector
        def _(dve):
            v = nc.vector
            v.memset(o[:, 1, 1, CH - 1:CH], 0.0).then_inc(vinit, 1)
            dve.wait_ge(vinit, 1)
            ch = Chain(dve, vchain, 2)
            for i in pairs(dve, NCH):
                ch.start(i)
                for u in range(2):
                    c = 2 * i + u
                    moved.wait(dve, c)
                    masked.wait(dve, i, u)
                    stored.wait_before(dve, i, u)
                    ch.did(v.tensor_tensor_scan(out=o[:, u, 1], data0=mk[:, u, 0], data1=o[:, u, 0],
                                                initial=o[:, 1 - u, 1, CH - 1:CH], op0=ALU.add, op1=ALU.max))
                    ch.sync()
                    dve.sem_inc(scanned.sem, 1)
                ch.end()

        @block.scalar
        def _(act):
            for i in pairs(act, NCH):
                for u in range(2):
                    c = 2 * i + u
                    turned.wait(act, c)
                    stored.wait_before(act, i, u)
                    nc.scalar.copy(o[:, u, 0], ps_x[:, u]).then_inc(moved.sem, 1)

        @block.tensor
        def _(pe):
            pe.wait_ge(consts, 16)
            for i in pairs(pe, NCH):
                for u in range(2):
                    c = 2 * i + u
                    gathered.wait(pe, i, u)
                    moved.wait(pe, c, back=2)
                    for k in range(K):
                        done = nc.tensor.transpose(ps_x[:, u, k * P:(k + 1) * P], rows[:, u, k], I[:])
                    done.then_inc(turned.sem, 1)
    ph.close()


def lse_backward(nc, primer, x3, idx, masks, a, ident, small, xm, out):
    ph = Phase(nc, "l1", primer)
    W3 = ph.sb("w3", [P, 2, D]); I = ph.sb("i", [P, P]); sm = ph.sb("sm", [P, 4])
    B3 = ph.sb("b3", [P, D]); GA = ph.sb("ga", [P, D]); BE = ph.sb("be", [P, D])
    xs = ph.sb("xs", [P, 2, 2, CH]); mk = ph.sb("mk", [P, 2, 2, CH], BF16); rows = ph.sb("rows", [P, 2, K, D])
    t1 = ph.sb("t1", [P, 2, CH]); mx = ph.sb("mx", [P, 2, CH]); ex = ph.sb("ex", [P, 2, CH]); sums = ph.sb("sums", [P, 2, CH])
    cl = ph.sb("cl", [P, 2, CH]); agg = ph.sb("agg", [P, 2, CH]); xt = ph.sb("xt", [P, 2, CH])
    h = ph.sb("h", [P, 2, K, D]); hn = ph.sb("hn", [P, 2, K, D]); w_ = ph.sb("w", [P, 2, K, D]); o = ph.sb("o", [P, 2, K, D])
    st = ph.sb("st", [P, 2, 2, K, 6]); mv = ph.sb("mv", [P, 2, 2, K, 2]); lnv = ph.sb("lnv", [P, 2, 2, K]); rstd = ph.sb("rstd", [P, 2, 2, K])
    ps_x = ph.ps("x", [P, 2, CH]); ps_h = ph.ps("h", [P, 2, K, D])
    rr = Rows(ph, nc, idx, "rows", 2)
    consts, vinit, vchain, achain, passed, pchain = (ph.sem(s) for s in ("consts", "vinit", "vchain", "achain", "passed", "pchain"))
    gathered = ph.dma("gathered", each=K)
    loaded = ph.dma("loaded", each=2)
    scattered = ph.dma("scattered", each=K, primed_by="pool")
    names = "started spread shifted exped scanned clamped logged agg_made turned moved h_made h_biased moved0 scaled0 h_normed affine activated moved1 scaled1 out_made".split()
    s = {n: ph.step(n) for n in names}
    back = lambda c: c * -1 + (NCH - 1)
    with nc.Block() as block:
        @block.sync
        def _(sp):
            ph.prime(sp, "sp")
            for p, q in ((W3[:], a["w3"].rearrange("j d e -> d j e")), (I[:], ident), (sm[:], small), (B3[:], spread(a["b3"])),
                         (GA[:], spread(a["gamma"])), (BE[:], spread(a["beta"]))):
                sp.dma_start(p, q).then_inc(consts, 16)
            for i in pairs(sp, NCH):
                for u in range(2):
                    c = 2 * i + u
                    s["shifted"].wait(sp, c, back=2)
                    s["scanned"].wait(sp, c, back=2)
                    sp.dma_start(xs[:, u], xm[back(c), :, 0:2]).then_inc(loaded.sems[u], 16)
                    sp.dma_start(mk[:, u], mask_rows(masks, 1, 0, 2, back(c))).then_inc(loaded.sems[u], 16)

        @block.gpsimd
        def _(pool):
            g = nc.gpsimd
            ph.prime(pool, "pool")
            pool.wait_ge(consts, 96)
            for i in pairs(pool, NCH):
                for u in range(2):
                    c = 2 * i + u
                    s["turned"].wait(pool, c, back=2)
                    s["moved1"].wait(pool, c, back=2)
                    scattered.wait_before(pool, i, u)
                    rr.stage(pool, back(c), c, u, (DST, FIRST))
                    rr.gather(u, 0, rows[:, u], x3, gathered.sems[u])
                for u in range(2):
                    c = 2 * i + u
                    loaded.wait(pool, i, u)
                    s["spread"].wait(pool, c, back=2)
                    g.tensor_tensor(t1[:, u], mk[:, u, 1], xs[:, u, 1], ALU.mult).then_inc(s["started"].sem, 1)
                for u in range(2):
                    c = 2 * i + u
                    s["logged"].wait(pool, c)
                    s["h_made"].wait(pool, c, back=2)
                    g.tensor_tensor(agg[:, u], cl[:, u], mx[:, u], ALU.add).then_inc(s["agg_made"].sem, 1)
                for u in range(2):
                    c = 2 * i + u
                    s["h_normed"].wait(pool, c)
                    g.tensor_tensor(w_[:, u], hn[:, u], GA[:, None, :].to_broadcast([P, K, D]), ALU.mult).then_inc(s["affine"].sem, 1)
                    s["affine"].wait(pool, c)
                    g.tensor_tensor(w_[:, u], w_[:, u], BE[:, None, :].to_broadcast([P, K, D]), ALU.add).then_inc(s["activated"].sem, 1)
                for u in range(2):
                    c = 2 * i + u
                    s["out_made"].wait(pool, c)
                    pool.sem_inc(passed, 1)
                    rr.scatter(u, 1, o[:, u], out, scattered.sems[u])
            scattered.wait_all(pool, NCH // 2)

        @block.vector
        def _(dve):
            v = nc.vector
            v.memset(mx[:, 1, 0:1], 0.0).then_inc(vinit, 1)
            v.memset(sums[:, 1, 0:1], 0.0).then_inc(vinit, 1)
            dve.wait_ge(vinit, 2)
            dve.wait_ge(consts, 96)
            ch = Chain(dve, vchain, 2 + 2 + 2 * K + 2 + 2 * K)
            for i in pairs(dve, NCH):
                ch.start(i)
                for u in range(2):
                    c = 2 * i + u
                    s["started"].wait(dve, c)
                    s["agg_made"].wait(dve, c, back=2)
                    ch.did(v.tensor_tensor_scan(out=mx[:, u, ::-1], data0=mk[:, u, 0, ::-1], data1=t1[:, u, ::-1],
                                                initial=mx[:, 1 - u, 0:1], op0=ALU.mult, op1=ALU.add))
                    ch.sync()
                    dve.sem_inc(s["spread"].sem, 1)
                    s["exped"].wait(dve, c, back=2)
                    v.tensor_tensor(xs[:, u, 0], xs[:, u, 0], mx[:, u], ALU.subtract).then_inc(s["shifted"].sem, 1)
                for u in range(2):
                    c = 2 * i + u
                    s["exped"].wait(dve, c)
                    s["clamped"].wait(dve, c, back=2)
                    ch.did(v.tensor_tensor_scan(out=sums[:, u, ::-1], data0=mk[:, u, 0, ::-1], data1=ex[:, u, ::-1],
                                                initial=sums[:, 1 - u, 0:1], op0=ALU.mult, op1=ALU.add))
                    ch.sync()
                    dve.sem_inc(s["scanned"].sem, 1)
                    s["agg_made"].wait(dve, c, back=2)
                    v.tensor_scalar(cl[:, u], sums[:, u], 1e-30, None, ALU.max).then_inc(s["clamped"].sem, 1)
                for u in range(2):
                    c = 2 * i + u
                    s["h_made"].wait(dve, c)
                    s["h_normed"].wait(dve, c, back=2)
                    v.tensor_tensor(h[:, u], ps_h[:, u], B3[:, None, :].to_broadcast([P, K, D]), ALU.add).then_inc(s["h_biased"].sem, 1)
                    s["h_biased"].wait(dve, c)
                    row_norm(nc, ch, passed, h[:, u], st[:, u, 0], mv[:, u, 0]).then_inc(s["moved0"].sem, 1)
                for u in range(2):
                    c = 2 * i + u
                    s["scaled0"].wait(dve, c)
                    s["affine"].wait(dve, c, back=2)
                    row_scale(nc, hn[:, u], h[:, u], mv[:, u, 0], rstd[:, u, 0]).then_inc(s["h_normed"].sem, 1)
                for u in range(2):
                    c = 2 * i + u
                    s["activated"].wait(dve, c)
                    ch.did(v.scalar_tensor_tensor(w_[:, u], w_[:, u], 0.0, rows[:, u], ALU.max, ALU.add))
                    ch.sync()
                    row_norm(nc, ch, passed, w_[:, u], st[:, u, 1], mv[:, u, 1]).then_inc(s["moved1"].sem, 1)
                for u in range(2):
                    c = 2 * i + u
                    s["scaled1"].wait(dve, c)
                    scattered.wait_before(dve, i, u)
                    row_scale(nc, o[:, u], w_[:, u], mv[:, u, 1], rstd[:, u, 1]).then_inc(s["out_made"].sem, 1)
                ch.end()

        @block.scalar
        def _(act):
            f = nc.scalar
            f.preload_act_table_set("natural_log_exp_and_others")
            act.wait_ge(consts, 96)
            ch = Chain(act, achain, 4)
            for i in pairs(act, NCH):
                ch.start(i)

                def invert(c, u, j):
                    s[f"moved{j}"].wait(act, c)
                    ch.did(f.activation(lnv[:, u, j], mv[:, u, j, :, 1], ACT.Ln, bias=sm[:, 0:1]))
                    ch.sync()
                    s[("h_normed", "out_made")[j]].wait(act, c, back=2)
                    f.activation(rstd[:, u, j], lnv[:, u, j], ACT.Exp, scale=-0.5).then_inc(s[f"scaled{j}"].sem, 1)
                for u in range(2):
                    c = 2 * i + u
                    s["turned"].wait(act, c)
                    s["h_made"].wait(act, c, back=2)
                    f.copy(xt[:, u], ps_x[:, u]).then_inc(s["moved"].sem, 1)
                for u in range(2):
                    c = 2 * i + u
                    s["shifted"].wait(act, c)
                    s["scanned"].wait(act, c, back=2)
                    f.activation(ex[:, u], xs[:, u, 0], ACT.Exp).then_inc(s["exped"].sem, 1)
                for u in range(2):
                    c = 2 * i + u
                    s["clamped"].wait(act, c)
                    f.activation(cl[:, u], cl[:, u], ACT.Ln).then_inc(s["logged"].sem, 1)
                for u in range(2):
                    invert(2 * i + u, u, 0)
                for u in range(2):
                    invert(2 * i + u, u, 1)
                ch.end()

        @block.tensor
        def _(pe):
            t = nc.tensor
            pe.wait_ge(consts, 96)
            for i in pairs(pe, NCH):
                for u in range(2):
                    c = 2 * i + u
                    gathered.wait(pe, i, u)
                    s["moved"].wait(pe, c, back=2)
                    for k in range(K):
                        done = t.transpose(ps_x[:, u, k * P:(k + 1) * P], rows[:, u, k], I[:])
                    done.then_inc(s["turned"].sem, 1)
                for u in range(2):
                    c = 2 * i + u
                    s["moved"].wait(pe, c)
                    s["agg_made"].wait(pe, c)
                    s["h_biased"].wait(pe, c, back=2)
                    for k in range(K):
                        t.matmul(ps_h[:, u, k], xt[:, u, k * P:(k + 1) * P], W3[:, 0], start=True, stop=False)
                        done = t.matmul(ps_h[:, u, k], agg[:, u, k * P:(k + 1) * P], W3[:, 1], start=False, stop=True)
                    done.then_inc(s["h_made"].sem, 1)
    ph.close()


def gnn(nc, a, out, keep="Internal", stop=99):
    def dram(name, shape, dt=F32, kind="Internal"):
        return nc.dram_tensor(name, shape, dt, kind=kind).ap()

    primer = (dram("primer_out", (32, 64)), a["primer"])
    sorted_edges = [dram("edges0", (SLOTS, 2), I32), dram("edges1", (SLOTS, 2), I32)]
    masks, lists, src_row = dram("masks", (2, 3, SLOTS), BF16), dram("lists", (5, SLOTS), I32), dram("src_row", (SLOTS,))
    x1, x2, x3 = (dram(n, (N, D), F32, keep) for n in ("x1", "x2", "x3"))
    ain, aout = dram("ain", (N, D), F32, keep), dram("aout", (N + P, AW), F32, keep)
    l0t, rows0 = dram("l0t", (NCH, P, 3, CH)), dram("rows0", (NCH, P, K, D))
    zt, ct = dram("zt", (NCH, P, CH)), dram("ct", (NCH, P, CH))
    ident, small = a["ident"], a["small"]
    with nc.sbuf_tensor("idx", [P, 5, T], I32) as idx, nc.sbuf_tensor("src_col", [P, T], F32) as src_col:
        sort_edges(nc, primer, a["src"], a["dst"], sorted_edges, a)
        slot_tables(nc, primer, sorted_edges[0], masks, lists, src_row, idx, src_col)
        dense_first(nc, primer, a["x"], x1, x2, a["w1t"], a["bias0"], a["b1"], ident, small, [ain, aout])
        if stop < 1: return
        gat_forward(nc, primer, a["x"], idx, masks, a["w0"], a["w0t"], a["al"], a["ar"], a["bo16"], ident, l0t, rows0)
        gat_backward(nc, primer, idx, masks, a["bias0"], a["sel8"], ident, small, l0t, rows0, x1)
        if stop < 2: return
        route_start(nc, primer, x1, idx, a["w1t"], a["b1"], a["bo32"], ident, small, zt, ct, rows0)
        for n in range(ROUTINGS + 1):
            route(nc, primer, n, idx, masks, a["bo32"], a["av32"], ident, small, zt, ct, rows0, x2)
        if stop < 3: return
        edge_means(nc, primer, x2, idx, src_col, masks, src_row, a, ident, rows0, ain, aout)
        if stop < 4: return
        dense_second(nc, primer, x2, ain, aout, x3, out, a, ident, small)
        if stop < 5: return
        lse_forward(nc, primer, x3, idx, masks, ident, l0t)
        lse_backward(nc, primer, x3, idx, masks, a, ident, small, l0t, out)


def constants():
    f = np.float32
    small = np.zeros((P, 4), f)
    small[:, 0] = LN_EPS
    small[:, 1] = 10 * np.log(2.0)
    small[:, 2] = 1.0 / P
    small[:, 3] = N + np.arange(P)
    i = np.arange(P)
    same32 = (i[:, None] // PER_GROUP == i[None] // PER_GROUP).astype(f)
    return {
        "primer": np.zeros((32, 64), f),
        "iota": np.tile(np.arange(64, dtype=f), (P, 1)),
        "tri": np.triu(np.ones((P, P), f), 1),
        "ones": np.ones((P, P), f),
        "padding": np.tile(np.array([N, 0], np.int32), (P, T, 1)),
        "ident": np.eye(P, dtype=f),
        "small": small,
        "bo16": (i[:, None] // PER_HEAD == i[None] // PER_HEAD).astype(f),
        "sel8": (i[:, None] == PER_HEAD * np.arange(HEADS)[None]).astype(f),
        "bo32": same32,
        "av32": np.full((P, P), 1.0 / PER_GROUP, f),
    }


def layout(v):
    c = np.ascontiguousarray
    return {
        "x": c(v["x"]), "src": c(v["src"]), "dst": c(v["dst"]),
        "w0": c(v["L0_gnn_W"]), "w0t": c(v["L0_gnn_W"].T),
        "al": c(v["L0_gnn_attn_l"].reshape(D, 1)), "ar": c(v["L0_gnn_attn_r"].reshape(D, 1)), "bias0": c(v["L0_gnn_bias"]),
        "w1t": c(v["L1_gnn_W"].T), "b1": c(v["L1_gnn_b"]),
        "w_in_t": c(v["L2_gnn_W_in"].T), "b_in": c(v["L2_gnn_b_in"]),
        "w_out_t": c(v["L2_gnn_W_out"].T), "b_out": c(v["L2_gnn_b_out"]),
        "w_ih_t": c(v["L2_gnn_w_ih"].T.reshape(2, D, 3 * D)), "w_hh_t": c(v["L2_gnn_w_hh"].T),
        "b_ih": c(v["L2_gnn_b_ih"]), "b_hh": c(v["L2_gnn_b_hh"]),
        "w3": c(v["L3_gnn_W"].reshape(2, D, D)), "b3": c(v["L3_gnn_b"]),
        "gamma": c(v["L3_gnn_gamma"]), "beta": c(v["L3_gnn_beta"]),
    }


def kernel(**inputs):
    import concourse.bacc as bacc
    from concourse.bass_utils import run_bass_kernel_spmd

    arrays = {**layout({k: np.asarray(v) for k, v in inputs.items()}), **constants()}
    nc = bacc.Bacc("TRN2", target_bir_lowering=False, num_devices=1)
    aps = {k: nc.dram_tensor(f"in_{k}", v.shape, mybir.dt.from_np(v.dtype), kind="ExternalInput").ap()
           for k, v in arrays.items()}
    out = nc.dram_tensor("out", (N, D), F32, kind="ExternalOutput").ap()
    gnn(nc, aps, out)
    r = run_bass_kernel_spmd(nc, [{f"in_{k}": v for k, v in arrays.items()}], core_ids=[0])
    return r.results[0]["out"]
```

```python
import numpy as np
from contextlib import ExitStack, contextmanager

import concourse.bass as bass
from concourse import mybir

F32 = mybir.dt.float32
BF16 = mybir.dt.bfloat16
I32 = mybir.dt.int32
ALU = mybir.AluOpType
ACT = mybir.ActivationFunctionType
AX = mybir.AxisListType.X

P = 128
D = 128
N = 100000
E = 25000
K = 4
CH = K * P
NCH = -(-E // CH)
SLOTS = NCH * CH
T = SLOTS // P
assert T % 14 == 0
HEADS, PER_HEAD = 8, 16
GROUPS, PER_GROUP = 4, 32
ROUTINGS = 6
LN_EPS = 1e-5
OUTSIDE = 1 << 20
RADIX_BITS = (6, 6, 5)
NEG = -1e30
AW = D + 4


class Step:
    CREDIT = 4

    def __init__(self, sem):
        self.sem = sem

    def wait(self, eng, chunk, back=0):
        eng.wait_ge(self.sem, chunk + (self.CREDIT + 1 - back))


class Dma:

    def __init__(self, sems, each, primed):
        self.sems, self.each, self.primed = sems, each, primed

    def wait(self, eng, turn, u):
        eng.wait_ge(self.sems[u], turn * (16 * self.each) + 16 * self.each + 16 * self.primed)

    def wait_before(self, eng, turn, u):
        eng.wait_ge(self.sems[u], turn * (16 * self.each) + 16)

    def wait_all(self, eng, n):
        for u, s in enumerate(self.sems):
            uses = len(range(u, n, len(self.sems)))
            eng.wait_ge(s, 16 * (self.each * uses + self.primed))


class Phase:

    def __init__(self, nc, name, primer):
        self.nc, self.name, self.primer = nc, name, primer
        self.ctx = ExitStack()
        self.steps, self.dmas, self.sems = [], [], []

    def sb(self, name, shape, dt=F32):
        return self.ctx.enter_context(self.nc.sbuf_tensor(f"{self.name}_{name}", shape, dt))

    def ps(self, name, shape, dt=F32):
        return self.ctx.enter_context(self.nc.psum_tensor(f"{self.name}_ps_{name}", shape, dt))

    def sem(self, name):
        s = self.nc.alloc_semaphore(f"{self.name}_{name}")
        self.sems.append(s)
        return s

    def step(self, name):
        self.steps.append(Step(self.sem(name)))
        return self.steps[-1]

    def dma(self, name, each=1, primed_by=None, bufs=2):
        d = Dma([self.sem(f"{name}{u}") for u in range(bufs)], each, int(primed_by is not None))
        if primed_by:
            self.dmas.append((d, primed_by))
        return d

    def prime(self, eng, who):
        row = 0
        for d, by in self.dmas:
            for s in d.sems:
                if by == who:
                    eng.dma_start(self.primer[0][row], self.primer[1][row]).then_inc(s, 16)
                row += 1
        if who == "sp":
            for s in self.steps:
                eng.sem_inc(s.sem, Step.CREDIT)

    def close(self):
        self.ctx.close()
        self.nc.clear_and_free_semaphores(self.sems)
        self.nc.all_engine_barrier()


def chunks(eng, n=NCH):
    with eng.Fori(0, n // 2) as i:
        for u in range(2):
            yield 2 * i + u, i, u


def rank_and_scatter(nc, primer, name, shift, bits, load, table_out, iota_in, tri_in, ones_in, unsorted):
    B = 1 << bits
    SC = T // 14
    ph = Phase(nc, name, primer)
    pairs = ph.sb("pairs", [P, T, 2], I32)
    dig_i = ph.sb("dig_i", [P, T], I32)
    dig = ph.sb("dig", [P, T])
    onehot = ph.sb("onehot", [P, B, T], BF16)
    count = ph.sb("count", [P, B, T])
    iota = ph.sb("iota", [P, B])
    tri = ph.sb("tri", [P, P])
    ones = ph.sb("ones", [P, P])
    ends = ph.sb("ends", [P, B])
    before = ph.sb("before", [P, B])
    held = ph.sb("held", [P, B])
    cum = ph.sb("cum", [P, B])
    base = ph.sb("base", [P, B])
    rank = ph.sb("rank", [P, T])
    rank_i = ph.sb("rank_i", [P, T], I32)
    st_rank = ph.sb("st_rank", [P, 2, SC], I32)
    st_pair = ph.sb("st_pair", [P, 2, SC, 2], I32)
    ps_below = ph.ps("below", [P, B])
    ps_total = ph.ps("total", [P, B])
    loaded, ranked, counted, summed, link_s = (ph.sem(x) for x in ("loaded", "ranked", "counted", "summed", "link"))
    staged = ph.sem("staged")
    passed = ph.sem("passed")
    scattered = ph.dma("scattered", each=SC, primed_by="pool")
    n_loads = [0]

    with nc.Block() as block:
        @block.sync
        def _(sp):
            with sp.If(sp.value_load(unsorted[0:1, 0:1], min_val=0, max_val=SLOTS) > 0):
                ph.prime(sp, "sp")
                for dst, src in ((iota[:], iota_in[:, 0:B]), (tri[:], tri_in), (ones[:], ones_in)):
                    sp.dma_start(dst, src).then_inc(loaded, 16)
                n_loads[0] = 3 + load(sp, pairs, loaded)

        @block.vector
        def _(dve):
            with dve.If(dve.value_load(unsorted[0:1, 0:1], min_val=0, max_val=SLOTS) > 0):
                v = nc.vector
                n = [0]

                def link(ins):
                    n[0] += 1
                    ins.then_inc(link_s, 1)
                    dve.wait_ge(link_s, n[0])

                dve.wait_ge(loaded, 16 * n_loads[0])
                link(v.tensor_scalar(dig_i[:], pairs[:, :, 0], shift, B - 1, ALU.logical_shift_right, ALU.bitwise_and))
                link(v.tensor_copy(dig[:], dig_i[:]))
                link(v.tensor_tensor(onehot[:], dig[:, None, :].to_broadcast([P, B, T]),
                                     iota[:, :, None].to_broadcast([P, B, T]), ALU.is_equal))
                flat_hot = onehot[:].rearrange("p b t -> p (b t)")
                flat = count[:].rearrange("p b t -> p (b t)")
                link(v.tensor_tensor_scan(out=flat, data0=flat_hot, data1=flat_hot, initial=0.0, op0=ALU.add, op1=ALU.max))
                link(v.tensor_copy(ends[:], count[:, :, T - 1]))
                v.memset(before[:, 0:1], 0.0)
                link(v.tensor_copy(before[:, 1:B], ends[:, 0:B - 1]))
                v.tensor_tensor(held[:], ends[:], before[:], ALU.subtract).then_inc(counted, 1)
                dve.wait_ge(summed, 1)
                link(v.tensor_copy(held[:], ps_total[:]))
                link(v.tensor_tensor_scan(out=cum[:], data0=held[:], data1=held[:], initial=0.0, op0=ALU.add, op1=ALU.max))
                link(v.tensor_tensor(base[:], cum[:], held[:], ALU.subtract))
                link(v.tensor_tensor(base[:], base[:], ps_below[:], ALU.add))
                link(v.scalar_tensor_tensor(base[:], base[:], -1.0, before[:], ALU.add, ALU.subtract))
                link(v.tensor_tensor(count[:], count[:], base[:, :, None].to_broadcast([P, B, T]), ALU.add))
                link(v.tensor_tensor(count[:], count[:], onehot[:], ALU.mult))
                link(v.tensor_reduce(rank[:], count[:].rearrange("p b t -> p t b"), AX, ALU.add))
                v.tensor_copy(rank_i[:], rank[:]).then_inc(ranked, 1)

        @block.tensor
        def _(pe):
            with pe.If(pe.value_load(unsorted[0:1, 0:1], min_val=0, max_val=SLOTS) > 0):
                pe.wait_ge(loaded, 48)
                pe.wait_ge(counted, 1)
                nc.tensor.matmul(ps_below[:], tri[:], held[:], start=True, stop=True)
                nc.tensor.matmul(ps_total[:], ones[:], held[:], start=True, stop=True).then_inc(summed, 1)

        @block.gpsimd
        def _(pool):
            with pool.If(pool.value_load(unsorted[0:1, 0:1], min_val=0, max_val=SLOTS) > 0):
                ph.prime(pool, "pool")
                pool.wait_ge(ranked, 1)
                for c, i, u in chunks(pool, T // SC):
                    scattered.wait_before(pool, i, u)
                    nc.gpsimd.tensor_copy(st_rank[:, u], rank_i[:, bass.ds(c * SC, SC)])
                    nc.gpsimd.tensor_copy(st_pair[:, u], pairs[:, bass.ds(c * SC, SC), :]).then_inc(staged, 1)
                    pool.wait_ge(staged, c + 1)
                    pool.sem_inc(passed, 1)
                    for k in range(SC):
                        nc.gpsimd.indirect_dma_start(
                            table_out, bass.IndirectOffsetOnAxis(ap=st_rank[:, u, k:k + 1], axis=0),
                            st_pair[:, u, k], None).then_inc(scattered.sems[u], 16)
                scattered.wait_all(pool, T // SC)
    ph.close()


def check_order(nc, primer, load, table, ones_in, unsorted):
    ph = Phase(nc, "order", primer)
    pairs = ph.sb("pairs", [P, T, 2], I32); after = ph.sb("after", [P, 2], I32); ones = ph.sb("ones", [P, P])
    key = ph.sb("key", [P, T + 1]); above = ph.sb("above", [P, T]); count = ph.sb("count", [P, 1])
    ps_total = ph.ps("total", [P, 1])
    loaded, stored, turned, cleared, link_s, counted, totalled = (
        ph.sem(x) for x in ("loaded", "stored", "turned", "cleared", "link", "counted", "totalled"))
    flat = table.rearrange("(p t) w -> p t w", t=T)
    n_loads = [0]
    with nc.Block() as block:
        @block.sync
        def _(sp):
            n_loads[0] = 1 + load(sp, pairs, loaded)
            sp.dma_start(ones[:], ones_in).then_inc(loaded, 16)
            sp.wait_ge(loaded, 16 * n_loads[0])
            sp.dma_start(flat, pairs[:]).then_inc(stored, 16)
            sp.wait_ge(stored, 16)
            sp.wait_ge(cleared, 1)
            sp.dma_start(after[0:P - 1], flat[1:P, 0]).then_inc(turned, 16)

        @block.vector
        def _(dve):
            v = nc.vector
            v.memset(after[:], N).then_inc(cleared, 1)
            dve.wait_ge(loaded, 16 * n_loads[0])
            v.tensor_copy(key[:, 0:T], pairs[:, :, 0]).then_inc(link_s, 1)
            dve.wait_ge(turned, 16)
            v.tensor_copy(key[:, T:T + 1], after[:, 0:1]).then_inc(link_s, 1)
            dve.wait_ge(link_s, 2)
            v.tensor_tensor(above[:], key[:, 0:T], key[:, 1:T + 1], ALU.is_gt).then_inc(link_s, 1)
            dve.wait_ge(link_s, 3)
            v.tensor_reduce(count[:], above[:], AX, ALU.add).then_inc(counted, 1)
            dve.wait_ge(totalled, 1)
            v.tensor_copy(unsorted[:], ps_total[:]).then_inc(link_s, 1)
            dve.wait_ge(link_s, 4)

        @block.tensor
        def _(pe):
            pe.wait_ge(loaded, 16 * n_loads[0])
            pe.wait_ge(counted, 1)
            nc.tensor.matmul(ps_total[:], ones[:], count[:], start=True, stop=True).then_inc(totalled, 1)
    ph.close()


def sort_edges(nc, primer, src, dst, tables, consts, unsorted):
    own, rest = divmod(E, T)
    assert rest > 0

    def load_inputs(sp, pairs, loaded):
        sp.dma_start(pairs[own:own + 1, rest:T], consts["padding"][own:own + 1, rest:T]).then_inc(loaded, 16)
        n = 1
        if own + 1 < P:
            sp.dma_start(pairs[own + 1:P], consts["padding"][own + 1:P]).then_inc(loaded, 16)
            n += 1
        with nc.allow_non_contiguous_dma(reason="interleaves the edge list once"):
            for w, nodes in enumerate((dst, src)):
                sp.dma_start(pairs[0:own, :, w], nodes[0:own * T].rearrange("(p t) -> p t", t=T)).then_inc(loaded, 16)
                sp.dma_start(pairs[own:own + 1, 0:rest, w], nodes[own * T:E][None, :]).then_inc(loaded, 16)
                n += 2
        return n

    def load_table(table):
        def load(sp, pairs, loaded):
            sp.dma_start(pairs[:], table.rearrange("(p t) w -> p t w", t=T)).then_inc(loaded, 16)
            return 1
        return load

    loads = [load_inputs, load_table(tables[0]), load_table(tables[1])]
    outs = [tables[0], tables[1], tables[0]]
    check_order(nc, primer, loads[0], tables[0], consts["ones"], unsorted)
    shift = 0
    for n, bits in enumerate(RADIX_BITS):
        rank_and_scatter(nc, primer, f"sort{n}", shift, bits, loads[n], outs[n], consts["iota"], consts["tri"], consts["ones"],
                         unsorted)
        shift += bits


def slot_tables(nc, primer, table, masks, lists, src_row, idx, src_col):
    ph = Phase(nc, "slots", primer)
    pairs = ph.sb("pairs", [P, T, 2], I32)
    edge = ph.sb("edge", [P, 2, 2], I32)
    key = ph.sb("key", [P, T + 2])
    mk = ph.sb("mk", [P, 6, T], BF16)
    same = ph.sb("same", [P, 2, T])
    row = ph.sb("row", [P, 6, T])
    row_i = ph.sb("row_i", [P, 5, T], I32)
    cleared, loaded, link_s, built, stored, indexed = (
        ph.sem(x) for x in ("cleared", "loaded", "link", "built", "stored", "indexed"))
    flat = table.rearrange("(p t) w -> p t w", t=T)
    with nc.Block() as block:
        @block.sync
        def _(sp):
            sp.dma_start(pairs[:], flat).then_inc(loaded, 16)
            sp.wait_ge(cleared, 1)
            sp.dma_start(edge[1:P, 0], flat[0:P - 1, T - 1]).then_inc(loaded, 16)
            sp.dma_start(edge[0:P - 1, 1], flat[1:P, 0]).then_inc(loaded, 16)
            sp.wait_ge(built, 1)
            for d in range(2):
                for m in range(3):
                    sp.dma_start(masks[d, m].rearrange("(p t) -> p t", t=T), mk[:, 3 * d + m]).then_inc(stored, 16)
            for n in range(5):
                sp.dma_start(lists[n].rearrange("(p t) -> p t", t=T), row_i[:, n]).then_inc(stored, 16)
            sp.dma_start(src_row.rearrange("(p t) -> p t", t=T), row[:, 4]).then_inc(stored, 16)
            sp.wait_ge(stored, 16 * 12)
            with nc.allow_non_contiguous_dma(reason="slot t * 128 + p to partition p, once"):
                for n in range(5):
                    sp.dma_start(idx[:, n], lists[n].rearrange("(t p) -> p t", p=P)).then_inc(indexed, 16)
            sp.wait_ge(indexed, 16 * 5)

        @block.vector
        def _(dve):
            v = nc.vector
            n = [0]

            def link(ins):
                n[0] += 1
                ins.then_inc(link_s, 1)
                dve.wait_ge(link_s, n[0])

            v.memset(edge[:], -1).then_inc(cleared, 1)
            dve.wait_ge(loaded, 48)
            v.tensor_copy(key[:, 1:T + 1], pairs[:, :, 0])
            v.tensor_copy(key[:, 0:1], edge[:, 0, 0:1])
            v.tensor_copy(key[:, T + 1:T + 2], edge[:, 1, 0:1])
            link(v.tensor_copy(row[:, 0], pairs[:, :, 1]))
            v.tensor_tensor(same[:, 0], key[:, 1:T + 1], key[:, 0:T], ALU.is_equal)
            link(v.tensor_tensor(same[:, 1], key[:, 1:T + 1], key[:, 2:T + 2], ALU.is_equal))
            for d in range(2):
                v.tensor_copy(mk[:, 3 * d], same[:, d])
                v.tensor_scalar(mk[:, 3 * d + 1], same[:, d], -1.0, 1.0, ALU.mult, ALU.add)
                v.tensor_scalar(mk[:, 3 * d + 2], same[:, d], -1.0, -NEG, ALU.add, ALU.mult)
            v.tensor_scalar(row[:, 1], key[:, 1:T + 1], float(N - 1), None, ALU.min)
            v.scalar_tensor_tensor(row[:, 2], same[:, 0], float(OUTSIDE), key[:, 1:T + 1], ALU.mult, ALU.add)
            v.scalar_tensor_tensor(row[:, 3], same[:, 1], float(OUTSIDE), key[:, 1:T + 1], ALU.mult, ALU.add)
            link(v.tensor_scalar(row[:, 5], key[:, 1:T + 1], float(N), float(OUTSIDE), ALU.is_ge, ALU.mult))
            link(v.tensor_tensor(row[:, 4], row[:, 5], row[:, 0], ALU.add))
            v.tensor_copy(row_i[:], row[:, 0:5]).then_inc(built, 1)
            dve.wait_ge(indexed, 16 * 5)
            v.tensor_copy(src_col[:], idx[:, 4])
    ph.close()


U = 4


class Tick:

    def __init__(self, n, t, loop=None):
        self.n, self.t, self.loop = n, t, loop

    def at(self, delay):
        c = self.t - delay
        if self.loop is not None:
            yield self.loop * U + c, self.loop + c // U, c % U
        elif 0 <= c < self.n:
            yield c, c // U, c % U


def ticks(eng, n, depth, peeled=0):
    fill = -(-depth // U) * U
    full = (n - peeled) // U * U
    assert full > fill
    for t in range(fill):
        yield Tick(n, t)
    with eng.Fori(0, (full - fill) // U) as loop:
        for t in range(fill, fill + U):
            yield Tick(n, t, loop)
    for t in range(full, n + depth):
        yield Tick(n, t)


def wait_other(step, eng, chunk, ahead, n):
    if not isinstance(chunk, int):
        step.wait(eng, chunk, back=-ahead)
    elif chunk + ahead >= 0:
        step.wait(eng, min(chunk + ahead, n - 1))


def row_scale(nc, out, src, mv, rstd, k=K):
    for j in range(k):
        last = nc.vector.tensor_scalar(out[:, j], src[:, j], mv[:, j, 0:1], rstd[:, j:j + 1], ALU.subtract, ALU.mult)
    return last


def spread(row):
    return row[None, :].to_broadcast([P, row.shape[0]])


NG = -(-N // CH) // 2 * 2 + (-(-N // CH)) % 2 * 2
assert NG * CH >= N and (NG - 1) * CH < N


def group_rows(table, c):
    start = N - CH if isinstance(c, int) and c == NG - 1 else c * CH
    return table[bass.ds(start, CH)].rearrange("(p k) d -> p k d", k=K)


def row_stats(nc, src, stats, k=K):
    for j in range(k):
        last = nc.vector.bn_stats(stats[:, j], src[:, j])
    return last


def row_moments(nc, stats, mv, k=K):
    for j in range(k):
        last = nc.vector.bn_aggr(mv[:, j], stats[:, j])
    return last


def dense_first(nc, primer, x, x1, x2, w1t, bias0, b1, ident, small, tables_to_clear):
    ph = Phase(nc, "d1", primer)
    W = ph.sb("w", [P, D]); B0 = ph.sb("b0", [P, D]); B1 = ph.sb("b1", [P, D]); I = ph.sb("i", [P, P])
    sm = ph.sb("sm", [P, 4])
    zeros = ph.sb("zeros", [P, K, AW])
    xin, xb, x1r, h, sq, hn, y, x2r = (ph.sb(s, [P, U, K, D]) for s in "xin xb x1r h sq hn y x2r".split())
    x1t = ph.sb("x1t", [P, U, CH])
    st = ph.sb("st", [P, U, 2, K, 6]); mv = ph.sb("mv", [P, U, 2, K, 2])
    lnv = ph.sb("lnv", [P, U, 2, K]); rstd = ph.sb("rstd", [P, U, 2, K]); shift = ph.sb("shift", [P, U, K])
    n2, ln2, rn = (ph.sb(s, [P, U, K * GROUPS]) for s in "n2 ln2 rn".split())
    ps_t = ph.ps("t", [P, 2, CH]); ps_h = ph.ps("h", [P, 2, K, D])
    consts, cleared, zero, passed = (ph.sem(s) for s in ("consts", "cleared", "zero", "passed"))
    loaded = ph.dma("loaded", bufs=U)
    stored1 = ph.dma("stored1", primed_by="sp", bufs=U); stored2 = ph.dma("stored2", primed_by="sp", bufs=U)
    names = ("biased measured0 moved0 logged0 scaled0 x1_made x1_turned x1t_made h_made h_biased squared reduced summed "
             "n_logged n_made h_normed added measured1 moved1 logged1 scaled1 shifted x2_made").split()
    s = {n: ph.step(n) for n in names}
    groups = lambda ap: ap.rearrange("p k (g e) -> p (k g) e", g=GROUPS)
    BIAS, NORM0, RSTD0, X1, HB, SUM, ADD, NORM1, RSTD1, SCALE, STORE = 1, 2, 3, 4, 5, 6, 7, 8, 9, 10, 11
    DEPTH = STORE
    with nc.Block() as block:
        @block.sync
        def _(sp):
            n_spare = 0
            ph.prime(sp, "sp")
            for a, b in ((W[:], w1t), (B0[:], spread(bias0)), (B1[:], spread(b1)), (I[:], ident), (sm[:], small)):
                sp.dma_start(a, b).then_inc(consts, 16)
            sp.wait_ge(zero, 1)
            for t in tables_to_clear:
                if t.shape[0] > N:
                    sp.dma_start(t[N:N + P], zeros[:, 0, 0:t.shape[1]]).then_inc(cleared, 16)
                    n_spare = n_spare + 1
            for tick in ticks(sp, NG, DEPTH, peeled=1):
                for c, i, u in tick.at(0):
                    s["biased"].wait(sp, c, back=U)
                    sp.dma_start(xin[:, u], group_rows(x, c)).then_inc(loaded.sems[u], 16)
                for c, i, u in tick.at(STORE):
                    if isinstance(c, int) and c == NG - 1:
                        stored2.wait(sp, i, u - 1)
                        sp.wait_ge(cleared, 16 * (c * len(tables_to_clear) + n_spare))
                    s["x2_made"].wait(sp, c)
                    sp.dma_start(group_rows(x2, c), x2r[:, u]).then_inc(stored2.sems[u], 16)
                    for t in tables_to_clear:
                        sp.dma_start(group_rows(t[0:N], c), zeros[:, :, 0:t.shape[1]]).then_inc(cleared, 16)
                for c, i, u in tick.at(HB):
                    if isinstance(c, int) and c == NG - 1:
                        stored1.wait(sp, i, u - 1)
                    s["x1_made"].wait(sp, c)
                    sp.dma_start(group_rows(x1, c), x1r[:, u]).then_inc(stored1.sems[u], 16)
            stored1.wait_all(sp, NG)
            stored2.wait_all(sp, NG)
            sp.wait_ge(cleared, 16 * (NG * len(tables_to_clear) + n_spare))

        @block.gpsimd
        def _(pool):
            g = nc.gpsimd
            pool.wait_ge(consts, 80)
            for tick in ticks(pool, NG, DEPTH, peeled=1):
                for c, i, u in tick.at(ADD):
                    s["n_made"].wait(pool, c)
                    s["added"].wait(pool, c, back=U)
                    g.tensor_tensor(groups(hn[:, u]), groups(h[:, u]),
                                    rn[:, u][:, :, None].to_broadcast([P, K * GROUPS, PER_GROUP]), ALU.mult).then_inc(s["h_normed"].sem, 1)
                for c, i, u in tick.at(BIAS):
                    loaded.wait(pool, i, u)
                    s["x1_made"].wait(pool, c, back=U)
                    g.tensor_tensor(xb[:, u], xin[:, u], B0[:, None, :].to_broadcast([P, K, D]), ALU.add).then_inc(s["biased"].sem, 1)
                for c, i, u in tick.at(ADD):
                    s["h_normed"].wait(pool, c)
                    s["x2_made"].wait(pool, c, back=U)
                    g.tensor_tensor(y[:, u], hn[:, u], x1r[:, u], ALU.add).then_inc(s["added"].sem, 1)

        @block.vector
        def _(dve):
            v = nc.vector
            v.memset(zeros[:], 0.0).then_inc(zero, 1)
            dve.wait_ge(consts, 80)
            for tick in ticks(dve, NG, DEPTH, peeled=1):
                for c, i, u in tick.at(X1):
                    s["scaled0"].wait(dve, c)
                    stored1.wait_before(dve, i, u)
                    s["added"].wait(dve, c, back=U)
                    s["x1_turned"].wait(dve, c, back=U)
                    row_scale(nc, x1r[:, u], xb[:, u], mv[:, u, 0], rstd[:, u, 0]).then_inc(s["x1_made"].sem, 1)
                for c, i, u in tick.at(NORM1):
                    s["added"].wait(dve, c)
                    row_stats(nc, y[:, u], st[:, u, 1]).then_inc(s["measured1"].sem, 1)
                for c, i, u in tick.at(SUM):
                    s["squared"].wait(dve, c)
                    s["summed"].wait(dve, c, back=U)
                    s["n_logged"].wait(dve, c, back=U)
                    v.tensor_reduce(n2[:, u], groups(sq[:, u]), AX, ALU.add).then_inc(s["reduced"].sem, 1)
                for c, i, u in tick.at(NORM1):
                    s["scaled1"].wait(dve, c, back=U)
                    s["measured1"].wait(dve, c)
                    dve.sem_inc(passed, 1)
                    row_moments(nc, st[:, u, 1], mv[:, u, 1]).then_inc(s["moved1"].sem, 1)
                for c, i, u in tick.at(SUM):
                    s["reduced"].wait(dve, c)
                    v.tensor_scalar(n2[:, u], n2[:, u], 1e-25, None, ALU.max).then_inc(s["summed"].sem, 1)
                for c, i, u in tick.at(NORM0):
                    s["biased"].wait(dve, c)
                    row_stats(nc, xb[:, u], st[:, u, 0]).then_inc(s["measured0"].sem, 1)
                for c, i, u in tick.at(HB):
                    s["h_made"].wait(dve, c)
                    s["h_normed"].wait(dve, c, back=U)
                    s["squared"].wait(dve, c, back=U)
                    v.tensor_tensor(h[:, u], ps_h[:, u % 2], B1[:, None, :].to_broadcast([P, K, D]), ALU.add).then_inc(s["h_biased"].sem, 1)
                for c, i, u in tick.at(NORM0):
                    s["measured0"].wait(dve, c)
                    dve.sem_inc(passed, 1)
                    row_moments(nc, st[:, u, 0], mv[:, u, 0]).then_inc(s["moved0"].sem, 1)
                for c, i, u in tick.at(RSTD1):
                    s["scaled1"].wait(dve, c)
                    s["x2_made"].wait(dve, c, back=U)
                    v.scalar_tensor_tensor(shift[:, u], mv[:, u, 1, :, 0], -1.0, rstd[:, u, 1], ALU.mult, ALU.mult).then_inc(s["shifted"].sem, 1)

        @block.scalar
        def _(act):
            a = nc.scalar
            a.preload_act_table_set("natural_log_exp_and_others")
            act.wait_ge(consts, 80)
            for tick in ticks(act, NG, DEPTH, peeled=1):
                for c, i, u in tick.at(SUM):
                    s["h_biased"].wait(act, c)
                    s["reduced"].wait(act, c, back=U)
                    a.activation(sq[:, u], h[:, u], ACT.Square).then_inc(s["squared"].sem, 1)
                for c, i, u in tick.at(RSTD0):
                    s["moved0"].wait(act, c)
                    a.activation(lnv[:, u, 0], mv[:, u, 0, :, 1], ACT.Ln, bias=sm[:, 0:1]).then_inc(s["logged0"].sem, 1)
                for c, i, u in tick.at(ADD):
                    s["summed"].wait(act, c)
                    a.activation(ln2[:, u], n2[:, u], ACT.Ln, scale=2.0 ** 20).then_inc(s["n_logged"].sem, 1)
                for c, i, u in tick.at(RSTD1):
                    s["moved1"].wait(act, c)
                    a.activation(lnv[:, u, 1], mv[:, u, 1, :, 1], ACT.Ln, bias=sm[:, 0:1]).then_inc(s["logged1"].sem, 1)
                for c, i, u in tick.at(ADD):
                    s["n_logged"].wait(act, c)
                    s["h_normed"].wait(act, c, back=U)
                    a.activation(rn[:, u], ln2[:, u], ACT.Exp, scale=-0.5, bias=sm[:, 1:2]).then_inc(s["n_made"].sem, 1)
                for c, i, u in tick.at(RSTD0):
                    s["logged0"].wait(act, c)
                    s["x1_made"].wait(act, c, back=U)
                    a.activation(rstd[:, u, 0], lnv[:, u, 0], ACT.Exp, scale=-0.5).then_inc(s["scaled0"].sem, 1)
                for c, i, u in tick.at(RSTD1):
                    s["logged1"].wait(act, c)
                    a.activation(rstd[:, u, 1], lnv[:, u, 1], ACT.Exp, scale=-0.5).then_inc(s["scaled1"].sem, 1)
                for c, i, u in tick.at(SCALE):
                    s["shifted"].wait(act, c)
                    stored2.wait_before(act, i, u)
                    for k in range(K):
                        last = a.activation(x2r[:, u, k], y[:, u, k], ACT.Identity, scale=rstd[:, u, 1, k:k + 1], bias=shift[:, u, k:k + 1])
                    last.then_inc(s["x2_made"].sem, 1)
                for c, i, u in tick.at(X1):
                    s["x1_turned"].wait(act, c)
                    s["h_made"].wait(act, c, back=U)
                    a.copy(x1t[:, u], ps_t[:, u % 2]).then_inc(s["x1t_made"].sem, 1)

        @block.tensor
        def _(pe):
            pe.wait_ge(consts, 80)
            for tick in ticks(pe, NG, DEPTH, peeled=1):
                for c, i, u in tick.at(HB):
                    s["x1t_made"].wait(pe, c)
                    s["h_biased"].wait(pe, c, back=2)
                    for k in range(K):
                        last = nc.tensor.matmul(ps_h[:, u % 2, k], x1t[:, u, k * P:(k + 1) * P], W[:], start=True, stop=True)
                    last.then_inc(s["h_made"].sem, 1)
                for c, i, u in tick.at(X1):
                    s["x1_made"].wait(pe, c)
                    s["x1t_made"].wait(pe, c, back=2)
                    for k in range(K):
                        last = nc.tensor.transpose(ps_t[:, u % 2, k * P:(k + 1) * P], x1r[:, u, k], I[:])
                    last.then_inc(s["x1_turned"].sem, 1)
    ph.close()


SRC, DST, FIRST, LAST, SRC_OUT = range(5)


class Rows:

    def __init__(self, ph, nc, idx, name, n_lists, bufs=2):
        self.nc, self.idx = nc, idx
        self.at = ph.sb(f"{name}_at", [P, bufs, n_lists, K], I32)
        self.staged, self.passed = ph.sem(f"{name}_staged"), ph.sem(f"{name}_passed")
        self.n_lists = n_lists

    def stage(self, pool, chunk, count, u, lists):
        for n, which in enumerate(lists):
            last = self.nc.gpsimd.tensor_copy(self.at[:, u, n], self.idx[:, which, bass.ds(chunk * K, K)])
        last.then_inc(self.staged, 1)
        pool.wait_ge(self.staged, count + 1)
        pool.sem_inc(self.passed, 1)

    def gather(self, u, n, rows, table, sem, tiles=range(K)):
        for k in tiles:
            self.nc.gpsimd.indirect_dma_start(rows[:, k], None, table, bass.IndirectOffsetOnAxis(
                ap=self.at[:, u, n, k:k + 1], axis=0)).then_inc(sem, 16)

    def scatter(self, u, n, rows, table, sem, tiles=range(K)):
        for k in tiles:
            self.nc.gpsimd.indirect_dma_start(table, bass.IndirectOffsetOnAxis(
                ap=self.at[:, u, n, k:k + 1], axis=0), rows[:, k], None,
                bounds_check=N - 1, oob_is_err=False).then_inc(sem, 16)


def mask_rows(masks, direction, first, n, chunk):
    return masks[direction, first:first + n, bass.ds(chunk * CH, CH)][None].to_broadcast([P, n, CH])


def gat_forward(nc, primer, x, idx, masks, w0, wt0, al, ar, bo16, ident, zt, l0t, xd0):
    ph = Phase(nc, "g0", primer)
    W = ph.sb("w", [P, D]); WT = ph.sb("wt", [P, D]); B16 = ph.sb("b16", [P, P]); I = ph.sb("i", [P, P])
    acol = ph.sb("acol", [P, 2]); ab = ph.sb("ab", [P, 2, P]); WA = ph.sb("wa", [P, 2, P]); none = ph.sb("none", [P, 1])
    rows = ph.sb("rows", [P, U, 2, K, D])
    xt = ph.sb("xt", [P, U, 2, CH]); mk = ph.sb("mk", [P, U, 1, CH], BF16)
    er = ph.sb("er", [P, U, CH]); o = ph.sb("o", [P, U, 3, CH])
    ps_x = ph.ps("x", [P, 2, 2, CH]); ps_ze = ph.ps("ze", [P, 2, 2, CH])
    rr = Rows(ph, nc, idx, "rows", 2, bufs=U)
    consts, ready, vinit = ph.sem("consts"), ph.sem("ready"), ph.sem("vinit")
    gathered = ph.dma("gathered", each=2 * K, bufs=U)
    masked = ph.dma("masked", bufs=U)
    kept = ph.dma("kept", primed_by="sp", bufs=U)
    stored = ph.dma("stored", each=2, primed_by="sp", bufs=U)
    turned, moved, moved_v, made, copied, scored, scanned = (ph.step(s) for s in (
        "turned", "moved", "moved_v", "made", "copied", "scored", "scanned"))
    TURN, MAKE, COPY, SCAN, STORE = 2, 3, 4, 5, 6
    DEPTH = STORE
    with nc.Block() as block:
        @block.sync
        def _(sp):
            ph.prime(sp, "sp")
            for a, b in ((W[:], w0), (WT[:], wt0), (B16[:], bo16), (I[:], ident), (acol[:, 0:1], al), (acol[:, 1:2], ar)):
                sp.dma_start(a, b).then_inc(consts, 16)
            for tick in ticks(sp, NCH, DEPTH):
                for c, i, u in tick.at(STORE):
                    scanned.wait(sp, c)
                    sp.dma_start(zt[c], o[:, u, 0]).then_inc(stored.sems[u], 16)
                    sp.dma_start(l0t[c], o[:, u, 1:3]).then_inc(stored.sems[u], 16)
                for c, i, u in tick.at(MAKE):
                    scanned.wait(sp, c, back=U)
                    sp.dma_start(mk[:, u], mask_rows(masks, 0, 2, 1, c)).then_inc(masked.sems[u], 16)
                for c, i, u in tick.at(TURN):
                    gathered.wait(sp, i, u)
                    sp.dma_start(xd0[c], rows[:, u, 1]).then_inc(kept.sems[u], 16)
            kept.wait_all(sp, NCH)
            stored.wait_all(sp, NCH)

        @block.gpsimd
        def _(pool):
            for tick in ticks(pool, NCH, DEPTH):
                for c, i, u in tick.at(0):
                    turned.wait(pool, c, back=U)
                    kept.wait_before(pool, i, u)
                    rr.stage(pool, c, c, u, (SRC, DST))
                    rr.gather(u, 0, rows[:, u, 0], x, gathered.sems[u])
                    rr.gather(u, 1, rows[:, u, 1], x, gathered.sems[u])

        @block.vector
        def _(dve):
            v = nc.vector
            dve.wait_ge(consts, 96)
            for j in range(2):
                v.tensor_scalar(ab[:, j], B16[:], acol[:, j:j + 1], None, ALU.mult).then_inc(vinit, 1)
            dve.wait_ge(ready, 1)
            v.memset(none[:], 0.0).then_inc(vinit, 1)
            v.tensor_copy(WA[:], ps_x[:, 0, 0, 0:2 * P].rearrange("p (j o) -> p j o", j=2)).then_inc(vinit, 1)
            dve.wait_ge(vinit, 4)
            for tick in ticks(dve, NCH, DEPTH):
                for c, i, u in tick.at(SCAN):
                    copied.wait(dve, c)
                    stored.wait_before(dve, i, u)
                    masked.wait(dve, i, u)
                    v.scalar_tensor_tensor(o[:, u, 1], er[:, u], 0.2, er[:, u], ALU.mult, ALU.max).then_inc(scored.sem, 1)
                for c, i, u in tick.at(TURN):
                    turned.wait(dve, c)
                    made.wait(dve, c, back=U)
                    v.tensor_copy(xt[:, u, 1], ps_x[:, u % 2, 1]).then_inc(moved_v.sem, 1)
                for c, i, u in tick.at(SCAN):
                    scored.wait(dve, c)
                    scanned.wait(dve, c, back=1)
                    v.tensor_tensor_scan(out=o[:, u, 2], data0=mk[:, u, 0], data1=o[:, u, 1],
                                         initial=none[:] if isinstance(c, int) and c == 0 else o[:, (u - 1) % U, 2, CH - 1:CH],
                                         op0=ALU.add, op1=ALU.max).then_inc(scanned.sem, 1)

        @block.scalar
        def _(act):
            a = nc.scalar
            for tick in ticks(act, NCH, DEPTH):
                for c, i, u in tick.at(COPY):
                    made.wait(act, c)
                    stored.wait_before(act, i, u)
                    scored.wait(act, c, back=U)
                    a.copy(o[:, u, 0], ps_ze[:, u % 2, 0])
                    a.copy(er[:, u], ps_ze[:, u % 2, 1]).then_inc(copied.sem, 1)
                for c, i, u in tick.at(TURN):
                    turned.wait(act, c)
                    made.wait(act, c, back=U)
                    a.copy(xt[:, u, 0], ps_x[:, u % 2, 0]).then_inc(moved.sem, 1)

        @block.tensor
        def _(pe):
            t = nc.tensor
            pe.wait_ge(consts, 96)
            pe.wait_ge(vinit, 2)
            for j in range(2):
                last = t.matmul(ps_x[:, 0, 0, j * P:(j + 1) * P], WT[:], ab[:, j], start=True, stop=True)
            last.then_inc(ready, 1)
            pe.wait_ge(vinit, 4)
            for tick in ticks(pe, NCH, DEPTH):
                for c, i, u in tick.at(MAKE):
                    moved.wait(pe, c)
                    moved_v.wait(pe, c)
                    copied.wait(pe, c, back=2)
                    t.matmul(ps_ze[:, u % 2, 0], W[:], xt[:, u, 0], start=True, stop=True)
                    t.matmul(ps_ze[:, u % 2, 1], WA[:, 0], xt[:, u, 0], start=True, stop=False)
                    t.matmul(ps_ze[:, u % 2, 1], WA[:, 1], xt[:, u, 1], start=False, stop=True).then_inc(made.sem, 1)
                for c, i, u in tick.at(TURN):
                    gathered.wait(pe, i, u)
                    moved.wait(pe, c, back=2)
                    moved_v.wait(pe, c, back=2)
                    for j in range(2):
                        for k in range(K):
                            last = t.transpose(ps_x[:, u % 2, j, k * P:(k + 1) * P], rows[:, u, j, k], I[:])
                    last.then_inc(turned.sem, 1)
    ph.close()


def gat_backward(nc, primer, idx, masks, bias0, sel8, ident, small, zt, l0t, xd0, x1):
    ph = Phase(nc, "g1", primer)
    B0 = ph.sb("b0", [P, D]); S8 = ph.sb("s8", [P, HEADS]); I = ph.sb("i", [P, P]); sm = ph.sb("sm", [P, 4]); none = ph.sb("none", [P, 1])
    z, t1, mx, a_, msg = (ph.sb(n, [P, U, CH]) for n in "z t1 mx a msg".split())
    em = ph.sb("em", [P, U, 2, CH]); mk = ph.sb("mk", [P, U, 2, CH], BF16); mk2 = ph.sb("mk2", [P, U, 1, CH], BF16)
    nd = ph.sb("nd", [P, U, 2, CH])
    xd, xb, agg, x1r = (ph.sb(n, [P, U, K, D]) for n in "xd xb agg x1r".split())
    den = ph.sb("den", [P, U, K * HEADS])
    st = ph.sb("st", [P, U, K, 6]); mv = ph.sb("mv", [P, U, K, 2]); lnv = ph.sb("lnv", [P, U, K]); rstd = ph.sb("rstd", [P, U, K])
    ps_n = ph.ps("n", [P, 2, CH]); ps_d = ph.ps("d", [P, 2, CH])
    rr = Rows(ph, nc, idx, "rows", 1, bufs=U)
    consts, vinit, passed = (ph.sem(s) for s in ("consts", "vinit", "passed"))
    loaded = ph.dma("loaded", each=2, bufs=U)
    loaded_z = ph.dma("loaded_z", bufs=U)
    masked2 = ph.dma("masked2", bufs=U)
    loaded_x = ph.dma("loaded_x", bufs=U)
    scattered = ph.dma("scattered", each=K, primed_by="pool", bufs=U)
    names = ("started spread shifted exped weighed scanned turned clamped inverted divided joined measured meaned logged "
             "scaled x1_made biased").split()
    s = {n: ph.step(n) for n in names}
    back = lambda c: c * -1 + (NCH - 1)
    START, SPREAD, EXP, MSG, SCAN, TURN, NORM, RSTD, X1, SCAT = 1, 2, 3, 4, 5, 6, 7, 8, 9, 10
    DEPTH = SCAT
    with nc.Block() as block:
        @block.sync
        def _(sp):
            ph.prime(sp, "sp")
            for a, b in ((B0[:], spread(bias0)), (S8[:], sel8), (I[:], ident), (sm[:], small)):
                sp.dma_start(a, b).then_inc(consts, 16)
            for tick in ticks(sp, NCH, DEPTH):
                for c, i, u in tick.at(SCAN):
                    s["biased"].wait(sp, c, back=U)
                    sp.dma_start(xd[:, u], xd0[back(c)]).then_inc(loaded_x.sems[u], 16)
                for c, i, u in tick.at(MSG):
                    s["scanned"].wait(sp, c, back=U)
                    sp.dma_start(mk2[:, u], mask_rows(masks, 1, 0, 1, back(c))).then_inc(masked2.sems[u], 16)
                for c, i, u in tick.at(EXP):
                    s["weighed"].wait(sp, c, back=U)
                    sp.dma_start(z[:, u], zt[back(c)]).then_inc(loaded_z.sems[u], 16)
                for c, i, u in tick.at(0):
                    s["spread"].wait(sp, c, back=U)
                    s["exped"].wait(sp, c, back=U)
                    sp.dma_start(em[:, u], l0t[back(c)]).then_inc(loaded.sems[u], 16)
                    sp.dma_start(mk[:, u], mask_rows(masks, 1, 0, 2, back(c))).then_inc(loaded.sems[u], 16)

        @block.gpsimd
        def _(pool):
            g = nc.gpsimd
            ph.prime(pool, "pool")
            pool.wait_ge(consts, 64)
            for tick in ticks(pool, NCH, DEPTH):
                for c, i, u in tick.at(MSG):
                    s["exped"].wait(pool, c)
                    loaded_z.wait(pool, i, u)
                    s["scanned"].wait(pool, c, back=U)
                    g.tensor_tensor(msg[:, u], z[:, u], a_[:, u], ALU.mult).then_inc(s["weighed"].sem, 1)
                for c, i, u in tick.at(START):
                    loaded.wait(pool, i, u)
                    s["spread"].wait(pool, c, back=U)
                    g.tensor_tensor(t1[:, u], mk[:, u, 1], em[:, u, 1], ALU.mult).then_inc(s["started"].sem, 1)
                for c, i, u in tick.at(TURN):
                    loaded_x.wait(pool, i, u)
                    s["joined"].wait(pool, c, back=U)
                    g.tensor_tensor(xb[:, u], xd[:, u], B0[:, None, :].to_broadcast([P, K, D]), ALU.add).then_inc(s["biased"].sem, 1)
                for c, i, u in tick.at(SCAT):
                    scattered.wait_before(pool, i, u)
                    s["x1_made"].wait(pool, c)
                    rr.stage(pool, back(c), c, u, (FIRST,))
                    rr.scatter(u, 0, x1r[:, u], x1, scattered.sems[u])
            scattered.wait_all(pool, NCH)

        @block.vector
        def _(dve):
            v = nc.vector
            v.memset(none[:], 0.0).then_inc(vinit, 1)
            dve.wait_ge(vinit, 1)
            for tick in ticks(dve, NCH, DEPTH):
                for c, i, u in tick.at(X1):
                    s["scaled"].wait(dve, c)
                    scattered.wait_before(dve, i, u)
                    row_scale(nc, x1r[:, u], agg[:, u], mv[:, u], rstd[:, u]).then_inc(s["x1_made"].sem, 1)
                for c, i, u in tick.at(NORM):
                    s["turned"].wait(dve, c)
                    s["divided"].wait(dve, c, back=U)
                    v.tensor_scalar(den[:, u], ps_d[:, u % 2, 0:K * HEADS], 1e-9, None, ALU.max).then_inc(s["clamped"].sem, 1)
                for c, i, u in tick.at(SPREAD):
                    s["started"].wait(dve, c)
                    s["spread"].wait(dve, c, back=1)
                    s["shifted"].wait(dve, c, back=U)
                    v.tensor_tensor_scan(out=mx[:, u, ::-1], data0=mk[:, u, 0, ::-1], data1=t1[:, u, ::-1],
                                         initial=none[:] if isinstance(c, int) and c == 0 else mx[:, (u - 1) % U, 0:1],
                                         op0=ALU.mult, op1=ALU.add).then_inc(s["spread"].sem, 1)
                for c, i, u in tick.at(NORM):
                    s["clamped"].wait(dve, c)
                    v.reciprocal(den[:, u], den[:, u]).then_inc(s["inverted"].sem, 1)
                for c, i, u in tick.at(SPREAD):
                    s["spread"].wait(dve, c)
                    v.tensor_tensor(em[:, u, 0], em[:, u, 0], mx[:, u], ALU.subtract).then_inc(s["shifted"].sem, 1)
                for c, i, u in tick.at(NORM):
                    s["inverted"].wait(dve, c)
                    s["x1_made"].wait(dve, c, back=U)
                    v.tensor_tensor(agg[:, u].rearrange("p k (h e) -> p (k h) e", h=HEADS),
                                    ps_n[:, u % 2].rearrange("p (g e) -> p g e", e=PER_HEAD),
                                    den[:, u][:, :, None].to_broadcast([P, K * HEADS, PER_HEAD]), ALU.mult).then_inc(s["divided"].sem, 1)
                for c, i, u in tick.at(SCAN):
                    s["weighed"].wait(dve, c)
                    masked2.wait(dve, i, u)
                    s["turned"].wait(dve, c, back=U)
                    s["scanned"].wait(dve, c, back=1)
                    for j, src in enumerate((msg, a_)):
                        done = v.tensor_tensor_scan(out=nd[:, u, j, ::-1], data0=mk2[:, u, 0, ::-1], data1=src[:, u, ::-1],
                                                    initial=none[:] if isinstance(c, int) and c == 0 else nd[:, (u - 1) % U, j, 0:1],
                                                    op0=ALU.mult, op1=ALU.add)
                    done.then_inc(s["scanned"].sem, 1)
                for c, i, u in tick.at(NORM):
                    s["divided"].wait(dve, c)
                    s["biased"].wait(dve, c)
                    v.tensor_tensor(agg[:, u], agg[:, u], xb[:, u], ALU.add).then_inc(s["joined"].sem, 1)
                    s["joined"].wait(dve, c)
                    row_stats(nc, agg[:, u], st[:, u]).then_inc(s["measured"].sem, 1)
                    s["measured"].wait(dve, c)
                    dve.sem_inc(passed, 1)
                    row_moments(nc, st[:, u], mv[:, u]).then_inc(s["meaned"].sem, 1)

        @block.scalar
        def _(act):
            a = nc.scalar
            a.preload_act_table_set("natural_log_exp_and_others")
            act.wait_ge(consts, 64)
            for tick in ticks(act, NCH, DEPTH):
                for c, i, u in tick.at(EXP):
                    s["shifted"].wait(act, c)
                    s["scanned"].wait(act, c, back=U)
                    s["weighed"].wait(act, c, back=U)
                    a.activation(a_[:, u], em[:, u, 0], ACT.Exp).then_inc(s["exped"].sem, 1)
                for c, i, u in tick.at(RSTD):
                    s["meaned"].wait(act, c)
                    a.activation(lnv[:, u], mv[:, u, :, 1], ACT.Ln, bias=sm[:, 0:1]).then_inc(s["logged"].sem, 1)
                    s["logged"].wait(act, c)
                    s["x1_made"].wait(act, c, back=U)
                    a.activation(rstd[:, u], lnv[:, u], ACT.Exp, scale=-0.5).then_inc(s["scaled"].sem, 1)

        @block.tensor
        def _(pe):
            t = nc.tensor
            pe.wait_ge(consts, 64)
            for tick in ticks(pe, NCH, DEPTH):
                for c, i, u in tick.at(TURN):
                    s["scanned"].wait(pe, c)
                    s["divided"].wait(pe, c, back=2)
                    for k in range(K):
                        t.transpose(ps_n[:, u % 2, k * P:(k + 1) * P], nd[:, u, 0, k * P:(k + 1) * P], I[:])
                    for k in range(K):
                        last = t.matmul(ps_d[:, u % 2, k * HEADS:(k + 1) * HEADS], nd[:, u, 1, k * P:(k + 1) * P], S8[:],
                                        start=True, stop=True)
                    last.then_inc(s["turned"].sem, 1)
    ph.close()


def route_start(nc, primer, x1, idx, w1t, b1, bo32, ident, small, zt, ct, x1d):
    ph = Phase(nc, "r0", primer)
    W = ph.sb("w", [P, D]); BO = ph.sb("bo", [P, P]); I = ph.sb("i", [P, P]); bcol = ph.sb("bcol", [P, 1]); sm = ph.sb("sm", [P, 4])
    rows = ph.sb("rows", [P, U, 2, K, D])
    xt, h, n2 = (ph.sb(s, [P, U, 2, CH]) for s in "xt h n2".split())
    sq = ph.sb("sq", [P, 2, 2, CH]); z = ph.sb("z", [P, U, CH])
    ps_x = ph.ps("x", [P, 2, CH]); ps_h = ph.ps("h", [P, 2, 2, CH]); ps_n = ph.ps("n", [P, 2, CH])
    rr = Rows(ph, nc, idx, "rows", 2, bufs=U)
    consts = ph.sem("consts")
    gathered = ph.dma("gathered", each=2 * K, bufs=U)
    kept = ph.dma("kept", primed_by="sp", bufs=U)
    stored = ph.dma("stored", primed_by="sp", bufs=U)
    names = "turned moved moved_v made biased squared summed clamped logged inverted z_made c_made".split()
    s = {n: ph.step(n) for n in names}
    TURN, H, SQ, ROOT, NORM, STORE = 2, 3, 4, 5, 6, 7
    DEPTH = STORE
    with nc.Block() as block:
        @block.sync
        def _(sp):
            ph.prime(sp, "sp")
            for a, b in ((W[:], w1t), (BO[:], bo32), (I[:], ident), (bcol[:], b1[:, None]), (sm[:], small)):
                sp.dma_start(a, b).then_inc(consts, 16)
            for tick in ticks(sp, NCH, DEPTH):
                for c, i, u in tick.at(TURN):
                    gathered.wait(sp, i, u)
                    sp.dma_start(x1d[c], rows[:, u, 1]).then_inc(kept.sems[u], 16)
                for c, i, u in tick.at(STORE):
                    s["z_made"].wait(sp, c)
                    sp.dma_start(zt[c], z[:, u]).then_inc(stored.sems[u], 16)
            kept.wait_all(sp, NCH)
            stored.wait_all(sp, NCH)

        @block.gpsimd
        def _(pool):
            for tick in ticks(pool, NCH, DEPTH):
                for c, i, u in tick.at(0):
                    s["turned"].wait(pool, c, back=U)
                    kept.wait_before(pool, i, u)
                    rr.stage(pool, c, c, u, (SRC, DST))
                    rr.gather(u, 0, rows[:, u, 0], x1, gathered.sems[u])
                    rr.gather(u, 1, rows[:, u, 1], x1, gathered.sems[u])

        @block.vector
        def _(dve):
            v = nc.vector
            for tick in ticks(dve, NCH, DEPTH):
                for c, i, u in tick.at(NORM):
                    s["inverted"].wait(dve, c)
                    v.tensor_tensor(ct[:, c], h[:, u, 1], n2[:, u, 1], ALU.mult).then_inc(s["c_made"].sem, 1)
                    stored.wait_before(dve, i, u)
                    v.tensor_tensor(z[:, u], h[:, u, 0], n2[:, u, 0], ALU.mult).then_inc(s["z_made"].sem, 1)
                for c, i, u in tick.at(TURN):
                    s["turned"].wait(dve, c)
                    s["made"].wait(dve, c, back=U)
                    v.tensor_copy(xt[:, u, 1], ps_x[:, 1]).then_inc(s["moved_v"].sem, 1)
                for c, i, u in tick.at(SQ):
                    s["summed"].wait(dve, c)
                    s["z_made"].wait(dve, c, back=U)
                    v.tensor_scalar(n2[:, u], ps_n[:], 1e-24, None, ALU.max).then_inc(s["clamped"].sem, 1)

        @block.scalar
        def _(act):
            a = nc.scalar
            a.preload_act_table_set("natural_log_exp_and_others")
            act.wait_ge(consts, 80)
            for tick in ticks(act, NCH, DEPTH):
                for c, i, u in tick.at(SQ):
                    s["biased"].wait(act, c)
                    s["summed"].wait(act, c, back=2)
                    a.activation(sq[:, u % 2], h[:, u], ACT.Square).then_inc(s["squared"].sem, 1)
                for c, i, u in tick.at(ROOT):
                    s["clamped"].wait(act, c)
                    a.activation(n2[:, u], n2[:, u], ACT.Ln, scale=2.0 ** 20).then_inc(s["logged"].sem, 1)
                for c, i, u in tick.at(TURN):
                    s["turned"].wait(act, c)
                    s["made"].wait(act, c, back=U)
                    a.copy(xt[:, u, 0], ps_x[:, 0]).then_inc(s["moved"].sem, 1)
                for c, i, u in tick.at(ROOT):
                    s["logged"].wait(act, c)
                    a.activation(n2[:, u], n2[:, u], ACT.Exp, scale=-0.5, bias=sm[:, 1:2]).then_inc(s["inverted"].sem, 1)
                for c, i, u in tick.at(H):
                    s["made"].wait(act, c)
                    s["z_made"].wait(act, c, back=U)
                    a.activation(h[:, u], ps_h[:, u % 2], ACT.Identity, bias=bcol[:]).then_inc(s["biased"].sem, 1)

        @block.tensor
        def _(pe):
            t = nc.tensor
            pe.wait_ge(consts, 80)
            for tick in ticks(pe, NCH, DEPTH):
                for c, i, u in tick.at(H):
                    s["moved"].wait(pe, c)
                    s["moved_v"].wait(pe, c)
                    s["biased"].wait(pe, c, back=2)
                    t.matmul(ps_h[:, u % 2, 0], W[:], xt[:, u, 0], start=True, stop=True)
                    t.matmul(ps_h[:, u % 2, 1], W[:], xt[:, u, 1], start=True, stop=True).then_inc(s["made"].sem, 1)
                for c, i, u in tick.at(TURN):
                    gathered.wait(pe, i, u)
                    s["moved"].wait(pe, c, back=1)
                    s["moved_v"].wait(pe, c, back=1)
                    for j in range(2):
                        for k in range(K):
                            last = t.transpose(ps_x[:, j, k * P:(k + 1) * P], rows[:, u, j, k], I[:])
                    last.then_inc(s["turned"].sem, 1)
                for c, i, u in tick.at(SQ):
                    s["squared"].wait(pe, c)
                    s["clamped"].wait(pe, c, back=1)
                    t.matmul(ps_n[:, 0], BO[:], sq[:, u % 2, 0], start=True, stop=True)
                    t.matmul(ps_n[:, 1], BO[:], sq[:, u % 2, 1], start=True, stop=True).then_inc(s["summed"].sem, 1)
    ph.close()


def route(nc, primer, n, idx, masks, bo32, av32, ident, small, zt, ct, x1d, x2):
    first, last = n == 0, n == ROUTINGS
    d = n % 2
    at = (lambda c: c) if d == 0 else (lambda c: c * -1 + (NCH - 1))
    way = slice(None) if d == 0 else slice(None, None, -1)
    end = slice(CH - 1, CH) if d == 0 else slice(0, 1)
    ph = Phase(nc, f"rt{n}", primer)
    BO = ph.sb("bo", [P, P]); AV = ph.sb("av", [P, P]); I = ph.sb("i", [P, P]); sm = ph.sb("sm", [P, 4])
    none = ph.sb("none", [P, 1])
    mk = ph.sb("mk", [P, U, 2, CH], BF16)
    a1, whole, rn, cn = (ph.sb(s, [P, U, CH]) for s in "a1 whole rn cn".split())
    if last:
        xd, y, x2r = (ph.sb(s, [P, U, K, D]) for s in "xd y x2r".split())
        st = ph.sb("st", [P, U, K, 6]); mv = ph.sb("mv", [P, U, K, 2]); lnv = ph.sb("lnv", [P, U, K]); rstd = ph.sb("rstd", [P, U, K])
        rr = Rows(ph, nc, idx, "rows", 1, bufs=U)
        scattered = ph.dma("scattered", each=K, primed_by="pool", bufs=U)
    else:
        mk2 = ph.sb("mk2", [P, U, 2, CH], BF16)
        z, pe_, pm, t2, ws = (ph.sb(s, [P, U, CH]) for s in "z pe pm t2 ws".split())
    ps_n = ph.ps("n", [P, 2, CH]); ps_p = ph.ps("p", [P, 2, CH]); ps_d = ph.ps("d", [P, 2, CH])
    consts, vinit, passed = (ph.sem(s) for s in ("consts", "vinit", "passed"))
    masked = ph.dma("masked", bufs=U)
    loaded = ph.dma("loaded", bufs=U)
    masked2 = ph.dma("masked2", bufs=U)
    stored = ph.dma("stored", primed_by="sp", bufs=U)
    names = ("started spread squared summed clamped logged inverted centred" +
             (" turned added measured meaned n_logged scaled x2_made" if last else
              " multiplied scored exped totalled lsummed shifted p_made kept weighted added scanned saved")).split()
    s = {n: ph.step(n) for n in names}
    START, SPREAD, SQ, CLAMP, ROOT, CN = 1, 2, 3, 4, 5, 6
    LOAD, SHIFT, WS, SCAN = (5 if last else 4), 7, 8, 9
    Y, RSTD, X2, STORE = 7, 8, 9, 10
    SAVE = DEPTH = STORE
    with nc.Block() as block:
        @block.sync
        def _(sp):
            ph.prime(sp, "sp")
            for a, b in ((BO[:], bo32), (AV[:], av32), (I[:], ident), (sm[:], small)):
                sp.dma_start(a, b).then_inc(consts, 16)
            for tick in ticks(sp, NCH, DEPTH):
                for c, i, u in tick.at(0):
                    if not first:
                        s["spread"].wait(sp, c, back=U)
                        sp.dma_start(mk[:, u], mask_rows(masks, d, 0, 2, at(c))).then_inc(masked.sems[u], 16)
                for c, i, u in tick.at(LOAD):
                    if last:
                        s["added"].wait(sp, c, back=U)
                        sp.dma_start(xd[:, u], x1d[at(c)]).then_inc(loaded.sems[u], 16)
                    else:
                        s["weighted"].wait(sp, c, back=U)
                        sp.dma_start(z[:, u], zt[at(c)]).then_inc(loaded.sems[u], 16)
                for c, i, u in tick.at(LOAD + 1):
                    if not last:
                        s["scanned"].wait(sp, c, back=U)
                        sp.dma_start(mk2[:, u], mask_rows(masks, d, 0, 2, at(c))).then_inc(masked2.sems[u], 16)
                for c, i, u in tick.at(STORE):
                    if last:
                        s["x2_made"].wait(sp, c)
                        sp.dma_start(x1d[at(c)], x2r[:, u]).then_inc(stored.sems[u], 16)
            if last:
                stored.wait_all(sp, NCH)

        @block.gpsimd
        def _(pool):
            g = nc.gpsimd
            ph.prime(pool, "pool")
            for tick in ticks(pool, NCH, DEPTH):
                for c, i, u in tick.at(START):
                    if not first:
                        masked.wait(pool, i, u)
                        s["summed"].wait(pool, c, back=U)
                        g.tensor_tensor(a1[:, u], mk[:, u, 1], ct[:, at(c)], ALU.mult).then_inc(s["started"].sem, 1)
                for c, i, u in tick.at(SHIFT):
                    if not last:
                        masked2.wait(pool, i, u)
                        if not first:
                            s["centred"].wait(pool, c)
                        s["added"].wait(pool, c, back=U)
                        g.tensor_tensor(t2[:, u], mk2[:, u, 1], ct[:, at(c)] if first else cn[:, u], ALU.mult).then_inc(s["kept"].sem, 1)
                for c, i, u in tick.at(WS):
                    if not last:
                        s["p_made"].wait(pool, c)
                        s["saved"].wait(pool, c, back=U)
                        s["scanned"].wait(pool, c, back=U - 1)
                        g.tensor_tensor(ws[:, u], z[:, u], pm[:, u], ALU.mult).then_inc(s["weighted"].sem, 1)
                        s["weighted"].wait(pool, c)
                        g.tensor_tensor(ws[:, u], ws[:, u], t2[:, u], ALU.add).then_inc(s["added"].sem, 1)
                for c, i, u in tick.at(STORE):
                    if last:
                        scattered.wait_before(pool, i, u)
                        s["x2_made"].wait(pool, c)
                        rr.stage(pool, c, c, u, (FIRST,))
                        rr.scatter(u, 0, x2r[:, u], x2, scattered.sems[u])
            if last:
                scattered.wait_all(pool, NCH)

        @block.vector
        def _(dve):
            v = nc.vector

            def carry(arr, u, c):
                return none[:] if isinstance(c, int) and c == 0 else arr[:, (u - 1) % U, end]

            v.memset(none[:], 0.0).then_inc(vinit, 1)
            dve.wait_ge(vinit, 1)
            for tick in ticks(dve, NCH, DEPTH):
                for c, i, u in tick.at(CN):
                    if not first:
                        s["inverted"].wait(dve, c)
                        s["turned" if last else "kept"].wait(dve, c, back=U)
                        v.tensor_tensor(cn[:, u], whole[:, u], rn[:, u], ALU.mult).then_inc(s["centred"].sem, 1)
                for c, i, u in tick.at(X2):
                    if last:
                        s["scaled"].wait(dve, c)
                        scattered.wait_before(dve, i, u)
                        stored.wait_before(dve, i, u)
                        row_scale(nc, x2r[:, u], y[:, u], mv[:, u], rstd[:, u]).then_inc(s["x2_made"].sem, 1)
                for c, i, u in tick.at(SPREAD):
                    if not first:
                        s["started"].wait(dve, c)
                        s["spread"].wait(dve, c, back=1)
                        s["centred"].wait(dve, c, back=U)
                        s["squared"].wait(dve, c, back=U)
                        v.tensor_tensor_scan(out=whole[:, u, way], data0=mk[:, u, 0, way], data1=a1[:, u, way],
                                             initial=carry(whole, u, c), op0=ALU.mult, op1=ALU.add).then_inc(s["spread"].sem, 1)
                for c, i, u in tick.at(CN):
                    if not last:
                        loaded.wait(dve, i, u)
                        if not first:
                            s["centred"].wait(dve, c)
                        s["totalled"].wait(dve, c, back=U)
                        v.tensor_tensor(pe_[:, u], z[:, u], ct[:, at(c)] if first else cn[:, u], ALU.mult).then_inc(s["multiplied"].sem, 1)
                for c, i, u in tick.at(CLAMP):
                    if not first:
                        s["summed"].wait(dve, c)
                        s["centred"].wait(dve, c, back=U)
                        v.tensor_scalar(rn[:, u], ps_n[:, u % 2], 1e-24, None, ALU.max).then_inc(s["clamped"].sem, 1)
                for c, i, u in tick.at(SHIFT):
                    if not last:
                        s["lsummed"].wait(dve, c)
                        v.tensor_tensor(pm[:, u], ps_p[:, u % 2], pm[:, u], ALU.subtract).then_inc(s["shifted"].sem, 1)
                for c, i, u in tick.at(SCAN):
                    if not last:
                        s["added"].wait(dve, c)
                        s["scanned"].wait(dve, c, back=1)
                        v.tensor_tensor_scan(out=ws[:, u, way], data0=mk2[:, u, 0, way], data1=ws[:, u, way],
                                             initial=carry(ws, u, c), op0=ALU.mult, op1=ALU.add).then_inc(s["scanned"].sem, 1)
                for c, i, u in tick.at(Y):
                    if last:
                        s["turned"].wait(dve, c)
                        loaded.wait(dve, i, u)
                        s["x2_made"].wait(dve, c, back=U)
                        v.tensor_tensor(y[:, u].rearrange("p k d -> p (k d)"), ps_p[:, u % 2],
                                        xd[:, u].rearrange("p k d -> p (k d)"), ALU.add).then_inc(s["added"].sem, 1)
                        s["added"].wait(dve, c)
                        row_stats(nc, y[:, u], st[:, u]).then_inc(s["measured"].sem, 1)
                        s["measured"].wait(dve, c)
                        dve.sem_inc(passed, 1)
                        row_moments(nc, st[:, u], mv[:, u]).then_inc(s["meaned"].sem, 1)

        @block.scalar
        def _(act):
            a = nc.scalar
            a.preload_act_table_set("natural_log_exp_and_others")
            act.wait_ge(consts, 64)
            for tick in ticks(act, NCH, DEPTH):
                for c, i, u in tick.at(SQ):
                    if not first:
                        s["spread"].wait(act, c)
                        a.activation(a1[:, u], whole[:, u], ACT.Square).then_inc(s["squared"].sem, 1)
                for c, i, u in tick.at(WS):
                    if not last:
                        s["shifted"].wait(act, c)
                        a.activation(pm[:, u], pm[:, u], ACT.Exp).then_inc(s["p_made"].sem, 1)
                for c, i, u in tick.at(ROOT):
                    if not first:
                        s["clamped"].wait(act, c)
                        a.activation(rn[:, u], rn[:, u], ACT.Ln, scale=2.0 ** 20).then_inc(s["logged"].sem, 1)
                for c, i, u in tick.at(SHIFT):
                    if not last:
                        s["totalled"].wait(act, c)
                        s["weighted"].wait(act, c, back=U)
                        a.activation(pm[:, u], ps_d[:, u % 2], ACT.Ln).then_inc(s["lsummed"].sem, 1)
                for c, i, u in tick.at(ROOT):
                    if not first:
                        s["logged"].wait(act, c)
                        a.activation(rn[:, u], rn[:, u], ACT.Exp, scale=-0.5, bias=sm[:, 1:2]).then_inc(s["inverted"].sem, 1)
                for c, i, u in tick.at(CN):
                    if not last:
                        s["scored"].wait(act, c)
                        a.activation(pe_[:, u], ps_p[:, u % 2], ACT.Exp).then_inc(s["exped"].sem, 1)
                for c, i, u in tick.at(SAVE):
                    if not last:
                        s["scanned"].wait(act, c)
                        a.copy(ct[:, at(c)], ws[:, u]).then_inc(s["saved"].sem, 1)
                for c, i, u in tick.at(RSTD):
                    if last:
                        s["meaned"].wait(act, c)
                        a.activation(lnv[:, u], mv[:, u, :, 1], ACT.Ln, bias=sm[:, 0:1]).then_inc(s["n_logged"].sem, 1)
                        s["n_logged"].wait(act, c)
                        s["x2_made"].wait(act, c, back=U)
                        a.activation(rstd[:, u], lnv[:, u], ACT.Exp, scale=-0.5).then_inc(s["scaled"].sem, 1)

        @block.tensor
        def _(pe):
            t = nc.tensor
            pe.wait_ge(consts, 64)
            for tick in ticks(pe, NCH, DEPTH):
                for c, i, u in tick.at(SHIFT):
                    if not last:
                        s["exped"].wait(pe, c)
                        s["lsummed"].wait(pe, c, back=2)
                        t.matmul(ps_d[:, u % 2], AV[:], pe_[:, u], start=True, stop=True).then_inc(s["totalled"].sem, 1)
                for c, i, u in tick.at(SQ):
                    if not first:
                        s["squared"].wait(pe, c)
                        s["clamped"].wait(pe, c, back=2)
                        t.matmul(ps_n[:, u % 2], BO[:], a1[:, u], start=True, stop=True).then_inc(s["summed"].sem, 1)
                for c, i, u in tick.at(CN):
                    if last:
                        s["centred"].wait(pe, c)
                        s["added"].wait(pe, c, back=2)
                        for k in range(K):
                            done = t.transpose(ps_p[:, u % 2, k * P:(k + 1) * P], cn[:, u, k * P:(k + 1) * P], I[:])
                        done.then_inc(s["turned"].sem, 1)
                    else:
                        s["multiplied"].wait(pe, c)
                        s["shifted"].wait(pe, c, back=2)
                        t.matmul(ps_p[:, u % 2], BO[:], pe_[:, u], start=True, stop=True).then_inc(s["scored"].sem, 1)
    ph.close()


def edge_means(nc, primer, x2, idx, src_col, masks, src_row, a, ident, x2d, ain, aout):
    ph = Phase(nc, "m", primer)
    WI = ph.sb("wi", [P, D]); WO = ph.sb("wo", [P, D]); I = ph.sb("i", [P, P]); bi = ph.sb("bi", [P, 1]); BOU = ph.sb("bou", [P, D])
    TRI = ph.sb("tri", [P, P]); sm = ph.sb("sm", [P, 4]); one = ph.sb("one", [P, CH]); none = ph.sb("none", [P, 1])
    rows, xd, mean = (ph.sb(n, [P, U, K, D]) for n in "rows xd mean".split())
    mk = ph.sb("mk", [P, U, CH], BF16)
    srow = ph.sb("srow", [P, U, K, P]); scol = ph.sb("scol", [P, U, K])
    xt = ph.sb("xt", [P, U, 2, CH]); fin = ph.sb("fin", [P, U, CH]); run = ph.sb("run", [P, U, 2, CH])
    rc = ph.sb("rc", [P, U, K]); fo = ph.sb("fo", [P, U, K, AW]); tot = ph.sb("tot", [P, U, K, AW])
    same = ph.sb("same", [P, U, K, P]); later = ph.sb("later", [P, K, P]); nl = ph.sb("nl", [P, U, K]); to = ph.sb("to", [P, U, K], I32)
    ps_x = ph.ps("x", [P, 2, CH]); ps_f = ph.ps("f", [P, CH]); ps_r = ph.ps("r", [P, CH]); ps_o = ph.ps("o", [P, K, D])
    ps_c = ph.ps("c", [P, K]); ps_t = ph.ps("t", [P, K, 256])
    rr = Rows(ph, nc, idx, "rows", 1, bufs=U)
    means = Rows(ph, nc, idx, "means", 1, bufs=U)
    consts, vinit, passed, serial = (ph.sem(n) for n in ("consts", "vinit", "passed", "serial"))
    gathered = ph.dma("gathered", each=K, bufs=U)
    loaded = ph.dma("loaded", each=2, bufs=U)
    masked = ph.dma("masked", bufs=U)
    scattered = ph.dma("scattered", each=K, primed_by="pool", bufs=U)
    names = ("turned moved moved_v made biased fo_made scanned run_turned counted inverted mean_made fo_biased compared "
             "masked_later found ranked listed summed copied accumulated staged").split()
    s = {n: ph.step(n) for n in names}
    TURN, CMP, F, FIN, LIST, SCAN, TOT, RUN, COPY, MEAN, ACC, SCAT = 2, 2, 3, 4, 4, 5, 5, 6, 6, 7, 7, 8
    DEPTH = SCAT
    with nc.Block() as block:
        @block.sync
        def _(sp):
            ph.prime(sp, "sp")
            for p, q in ((WI[:], a["w_in_t"]), (WO[:], a["w_out_t"]), (I[:], ident), (bi[:], a["b_in"][:, None]),
                         (BOU[:], spread(a["b_out"])), (TRI[:], a["tri"]), (sm[:], a["small"])):
                sp.dma_start(p, q).then_inc(consts, 16)
            for tick in ticks(sp, NCH, DEPTH):
                for c, i, u in tick.at(0):
                    s["turned"].wait(sp, c, back=U)
                    s["compared"].wait(sp, c, back=U)
                    sp.dma_start(xd[:, u], x2d[c]).then_inc(loaded.sems[u], 16)
                    sp.dma_start(srow[:, u].rearrange("p k e -> p (k e)"), spread(src_row[bass.ds(c * CH, CH)])).then_inc(loaded.sems[u], 16)
                for c, i, u in tick.at(FIN):
                    s["scanned"].wait(sp, c, back=U)
                    sp.dma_start(mk[:, u:u + 1], mask_rows(masks, 0, 0, 1, c)).then_inc(masked.sems[u], 16)

        @block.gpsimd
        def _(pool):
            g = nc.gpsimd
            ph.prime(pool, "pool")
            for tick in ticks(pool, NCH, DEPTH):
                for c, i, u in tick.at(0):
                    s["turned"].wait(pool, c, back=U)
                    s["ranked"].wait(pool, c, back=U)
                    g.tensor_copy(scol[:, u], src_col[:, bass.ds(c * K, K)]).then_inc(s["staged"].sem, 1)
                    rr.stage(pool, c, c, u, (SRC,))
                for c, i, u in tick.at(SCAT):
                    scattered.wait_before(pool, i, u)
                    s["mean_made"].wait(pool, c)
                    means.stage(pool, c, c, u, (LAST,))
                for k in range(K):
                    if k == 0:
                        for c, i, u in tick.at(ACC + 1):
                            pool.wait_ge(serial, c * (16 * K) + 16 * K)
                            pool.sem_inc(s["accumulated"].sem, 1)
                    for c, i, u in tick.at(ACC):
                        if k == 0:
                            s["copied"].wait(pool, c)
                            s["listed"].wait(pool, c)
                        else:
                            pool.wait_ge(serial, c * (16 * K) + 16 * k)
                        pool.sem_inc(passed, 1)
                        g.indirect_dma_start(aout, bass.IndirectOffsetOnAxis(ap=to[:, u, k:k + 1], axis=0), tot[:, u, k], None,
                                             compute_op=ALU.add).then_inc(serial, 16)
                    for c, i, u in tick.at(0):
                        rr.gather(u, 0, rows[:, u], x2, gathered.sems[u], tiles=(k,))
                    for c, i, u in tick.at(SCAT):
                        means.scatter(u, 0, mean[:, u], ain, scattered.sems[u], tiles=(k,))
            scattered.wait_all(pool, NCH)

        @block.vector
        def _(dve):
            v = nc.vector
            v.memset(one[:], 1.0).then_inc(vinit, 1)
            v.memset(none[:], 0.0).then_inc(vinit, 1)
            v.memset(fo[:, :, :, D:AW], 1.0).then_inc(vinit, 1)
            dve.wait_ge(vinit, 3)
            dve.wait_ge(consts, 16 * 7)
            for tick in ticks(dve, NCH, DEPTH):
                for c, i, u in tick.at(FIN):
                    s["fo_made"].wait(dve, c)
                    s["summed"].wait(dve, c, back=U)
                    v.tensor_tensor(fo[:, u, :, 0:D], ps_o[:], BOU[:, None, :].to_broadcast([P, K, D]), ALU.add).then_inc(s["fo_biased"].sem, 1)
                for c, i, u in tick.at(SCAN):
                    s["biased"].wait(dve, c)
                    masked.wait(dve, i, u)
                    s["run_turned"].wait(dve, c, back=U)
                    s["scanned"].wait(dve, c, back=1)
                    for j, terms in enumerate((fin[:, u], one[:])):
                        done = v.tensor_tensor_scan(out=run[:, u, j], data0=mk[:, u], data1=terms,
                                                    initial=none[:] if isinstance(c, int) and c == 0 else run[:, (u - 1) % U, j, CH - 1:CH],
                                                    op0=ALU.mult, op1=ALU.add)
                    done.then_inc(s["scanned"].sem, 1)
                for c, i, u in tick.at(MEAN):
                    s["run_turned"].wait(dve, c)
                    s["mean_made"].wait(dve, c, back=U)
                    v.tensor_copy(rc[:, u], ps_c[:]).then_inc(s["counted"].sem, 1)
                for c, i, u in tick.at(MEAN):
                    s["counted"].wait(dve, c)
                    v.reciprocal(rc[:, u], rc[:, u]).then_inc(s["inverted"].sem, 1)
                for c, i, u in tick.at(MEAN):
                    s["inverted"].wait(dve, c)
                    scattered.wait_before(dve, i, u)
                    v.tensor_tensor(mean[:, u], ps_r[:].rearrange("p (k d) -> p k d", k=K),
                                    rc[:, u][:, :, None].to_broadcast([P, K, D]), ALU.mult).then_inc(s["mean_made"].sem, 1)
                for c, i, u in tick.at(CMP):
                    loaded.wait(dve, i, u)
                    s["staged"].wait(dve, c)
                    s["summed"].wait(dve, c, back=U)
                    s["masked_later"].wait(dve, c, back=1)
                    for k in range(K):
                        done = v.tensor_scalar(same[:, u, k], srow[:, u, k], scol[:, u, k:k + 1], None, ALU.is_equal)
                    done.then_inc(s["compared"].sem, 1)
                for c, i, u in tick.at(TURN):
                    s["turned"].wait(dve, c)
                    s["fo_made"].wait(dve, c, back=U)
                    v.tensor_copy(xt[:, u, 1], ps_x[:, 1]).then_inc(s["moved_v"].sem, 1)
                for c, i, u in tick.at(LIST):
                    s["accumulated"].wait(dve, c, back=U)
                    s["ranked"].wait(dve, c)
                    v.tensor_scalar(to[:, u], nl[:, u], sm[:, 3:4], None, ALU.min).then_inc(s["listed"].sem, 1)
                for c, i, u in tick.at(CMP):
                    s["compared"].wait(dve, c)
                    s["found"].wait(dve, c, back=1)
                    v.tensor_tensor(later[:], same[:, u], TRI[:, None, :].to_broadcast([P, K, P]), ALU.mult).then_inc(s["masked_later"].sem, 1)
                    s["masked_later"].wait(dve, c)
                    s["listed"].wait(dve, c, back=U)
                    v.tensor_reduce(nl[:, u], later[:], AX, ALU.max).then_inc(s["found"].sem, 1)
                    s["found"].wait(dve, c)
                    v.scalar_tensor_tensor(nl[:, u], nl[:, u], sm[:, 3:4], scol[:, u], ALU.mult, ALU.max).then_inc(s["ranked"].sem, 1)

        @block.scalar
        def _(act):
            f = nc.scalar
            act.wait_ge(consts, 16 * 7)
            for tick in ticks(act, NCH, DEPTH):
                for c, i, u in tick.at(FIN):
                    s["made"].wait(act, c)
                    s["scanned"].wait(act, c, back=U)
                    f.activation(fin[:, u], ps_f[:], ACT.Identity, bias=bi[:]).then_inc(s["biased"].sem, 1)
                for c, i, u in tick.at(COPY):
                    s["summed"].wait(act, c)
                    s["accumulated"].wait(act, c, back=U)
                    f.copy(tot[:, u], ps_t[:, :, 0:AW]).then_inc(s["copied"].sem, 1)
                for c, i, u in tick.at(TURN):
                    s["turned"].wait(act, c)
                    s["made"].wait(act, c, back=U)
                    f.copy(xt[:, u, 0], ps_x[:, 0]).then_inc(s["moved"].sem, 1)

        @block.tensor
        def _(pe):
            t = nc.tensor
            pe.wait_ge(consts, 16 * 7)
            for tick in ticks(pe, NCH, DEPTH):
                for c, i, u in tick.at(RUN):
                    s["scanned"].wait(pe, c)
                    s["mean_made"].wait(pe, c, back=1)
                    for k in range(K):
                        t.transpose(ps_r[:, k * P:(k + 1) * P], run[:, u, 0, k * P:(k + 1) * P], I[:])
                    for k in range(K):
                        done = t.matmul(ps_c[:, k:k + 1], run[:, u, 1, k * P:(k + 1) * P], sm[:, 2:3], start=True, stop=True)
                    done.then_inc(s["run_turned"].sem, 1)
                for c, i, u in tick.at(TOT):
                    s["fo_biased"].wait(pe, c)
                    s["compared"].wait(pe, c)
                    s["copied"].wait(pe, c, back=1)
                    for k in range(K):
                        done = t.matmul(ps_t[:, k, 0:AW], same[:, u, k], fo[:, u, k], start=True, stop=True)
                    done.then_inc(s["summed"].sem, 1)
                for c, i, u in tick.at(F):
                    s["moved"].wait(pe, c)
                    s["biased"].wait(pe, c, back=1)
                    t.matmul(ps_f[:], WI[:], xt[:, u, 0], start=True, stop=True).then_inc(s["made"].sem, 1)
                    s["moved_v"].wait(pe, c)
                    s["fo_biased"].wait(pe, c, back=1)
                    for k in range(K):
                        done = t.matmul(ps_o[:, k], xt[:, u, 1, k * P:(k + 1) * P], WO[:], start=True, stop=True)
                    done.then_inc(s["fo_made"].sem, 1)
                for c, i, u in tick.at(TURN):
                    gathered.wait(pe, i, u)
                    loaded.wait(pe, i, u)
                    s["moved"].wait(pe, c, back=1)
                    s["moved_v"].wait(pe, c, back=1)
                    for j, src in enumerate((rows, xd)):
                        for k in range(K):
                            done = t.transpose(ps_x[:, j, k * P:(k + 1) * P], src[:, u, k], I[:])
                    done.then_inc(s["turned"].sem, 1)
    ph.close()


def dense_second(nc, primer, x2, ain, aout, x3, out, a, ident, small):
    ph = Phase(nc, "d2", primer)
    WIH = ph.sb("wih", [P, 2, 3 * D]); WHH = ph.sb("whh", [P, 3 * D]); W3 = ph.sb("w3", [P, D]); I = ph.sb("i", [P, P])
    bih = ph.sb("bih", [P, 3]); bhh = ph.sb("bhh", [P, 3]); brz = ph.sb("brz", [P, 2])
    B3 = ph.sb("b3", [P, D]); GA = ph.sb("ga", [P, D]); BE = ph.sb("be", [P, D]); half = ph.sb("half", [P, K])
    xin, ai, aon, yr, x3r, h, hn, w_, o = (ph.sb(n, [P, U, K, D]) for n in "xin ai aon yr x3r h hn w o".split())
    ao = ph.sb("ao", [P, U, K, AW]); rc = ph.sb("rc", [P, U, K])
    xt = ph.sb("xt", [P, U, 3, CH])
    rz = ph.sb("rz", [P, U, 2, CH])
    t_, n_, df, y, x3t = (ph.sb(n, [P, U, CH]) for n in "t n df y x3t".split())
    st = ph.sb("st", [P, U, 3, K, 6]); mv = ph.sb("mv", [P, U, 3, K, 2]); ve = ph.sb("ve", [P, U, 3, K]); rstd = ph.sb("rstd", [P, U, 3, K])
    ps_x = ph.ps("x", [P, 3, CH]); ps_g = ph.ps("g", [P, 4, CH]); ps_h = ph.ps("h", [P, K, D])
    consts, vinit, biases, passed = (ph.sem(s) for s in ("consts", "vinit", "biases", "passed"))
    loaded = ph.dma("loaded", each=3, bufs=U)
    stored3 = ph.dma("stored3", primed_by="sp", bufs=U)
    stored = ph.dma("stored", primed_by="sp", bufs=U)
    names = ("clamped counted averaged turned moved r_made z_made n_made r_gate z_gate reset gate_n tanhed differed weighed "
             "summed mixed y_turned y_moved x3_made x3_turned x3t_made h_made h_biased centred activated joined "
             "out_made measured0 meaned0 moved0 scaled0 measured1 meaned1 moved1 scaled1 measured2 meaned2 moved2 scaled2").split()
    s = {n: ph.step(n) for n in names}
    COUNT, AVG, TURN, GATE, TANH, MIX, Y, MEAN0, X3, MEAN1, HN, MEAN2, OUT, STORE = range(1, 15)
    DEPTH = STORE
    with nc.Block() as block:
        @block.sync
        def _(sp):
            ph.prime(sp, "sp")
            for p, q in ((WIH[:], a["w_ih_t"].rearrange("j d g -> d j g")), (WHH[:], a["w_hh_t"]), (W3[:], a["w3"][0]), (I[:], ident),
                         (B3[:], spread(a["b3"])), (GA[:], spread(a["gamma"])), (BE[:], spread(a["beta"]))):
                sp.dma_start(p, q).then_inc(consts, 16)
            with nc.allow_non_contiguous_dma(reason="biases to columns, once"):
                sp.dma_start(bih[:], a["b_ih"].rearrange("(g d) -> d g", g=3)).then_inc(consts, 16)
                sp.dma_start(bhh[:], a["b_hh"].rearrange("(g d) -> d g", g=3)).then_inc(consts, 16)
            for tick in ticks(sp, NG, DEPTH, peeled=1):
                for c, i, u in tick.at(0):
                    s["turned"].wait(sp, c, back=U)
                    s["averaged"].wait(sp, c, back=U)
                    sp.dma_start(xin[:, u], group_rows(x2, c)).then_inc(loaded.sems[u], 16)
                    sp.dma_start(ai[:, u], group_rows(ain, c)).then_inc(loaded.sems[u], 16)
                    sp.dma_start(ao[:, u], group_rows(aout, c)).then_inc(loaded.sems[u], 16)
                for c, i, u in tick.at(STORE):
                    if isinstance(c, int) and c == NG - 1:
                        stored.wait(sp, i, u - 1)
                    s["out_made"].wait(sp, c)
                    sp.dma_start(group_rows(out, c), o[:, u]).then_inc(stored.sems[u], 16)
                for c, i, u in tick.at(X3 + 1):
                    if isinstance(c, int) and c == NG - 1:
                        stored3.wait(sp, i, u - 1)
                    s["x3_made"].wait(sp, c)
                    sp.dma_start(group_rows(x3, c), x3r[:, u]).then_inc(stored3.sems[u], 16)
            stored3.wait_all(sp, NG)
            stored.wait_all(sp, NG)

        @block.gpsimd
        def _(pool):
            g = nc.gpsimd
            pool.wait_ge(consts, 16 * 9)
            g.memset(half[:], -0.5).then_inc(vinit, 1)
            pool.wait_ge(vinit, 1)
            for tick in ticks(pool, NG, DEPTH, peeled=1):
                for c, i, u in tick.at(MIX):
                    s["tanhed"].wait(pool, c)
                    s["mixed"].wait(pool, c, back=U)
                    g.tensor_tensor(df[:, u], xt[:, u, 0], n_[:, u], ALU.subtract).then_inc(s["differed"].sem, 1)
                for c, i, u in tick.at(AVG):
                    s["counted"].wait(pool, c)
                    s["turned"].wait(pool, c, back=U)
                    g.tensor_tensor(aon[:, u], ao[:, u, :, 0:D], rc[:, u][:, :, None].to_broadcast([P, K, D]), ALU.mult).then_inc(s["averaged"].sem, 1)
                for c, i, u in tick.at(MIX):
                    s["differed"].wait(pool, c)
                    g.tensor_tensor(df[:, u], df[:, u], rz[:, u, 1], ALU.mult).then_inc(s["weighed"].sem, 1)
                    s["y_turned"].wait(pool, c, back=U)
                    g.tensor_tensor(y[:, u], xt[:, u, 0], n_[:, u], ALU.add).then_inc(s["summed"].sem, 1)
                    s["weighed"].wait(pool, c)
                    s["summed"].wait(pool, c)
                    g.tensor_tensor(y[:, u], y[:, u], df[:, u], ALU.add).then_inc(s["mixed"].sem, 1)
                for j, delay in enumerate((MEAN0, MEAN1, MEAN2)):
                    for c, i, u in tick.at(delay):
                        s[f"moved{j}"].wait(pool, c)
                        s[("x3_made", "activated", "out_made")[j]].wait(pool, c, back=U)
                        g.tensor_tensor(rstd[:, u, j], ve[:, u, j], half[:], ALU.pow).then_inc(s[f"scaled{j}"].sem, 1)

        @block.vector
        def _(dve):
            v = nc.vector
            dve.wait_ge(consts, 16 * 9)
            v.tensor_tensor(brz[:], bih[:, 0:2], bhh[:, 0:2], ALU.add).then_inc(biases, 1)

            def stats(c, u, j, src):
                row_stats(nc, src, st[:, u, j]).then_inc(s[f"measured{j}"].sem, 1)

            def moments(c, u, j):
                s[f"measured{j}"].wait(dve, c)
                dve.sem_inc(passed, 1)
                row_moments(nc, st[:, u, j], mv[:, u, j]).then_inc(s[f"meaned{j}"].sem, 1)

            def variance(c, u, j):
                s[f"meaned{j}"].wait(dve, c)
                v.tensor_scalar(ve[:, u, j], mv[:, u, j, :, 1], LN_EPS, None, ALU.add).then_inc(s[f"moved{j}"].sem, 1)

            for tick in ticks(dve, NG, DEPTH, peeled=1):
                for c, i, u in tick.at(TANH):
                    s["n_made"].wait(dve, c)
                    s["r_gate"].wait(dve, c)
                    s["tanhed"].wait(dve, c, back=U)
                    v.scalar_tensor_tensor(t_[:, u], ps_g[:, 3], bhh[:, 2:3], rz[:, u, 0], ALU.add, ALU.mult).then_inc(s["reset"].sem, 1)
                for c, i, u in tick.at(X3):
                    s["scaled0"].wait(dve, c)
                    stored3.wait_before(dve, i, u)
                    s["x3_turned"].wait(dve, c, back=U)
                    s["joined"].wait(dve, c, back=U)
                    row_scale(nc, x3r[:, u], yr[:, u], mv[:, u, 0], rstd[:, u, 0]).then_inc(s["x3_made"].sem, 1)
                for c, i, u in tick.at(TANH):
                    s["reset"].wait(dve, c)
                    v.tensor_tensor(t_[:, u], t_[:, u], ps_g[:, 2], ALU.add).then_inc(s["gate_n"].sem, 1)
                for c, i, u in tick.at(HN):
                    s["scaled1"].wait(dve, c)
                    s["centred"].wait(dve, c)
                    s["out_made"].wait(dve, c, back=U)
                    for k in range(K):
                        done = v.scalar_tensor_tensor(w_[:, u, k], hn[:, u, k], rstd[:, u, 1, k:k + 1], BE[:], ALU.mult, ALU.add)
                    done.then_inc(s["activated"].sem, 1)
                for c, i, u in tick.at(OUT):
                    s["scaled2"].wait(dve, c)
                    stored.wait_before(dve, i, u)
                    row_scale(nc, o[:, u], w_[:, u], mv[:, u, 2], rstd[:, u, 2]).then_inc(s["out_made"].sem, 1)
                for c, i, u in tick.at(MEAN1):
                    s["h_made"].wait(dve, c)
                    s["centred"].wait(dve, c, back=U)
                    v.tensor_tensor(h[:, u], ps_h[:], B3[:, None, :].to_broadcast([P, K, D]), ALU.add).then_inc(s["h_biased"].sem, 1)
                for c, i, u in tick.at(MEAN0):
                    s["y_moved"].wait(dve, c)
                    stats(c, u, 0, yr[:, u])
                for c, i, u in tick.at(MEAN1):
                    s["h_biased"].wait(dve, c)
                    stats(c, u, 1, h[:, u])
                for c, i, u in tick.at(MEAN0):
                    moments(c, u, 0)
                for c, i, u in tick.at(MEAN2):
                    s["activated"].wait(dve, c)
                    v.scalar_tensor_tensor(w_[:, u], w_[:, u], 0.0, x3r[:, u], ALU.max, ALU.add).then_inc(s["joined"].sem, 1)
                for c, i, u in tick.at(MEAN1):
                    moments(c, u, 1)
                for c, i, u in tick.at(MEAN0):
                    variance(c, u, 0)
                for c, i, u in tick.at(MEAN2):
                    s["joined"].wait(dve, c)
                    stats(c, u, 2, w_[:, u])
                for c, i, u in tick.at(MEAN1):
                    s["meaned1"].wait(dve, c)
                    s["activated"].wait(dve, c, back=U)
                    for k in range(K):
                        done = v.scalar_tensor_tensor(hn[:, u, k], h[:, u, k], mv[:, u, 1, k, 0:1], GA[:], ALU.subtract, ALU.mult)
                    done.then_inc(s["centred"].sem, 1)
                for c, i, u in tick.at(MEAN1):
                    variance(c, u, 1)
                for c, i, u in tick.at(COUNT):
                    loaded.wait(dve, i, u)
                    s["averaged"].wait(dve, c, back=U)
                    v.tensor_scalar(rc[:, u], ao[:, u, :, D], 1.0, None, ALU.max).then_inc(s["clamped"].sem, 1)
                for c, i, u in tick.at(MEAN2):
                    moments(c, u, 2)
                for c, i, u in tick.at(COUNT):
                    s["clamped"].wait(dve, c)
                    v.reciprocal(rc[:, u], rc[:, u]).then_inc(s["counted"].sem, 1)
                for c, i, u in tick.at(MEAN2):
                    variance(c, u, 2)

        @block.scalar
        def _(act):
            f = nc.scalar
            f.preload_act_table_set("sigmoid_and_others")
            act.wait_ge(consts, 16 * 9)
            act.wait_ge(biases, 1)
            for tick in ticks(act, NG, DEPTH, peeled=1):
                for c, i, u in tick.at(TANH):
                    s["gate_n"].wait(act, c)
                    s["mixed"].wait(act, c, back=U)
                    f.activation(n_[:, u], t_[:, u], ACT.Tanh, bias=bih[:, 2:3]).then_inc(s["tanhed"].sem, 1)
                for c, i, u in tick.at(TURN):
                    s["turned"].wait(act, c)
                    s["n_made"].wait(act, c, back=U)
                    s["mixed"].wait(act, c, back=U)
                    f.copy(xt[:, u], ps_x[:]).then_inc(s["moved"].sem, 1)
                for c, i, u in tick.at(GATE):
                    s["r_made"].wait(act, c)
                    s["gate_n"].wait(act, c, back=U)
                    s["mixed"].wait(act, c, back=U)
                    f.activation(rz[:, u, 0], ps_g[:, 0], ACT.Sigmoid, bias=brz[:, 0:1]).then_inc(s["r_gate"].sem, 1)
                    s["z_made"].wait(act, c)
                    f.activation(rz[:, u, 1], ps_g[:, 1], ACT.Sigmoid, bias=brz[:, 1:2]).then_inc(s["z_gate"].sem, 1)
                for c, i, u in tick.at(Y):
                    s["y_turned"].wait(act, c)
                    s["x3_made"].wait(act, c, back=U)
                    f.copy(yr[:, u], ps_x[:, 0].rearrange("p (k d) -> p k d", k=K)).then_inc(s["y_moved"].sem, 1)
                for c, i, u in tick.at(X3):
                    s["x3_turned"].wait(act, c)
                    s["h_made"].wait(act, c, back=U)
                    f.copy(x3t[:, u], ps_x[:, 1]).then_inc(s["x3t_made"].sem, 1)

        @block.tensor
        def _(pe):
            t = nc.tensor
            pe.wait_ge(consts, 16 * 9)
            for tick in ticks(pe, NG, DEPTH, peeled=1):
                for c, i, u in tick.at(TURN):
                    loaded.wait(pe, i, u)
                    s["averaged"].wait(pe, c)
                    s["moved"].wait(pe, c, back=1)
                    wait_other(s["y_moved"], pe, c, TURN - Y - 1, NG)
                    wait_other(s["x3t_made"], pe, c, TURN - X3 - 1, NG)
                    for j, src in enumerate((xin, ai, aon)):
                        for k in range(K):
                            done = t.transpose(ps_x[:, j, k * P:(k + 1) * P], src[:, u, k], I[:])
                    done.then_inc(s["turned"].sem, 1)
                for c, i, u in tick.at(GATE):
                    s["moved"].wait(pe, c)
                    for gate, (made, read) in enumerate((("r_made", "r_gate"), ("z_made", "z_gate"))):
                        cols = slice(gate * D, (gate + 1) * D)
                        s[read].wait(pe, c, back=1)
                        t.matmul(ps_g[:, gate], WHH[:, cols], xt[:, u, 0], start=True, stop=False)
                        t.matmul(ps_g[:, gate], WIH[:, 0, cols], xt[:, u, 1], start=False, stop=False)
                        t.matmul(ps_g[:, gate], WIH[:, 1, cols], xt[:, u, 2], start=False, stop=True).then_inc(s[made].sem, 1)
                for c, i, u in tick.at(Y):
                    s["mixed"].wait(pe, c)
                    wait_other(s["moved"], pe, c, Y - TURN, NG)
                    for k in range(K):
                        done = t.transpose(ps_x[:, 0, k * P:(k + 1) * P], y[:, u, k * P:(k + 1) * P], I[:])
                    done.then_inc(s["y_turned"].sem, 1)
                for c, i, u in tick.at(X3):
                    s["x3_made"].wait(pe, c)
                    wait_other(s["moved"], pe, c, X3 - TURN, NG)
                    for k in range(K):
                        done = t.transpose(ps_x[:, 1, k * P:(k + 1) * P], x3r[:, u, k], I[:])
                    done.then_inc(s["x3_turned"].sem, 1)
                for c, i, u in tick.at(GATE):
                    s["gate_n"].wait(pe, c, back=1)
                    t.matmul(ps_g[:, 3], WHH[:, 2 * D:], xt[:, u, 0], start=True, stop=True)
                    t.matmul(ps_g[:, 2], WIH[:, 0, 2 * D:], xt[:, u, 1], start=True, stop=False)
                    t.matmul(ps_g[:, 2], WIH[:, 1, 2 * D:], xt[:, u, 2], start=False, stop=True).then_inc(s["n_made"].sem, 1)
                for c, i, u in tick.at(X3):
                    s["x3t_made"].wait(pe, c)
                    s["h_biased"].wait(pe, c, back=1)
                    for k in range(K):
                        done = t.matmul(ps_h[:, k], x3t[:, u, k * P:(k + 1) * P], W3[:], start=True, stop=True)
                    done.then_inc(s["h_made"].sem, 1)
    ph.close()


def lse_forward(nc, primer, x3, idx, masks, ident, xm):
    ph = Phase(nc, "l0", primer)
    I = ph.sb("i", [P, P]); rows = ph.sb("rows", [P, U, K, D]); mk = ph.sb("mk", [P, U, 1, CH], BF16); o = ph.sb("o", [P, U, 2, CH])
    none = ph.sb("none", [P, 1])
    ps_x = ph.ps("x", [P, 2, CH])
    rr = Rows(ph, nc, idx, "rows", 1, bufs=U)
    consts, vinit = (ph.sem(s) for s in ("consts", "vinit"))
    gathered = ph.dma("gathered", each=K, bufs=U)
    masked = ph.dma("masked", bufs=U)
    stored = ph.dma("stored", primed_by="sp", bufs=U)
    turned, moved, scanned = (ph.step(s) for s in ("turned", "moved", "scanned"))
    TURN, SCAN, STORE = 2, 3, 4
    DEPTH = STORE
    with nc.Block() as block:
        @block.sync
        def _(sp):
            ph.prime(sp, "sp")
            sp.dma_start(I[:], ident).then_inc(consts, 16)
            for tick in ticks(sp, NCH, DEPTH):
                for c, i, u in tick.at(STORE):
                    scanned.wait(sp, c)
                    sp.dma_start(xm[c], o[:, u]).then_inc(stored.sems[u], 16)
                for c, i, u in tick.at(TURN):
                    scanned.wait(sp, c, back=U)
                    sp.dma_start(mk[:, u], mask_rows(masks, 0, 2, 1, c)).then_inc(masked.sems[u], 16)
            stored.wait_all(sp, NCH)

        @block.gpsimd
        def _(pool):
            for tick in ticks(pool, NCH, DEPTH):
                for c, i, u in tick.at(0):
                    turned.wait(pool, c, back=U)
                    rr.stage(pool, c, c, u, (SRC,))
                    rr.gather(u, 0, rows[:, u], x3, gathered.sems[u])

        @block.vector
        def _(dve):
            v = nc.vector
            v.memset(none[:], 0.0).then_inc(vinit, 1)
            dve.wait_ge(vinit, 1)
            for tick in ticks(dve, NCH, DEPTH):
                for c, i, u in tick.at(SCAN):
                    moved.wait(dve, c)
                    masked.wait(dve, i, u)
                    stored.wait_before(dve, i, u)
                    scanned.wait(dve, c, back=1)
                    v.tensor_tensor_scan(out=o[:, u, 1], data0=mk[:, u, 0], data1=o[:, u, 0],
                                         initial=none[:] if isinstance(c, int) and c == 0 else o[:, (u - 1) % U, 1, CH - 1:CH],
                                         op0=ALU.add, op1=ALU.max).then_inc(scanned.sem, 1)

        @block.scalar
        def _(act):
            for tick in ticks(act, NCH, DEPTH):
                for c, i, u in tick.at(TURN):
                    turned.wait(act, c)
                    stored.wait_before(act, i, u)
                    nc.scalar.copy(o[:, u, 0], ps_x[:, u % 2]).then_inc(moved.sem, 1)

        @block.tensor
        def _(pe):
            pe.wait_ge(consts, 16)
            for tick in ticks(pe, NCH, DEPTH):
                for c, i, u in tick.at(TURN):
                    gathered.wait(pe, i, u)
                    moved.wait(pe, c, back=2)
                    for k in range(K):
                        done = nc.tensor.transpose(ps_x[:, u % 2, k * P:(k + 1) * P], rows[:, u, k], I[:])
                    done.then_inc(turned.sem, 1)
    ph.close()


def lse_backward(nc, primer, x3, idx, masks, a, ident, small, xm, out):
    ph = Phase(nc, "l1", primer)
    W3 = ph.sb("w3", [P, 2, D]); I = ph.sb("i", [P, P]); sm = ph.sb("sm", [P, 4]); none = ph.sb("none", [P, 1])
    B3 = ph.sb("b3", [P, D]); GA = ph.sb("ga", [P, D]); BE = ph.sb("be", [P, D])
    xs = ph.sb("xs", [P, U, 2, CH]); mk = ph.sb("mk", [P, U, 2, CH], BF16); mk2 = ph.sb("mk2", [P, U, 1, CH], BF16)
    rows, own, h, hn, w_, o = (ph.sb(n, [P, U, K, D]) for n in "rows own h hn w o".split())
    t1, mx, ex, sums, cl, xt = (ph.sb(n, [P, U, CH]) for n in "t1 mx ex sums cl xt".split())
    st = ph.sb("st", [P, U, 2, K, 6]); mv = ph.sb("mv", [P, U, 2, K, 2]); lnv = ph.sb("lnv", [P, U, 2, K]); rstd = ph.sb("rstd", [P, U, 2, K])
    ps_x = ph.ps("x", [P, 2, CH]); ps_h = ph.ps("h", [P, 2, K, D])
    rr = Rows(ph, nc, idx, "rows", 1, bufs=U)
    outs = Rows(ph, nc, idx, "outs", 1, bufs=U)
    consts, vinit, passed = (ph.sem(s) for s in ("consts", "vinit", "passed"))
    gathered = ph.dma("gathered", each=K, bufs=U)
    loaded = ph.dma("loaded", each=2, bufs=U)
    masked2 = ph.dma("masked2", bufs=U)
    scattered = ph.dma("scattered", each=K, primed_by="pool", bufs=U)
    names = ("started spread shifted exped scanned clamped logged turned moved kept h_made h_biased measured0 meaned0 "
             "v_logged0 scaled0 centred activated joined measured1 meaned1 v_logged1 scaled1 out_made").split()
    s = {n: ph.step(n) for n in names}
    back = lambda c: c * -1 + (NCH - 1)
    START, SPREAD, EXP, GATHER, SCAN, LOG, TURN, H, NORM0, RSTD0, NORM1, RSTD1, OUT, SCAT = 1, 2, 3, 3, 4, 5, 5, 6, 7, 8, 9, 10, 11, 12
    DEPTH = SCAT
    with nc.Block() as block:
        @block.sync
        def _(sp):
            ph.prime(sp, "sp")
            for p, q in ((W3[:], a["w3"].rearrange("j d e -> d j e")), (I[:], ident), (sm[:], small), (B3[:], spread(a["b3"])),
                         (GA[:], spread(a["gamma"])), (BE[:], spread(a["beta"]))):
                sp.dma_start(p, q).then_inc(consts, 16)
            for tick in ticks(sp, NCH, DEPTH):
                for c, i, u in tick.at(EXP):
                    s["scanned"].wait(sp, c, back=U)
                    sp.dma_start(mk2[:, u], mask_rows(masks, 1, 0, 1, back(c))).then_inc(masked2.sems[u], 16)
                for c, i, u in tick.at(0):
                    s["spread"].wait(sp, c, back=U)
                    s["exped"].wait(sp, c, back=U)
                    sp.dma_start(xs[:, u], xm[back(c)]).then_inc(loaded.sems[u], 16)
                    sp.dma_start(mk[:, u], mask_rows(masks, 1, 0, 2, back(c))).then_inc(loaded.sems[u], 16)

        @block.gpsimd
        def _(pool):
            g = nc.gpsimd
            ph.prime(pool, "pool")
            pool.wait_ge(consts, 96)
            for tick in ticks(pool, NCH, DEPTH):
                for c, i, u in tick.at(START):
                    loaded.wait(pool, i, u)
                    s["spread"].wait(pool, c, back=U)
                    g.tensor_tensor(t1[:, u], mk[:, u, 1], xs[:, u, 1], ALU.mult).then_inc(s["started"].sem, 1)
                for c, i, u in tick.at(SCAT):
                    s["out_made"].wait(pool, c)
                    scattered.wait_before(pool, i, u)
                    outs.stage(pool, back(c), c, u, (FIRST,))
                    outs.scatter(u, 0, o[:, u], out, scattered.sems[u])
                for c, i, u in tick.at(GATHER):
                    s["turned"].wait(pool, c, back=U)
                    s["kept"].wait(pool, c, back=U)
                    rr.stage(pool, back(c), c, u, (DST,))
                    rr.gather(u, 0, rows[:, u], x3, gathered.sems[u])

        @block.vector
        def _(dve):
            v = nc.vector
            v.memset(none[:], 0.0).then_inc(vinit, 1)
            dve.wait_ge(vinit, 1)
            dve.wait_ge(consts, 96)

            def moments(c, u, j):
                s[f"measured{j}"].wait(dve, c)
                dve.sem_inc(passed, 1)
                row_moments(nc, st[:, u, j], mv[:, u, j]).then_inc(s[f"meaned{j}"].sem, 1)

            for tick in ticks(dve, NCH, DEPTH):
                for c, i, u in tick.at(OUT):
                    s["scaled1"].wait(dve, c)
                    scattered.wait_before(dve, i, u)
                    row_scale(nc, o[:, u], w_[:, u], mv[:, u, 1], rstd[:, u, 1]).then_inc(s["out_made"].sem, 1)
                for c, i, u in tick.at(NORM1):
                    s["scaled0"].wait(dve, c)
                    s["out_made"].wait(dve, c, back=U)
                    for k in range(K):
                        done = v.scalar_tensor_tensor(w_[:, u, k], hn[:, u, k], rstd[:, u, 0, k:k + 1], BE[:], ALU.mult, ALU.add)
                    done.then_inc(s["activated"].sem, 1)
                for c, i, u in tick.at(NORM0):
                    s["h_made"].wait(dve, c)
                    s["centred"].wait(dve, c, back=U)
                    v.tensor_tensor(h[:, u], ps_h[:, u % 2], B3[:, None, :].to_broadcast([P, K, D]), ALU.add).then_inc(s["h_biased"].sem, 1)
                for c, i, u in tick.at(NORM1):
                    s["activated"].wait(dve, c)
                    s["kept"].wait(dve, c)
                    v.scalar_tensor_tensor(w_[:, u], w_[:, u], 0.0, own[:, u], ALU.max, ALU.add).then_inc(s["joined"].sem, 1)
                for c, i, u in tick.at(NORM0):
                    s["h_biased"].wait(dve, c)
                    row_stats(nc, h[:, u], st[:, u, 0]).then_inc(s["measured0"].sem, 1)
                for c, i, u in tick.at(NORM1):
                    s["joined"].wait(dve, c)
                    row_stats(nc, w_[:, u], st[:, u, 1]).then_inc(s["measured1"].sem, 1)
                for c, i, u in tick.at(NORM0):
                    moments(c, u, 0)
                for c, i, u in tick.at(SPREAD):
                    s["started"].wait(dve, c)
                    s["spread"].wait(dve, c, back=1)
                    s["shifted"].wait(dve, c, back=U)
                    s["h_made"].wait(dve, c, back=U)
                    v.tensor_tensor_scan(out=mx[:, u, ::-1], data0=mk[:, u, 0, ::-1], data1=t1[:, u, ::-1],
                                         initial=none[:] if isinstance(c, int) and c == 0 else mx[:, (u - 1) % U, 0:1],
                                         op0=ALU.mult, op1=ALU.add).then_inc(s["spread"].sem, 1)
                for c, i, u in tick.at(NORM1):
                    moments(c, u, 1)
                for c, i, u in tick.at(NORM0):
                    s["meaned0"].wait(dve, c)
                    s["activated"].wait(dve, c, back=U)
                    for k in range(K):
                        done = v.scalar_tensor_tensor(hn[:, u, k], h[:, u, k], mv[:, u, 0, k, 0:1], GA[:], ALU.subtract, ALU.mult)
                    done.then_inc(s["centred"].sem, 1)
                for c, i, u in tick.at(SCAN):
                    s["exped"].wait(dve, c)
                    masked2.wait(dve, i, u)
                    s["scanned"].wait(dve, c, back=1)
                    s["clamped"].wait(dve, c, back=U)
                    v.tensor_tensor_scan(out=sums[:, u, ::-1], data0=mk2[:, u, 0, ::-1], data1=ex[:, u, ::-1],
                                         initial=none[:] if isinstance(c, int) and c == 0 else sums[:, (u - 1) % U, 0:1],
                                         op0=ALU.mult, op1=ALU.add).then_inc(s["scanned"].sem, 1)
                for c, i, u in tick.at(SPREAD):
                    s["spread"].wait(dve, c)
                    v.tensor_tensor(xs[:, u, 0], xs[:, u, 0], mx[:, u], ALU.subtract).then_inc(s["shifted"].sem, 1)
                for c, i, u in tick.at(SCAN):
                    s["scanned"].wait(dve, c)
                    s["h_made"].wait(dve, c, back=U)
                    v.tensor_scalar(cl[:, u], sums[:, u], 1e-30, None, ALU.max).then_inc(s["clamped"].sem, 1)

        @block.scalar
        def _(act):
            f = nc.scalar
            f.preload_act_table_set("natural_log_exp_and_others")
            act.wait_ge(consts, 96)
            for tick in ticks(act, NCH, DEPTH):
                for j, delay in enumerate((RSTD0, RSTD1)):
                    for c, i, u in tick.at(delay):
                        s[f"meaned{j}"].wait(act, c)
                        f.activation(lnv[:, u, j], mv[:, u, j, :, 1], ACT.Ln, bias=sm[:, 0:1]).then_inc(s[f"v_logged{j}"].sem, 1)
                for j, delay in enumerate((RSTD0, RSTD1)):
                    for c, i, u in tick.at(delay):
                        s[f"v_logged{j}"].wait(act, c)
                        s[("activated", "out_made")[j]].wait(act, c, back=U)
                        f.activation(rstd[:, u, j], lnv[:, u, j], ACT.Exp, scale=-0.5).then_inc(s[f"scaled{j}"].sem, 1)
                for c, i, u in tick.at(LOG):
                    s["clamped"].wait(act, c)
                    f.activation(cl[:, u], cl[:, u], ACT.Ln).then_inc(s["logged"].sem, 1)
                for c, i, u in tick.at(H):
                    s["moved"].wait(act, c)
                    s["joined"].wait(act, c, back=U)
                    f.copy(own[:, u], rows[:, u]).then_inc(s["kept"].sem, 1)
                for c, i, u in tick.at(EXP):
                    s["shifted"].wait(act, c)
                    s["scanned"].wait(act, c, back=U)
                    f.activation(ex[:, u], xs[:, u, 0], ACT.Exp).then_inc(s["exped"].sem, 1)
                for c, i, u in tick.at(TURN):
                    s["turned"].wait(act, c)
                    s["h_made"].wait(act, c, back=U)
                    f.copy(xt[:, u], ps_x[:, u % 2]).then_inc(s["moved"].sem, 1)

        @block.tensor
        def _(pe):
            t = nc.tensor
            pe.wait_ge(consts, 96)
            for tick in ticks(pe, NCH, DEPTH):
                for c, i, u in tick.at(H):
                    s["moved"].wait(pe, c)
                    s["logged"].wait(pe, c)
                    s["h_biased"].wait(pe, c, back=2)
                    for k in range(K):
                        t.matmul(ps_h[:, u % 2, k], xt[:, u, k * P:(k + 1) * P], W3[:, 0], start=True, stop=False)
                        t.matmul(ps_h[:, u % 2, k], mx[:, u, k * P:(k + 1) * P], W3[:, 1], start=False, stop=False)
                        done = t.matmul(ps_h[:, u % 2, k], cl[:, u, k * P:(k + 1) * P], W3[:, 1], start=False, stop=True)
                    done.then_inc(s["h_made"].sem, 1)
                for c, i, u in tick.at(TURN):
                    gathered.wait(pe, i, u)
                    s["moved"].wait(pe, c, back=2)
                    for k in range(K):
                        done = t.transpose(ps_x[:, u % 2, k * P:(k + 1) * P], rows[:, u, k], I[:])
                    done.then_inc(s["turned"].sem, 1)
    ph.close()


def gnn(nc, a, out, keep="Internal", stop=99):
    def dram(name, shape, dt=F32, kind="Internal"):
        return nc.dram_tensor(name, shape, dt, kind=kind).ap()

    primer = (dram("primer_out", (32, 64)), a["primer"])
    sorted_edges = [dram("edges0", (SLOTS, 2), I32), dram("edges1", (SLOTS, 2), I32)]
    masks, lists, src_row = dram("masks", (2, 3, SLOTS), BF16), dram("lists", (5, SLOTS), I32), dram("src_row", (SLOTS,))
    x1, x2, x3 = (dram(n, (N, D), F32, keep) for n in ("x1", "x2", "x3"))
    ain, aout = dram("ain", (N, D), F32, keep), dram("aout", (N + P, AW), F32, keep)
    l0t, rows0 = dram("l0t", (NCH, P, 2, CH)), dram("rows0", (NCH, P, K, D))
    zt = dram("zt", (NCH, P, CH))
    ident, small = a["ident"], a["small"]
    with nc.sbuf_tensor("idx", [P, 5, T], I32) as idx, nc.sbuf_tensor("src_col", [P, T], F32) as src_col:
        with nc.sbuf_tensor("unsorted", [P, 1], I32) as unsorted:
            sort_edges(nc, primer, a["src"], a["dst"], sorted_edges, a, unsorted)
        slot_tables(nc, primer, sorted_edges[0], masks, lists, src_row, idx, src_col)
        dense_first(nc, primer, a["x"], x1, x2, a["w1t"], a["bias0"], a["b1"], ident, small, [ain, aout])
        if stop < 1: return
        gat_forward(nc, primer, a["x"], idx, masks, a["w0"], a["w0t"], a["al"], a["ar"], a["bo16"], ident, zt, l0t, rows0)
        gat_backward(nc, primer, idx, masks, a["bias0"], a["sel8"], ident, small, zt, l0t, rows0, x1)
        if stop < 2: return
        with nc.sbuf_tensor("ct", [P, NCH, CH], F32) as ct:
            route_start(nc, primer, x1, idx, a["w1t"], a["b1"], a["bo32"], ident, small, zt, ct, rows0)
            for n in range(ROUTINGS + 1):
                route(nc, primer, n, idx, masks, a["bo32"], a["av32"], ident, small, zt, ct, rows0, x2)
        if stop < 3: return
        edge_means(nc, primer, x2, idx, src_col, masks, src_row, a, ident, rows0, ain, aout)
        if stop < 4: return
        dense_second(nc, primer, x2, ain, aout, x3, out, a, ident, small)
        if stop < 5: return
        lse_forward(nc, primer, x3, idx, masks, ident, l0t)
        lse_backward(nc, primer, x3, idx, masks, a, ident, small, l0t, out)


def constants():
    f = np.float32
    small = np.zeros((P, 4), f)
    small[:, 0] = LN_EPS
    small[:, 1] = 10 * np.log(2.0)
    small[:, 2] = 1.0 / P
    small[:, 3] = N + np.arange(P)
    i = np.arange(P)
    same32 = (i[:, None] // PER_GROUP == i[None] // PER_GROUP).astype(f)
    return {
        "primer": np.zeros((32, 64), f),
        "iota": np.tile(np.arange(64, dtype=f), (P, 1)),
        "tri": np.triu(np.ones((P, P), f), 1),
        "ones": np.ones((P, P), f),
        "padding": np.tile(np.array([N, 0], np.int32), (P, T, 1)),
        "ident": np.eye(P, dtype=f),
        "small": small,
        "bo16": (i[:, None] // PER_HEAD == i[None] // PER_HEAD).astype(f),
        "sel8": (i[:, None] == PER_HEAD * np.arange(HEADS)[None]).astype(f),
        "bo32": same32,
        "av32": np.full((P, P), 1.0 / PER_GROUP, f),
    }


def layout(v):
    c = np.ascontiguousarray
    return {
        "x": c(v["x"]), "src": c(v["src"]), "dst": c(v["dst"]),
        "w0": c(v["L0_gnn_W"]), "w0t": c(v["L0_gnn_W"].T),
        "al": c(v["L0_gnn_attn_l"].reshape(D, 1)), "ar": c(v["L0_gnn_attn_r"].reshape(D, 1)), "bias0": c(v["L0_gnn_bias"]),
        "w1t": c(v["L1_gnn_W"].T), "b1": c(v["L1_gnn_b"]),
        "w_in_t": c(v["L2_gnn_W_in"].T), "b_in": c(v["L2_gnn_b_in"]),
        "w_out_t": c(v["L2_gnn_W_out"].T), "b_out": c(v["L2_gnn_b_out"]),
        "w_ih_t": c(v["L2_gnn_w_ih"].T.reshape(2, D, 3 * D)), "w_hh_t": c(v["L2_gnn_w_hh"].T),
        "b_ih": c(v["L2_gnn_b_ih"]), "b_hh": c(v["L2_gnn_b_hh"]),
        "w3": c(v["L3_gnn_W"].reshape(2, D, D)), "b3": c(v["L3_gnn_b"]),
        "gamma": c(v["L3_gnn_gamma"]), "beta": c(v["L3_gnn_beta"]),
    }


def kernel(**inputs):
    import concourse.bacc as bacc
    from concourse.bass_utils import run_bass_kernel_spmd

    arrays = {**layout({k: np.asarray(v) for k, v in inputs.items()}), **constants()}
    nc = bacc.Bacc("TRN2", target_bir_lowering=False, num_devices=1)
    aps = {k: nc.dram_tensor(f"in_{k}", v.shape, mybir.dt.from_np(v.dtype), kind="ExternalInput").ap()
           for k, v in arrays.items()}
    out = nc.dram_tensor("out", (N, D), F32, kind="ExternalOutput").ap()
    gnn(nc, aps, out)
    r = run_bass_kernel_spmd(nc, [{f"in_{k}": v for k, v in arrays.items()}], core_ids=[0])
    return r.results[0]["out"]
```
